# Optimizing a Trainium2 kernel written in Bass

```python
import numpy as np
import jax
import jax.numpy as jnp

def _softmax(x, axis=-1):
    return jax.nn.softmax(x, axis=axis)

def _gelu(x):
    return jax.nn.gelu(x, approximate=True)

def _silu(x):
    return jax.nn.silu(x)

def _sigmoid(x):
    return jax.nn.sigmoid(x)

def _layernorm(x, axis=-1, eps=1e-05):
    m = jnp.mean(x, axis=axis, keepdims=True)
    v = jnp.var(x, axis=axis, keepdims=True)
    return (x - m) / jnp.sqrt(v + eps)

def _scatter_add(tgt, idx, src, axis=0):
    return tgt.at[idx].add(src)

def _segment_sum(src, seg, n):
    return jax.ops.segment_sum(src, seg, n)
kernel_name = 'mk_vit_tower_d1_tok_img1024_r4_5307b2'

def setup_inputs(seed: int=0):
    np.random.seed(seed)
    _w = jnp.asarray

    def _rec_inputs():
        import jax
        import jax.numpy as jnp
        _rk = jax.random.key(seed)
        x = -0.00016672 + 0.999947 * jax.random.normal(jax.random.fold_in(_rk, 1), (64, 3, 224, 224), jnp.float32)
        return x
    x = _rec_inputs()

    def _L0_tok_setup():
        import jax, jax.numpy as jnp
        import numpy as np
        PATCH = 16
        key = jax.random.key(seed)
        k1, k2, k3 = jax.random.split(key, 3)
        B, C, H, Wd = (64, 3, 96, 96)
        patch_dim = C * PATCH * PATCH
        embed_dim = 256
        x = jax.random.normal(k1, (B, C, H, Wd), dtype=jnp.float32)
        W = jax.random.normal(k2, (embed_dim, patch_dim), dtype=jnp.float32) * patch_dim ** (-0.5)
        b = jax.random.normal(k3, (embed_dim,), dtype=jnp.float32) * 0.01
        return {'x': x, 'W': W, 'b': b}
    _L0_tok_all = _L0_tok_setup()
    _L0_tok_in = {k: v for k, v in _L0_tok_all.items() if k in ('W', 'b')}
    del _L0_tok_all

    def _L0_attn_setup():
        import jax, jax.numpy as jnp
        import numpy as np
        NUM_HEADS = 16

        def _sinusoid_rel_pos(seq_len, dim):
            pos = jnp.arange(seq_len - 1, -1, -1, dtype=jnp.float32)
            inv_freq = 1.0 / 10000.0 ** (jnp.arange(0, dim, 2, dtype=jnp.float32) / dim)
            ang = pos[:, None] * inv_freq[None, :]
            return jnp.concatenate([jnp.sin(ang), jnp.cos(ang)], axis=-1)

        def _rel_shift(x):
            B, H, S, L = x.shape
            x = jnp.pad(x, ((0, 0), (0, 0), (0, 0), (1, 0)))
            x = x.reshape(B, H, L + 1, S)
            return x[:, :, 1:S + 1, :]
        key = jax.random.key(seed)
        ks = jax.random.split(key, 8)
        B, S, C = (2, 512, 256)
        Dk, Dv, H = (256, 256, NUM_HEADS)
        dk = Dk // H
        scale = 0.02
        return {'x': jax.random.normal(ks[0], (B, S, C), dtype=jnp.float32), 'Wq': jax.random.normal(ks[1], (C, Dk), dtype=jnp.float32) * scale, 'Wk': jax.random.normal(ks[2], (C, Dk), dtype=jnp.float32) * scale, 'Wv': jax.random.normal(ks[3], (C, Dv), dtype=jnp.float32) * scale, 'u': jax.random.normal(ks[4], (H, dk), dtype=jnp.float32) * scale, 'v': jax.random.normal(ks[5], (H, dk), dtype=jnp.float32) * scale, 'Wo': jax.random.normal(ks[6], (Dv, C), dtype=jnp.float32) * scale, 'bo': jnp.zeros((C,), dtype=jnp.float32)}
    _L0_attn_all = _L0_attn_setup()
    _L0_attn_in = {k: v for k, v in _L0_attn_all.items() if k in ('Wq', 'Wk', 'Wv', 'u', 'v', 'Wo', 'bo')}
    del _L0_attn_all

    def _L0_ffn_setup():
        import jax, jax.numpy as jnp
        import numpy as np
        import math
        B, T, C = (4, 512, 256)
        E, K = (8, 2)
        EH, SH = (512, 1024)
        CAP_FACTOR = 1.25
        SCALING = 1.0
        FC_MULT = 1.0

        def _capacity(N, k):
            avg = math.ceil(N * k / E)
            return max(int(math.ceil(avg * CAP_FACTOR)), 1)
        key = jax.random.key(seed)
        ks = jax.random.split(key, 6)
        sd = 0.02
        return {'x': jax.random.normal(ks[0], (B, T, C), jnp.float32), 'proj_w': jax.random.normal(ks[1], (E, C), jnp.float32) * sd, 'proj_b': jnp.zeros((E,), jnp.float32), 'expert_bias': jnp.zeros((E,), jnp.float32), 'fc1_w': jax.random.normal(ks[2], (E, EH, C), jnp.float32) * sd, 'fc1_b': jnp.zeros((E, EH), jnp.float32), 'fc2_w': jax.random.normal(ks[3], (E, C, EH), jnp.float32) * sd, 'fc2_b': jnp.zeros((E, C), jnp.float32), 'sh1_w': jax.random.normal(ks[4], (SH, C), jnp.float32) * sd, 'sh1_b': jnp.zeros((SH,), jnp.float32), 'sh2_w': jax.random.normal(ks[5], (C, SH), jnp.float32) * sd, 'sh2_b': jnp.zeros((C,), jnp.float32)}
    _L0_ffn_all = _L0_ffn_setup()
    _L0_ffn_in = {k: v for k, v in _L0_ffn_all.items() if k in ('proj_w', 'proj_b', 'expert_bias', 'fc1_w', 'fc1_b', 'fc2_w', 'fc2_b', 'sh1_w', 'sh1_b', 'sh2_w', 'sh2_b')}
    del _L0_ffn_all
    return {'x': x, 'L0_tok_W': _L0_tok_in['W'], 'L0_tok_b': _L0_tok_in['b'], 'L0_attn_Wq': _L0_attn_in['Wq'], 'L0_attn_Wk': _L0_attn_in['Wk'], 'L0_attn_Wv': _L0_attn_in['Wv'], 'L0_attn_u': _L0_attn_in['u'], 'L0_attn_v': _L0_attn_in['v'], 'L0_attn_Wo': _L0_attn_in['Wo'], 'L0_attn_bo': _L0_attn_in['bo'], 'L0_ffn_proj_w': _L0_ffn_in['proj_w'], 'L0_ffn_proj_b': _L0_ffn_in['proj_b'], 'L0_ffn_expert_bias': _L0_ffn_in['expert_bias'], 'L0_ffn_fc1_w': _L0_ffn_in['fc1_w'], 'L0_ffn_fc1_b': _L0_ffn_in['fc1_b'], 'L0_ffn_fc2_w': _L0_ffn_in['fc2_w'], 'L0_ffn_fc2_b': _L0_ffn_in['fc2_b'], 'L0_ffn_sh1_w': _L0_ffn_in['sh1_w'], 'L0_ffn_sh1_b': _L0_ffn_in['sh1_b'], 'L0_ffn_sh2_w': _L0_ffn_in['sh2_w'], 'L0_ffn_sh2_b': _L0_ffn_in['sh2_b']}

def reference(x, L0_tok_W, L0_tok_b, L0_attn_Wq, L0_attn_Wk, L0_attn_Wv, L0_attn_u, L0_attn_v, L0_attn_Wo, L0_attn_bo, L0_ffn_proj_w, L0_ffn_proj_b, L0_ffn_expert_bias, L0_ffn_fc1_w, L0_ffn_fc1_b, L0_ffn_fc2_w, L0_ffn_fc2_b, L0_ffn_sh1_w, L0_ffn_sh1_b, L0_ffn_sh2_w, L0_ffn_sh2_b):
    import jax
    import jax.numpy as jnp

    def _L0_tok_ref(x, W, b):
        import jax, jax.numpy as jnp
        import numpy as np
        PATCH = 16
        B, C, H, Wd = x.shape
        ph = pw = PATCH
        gh, gw = (H // ph, Wd // pw)
        patches = x.reshape(B, C, gh, ph, gw, pw)
        patches = patches.transpose(0, 2, 4, 1, 3, 5).reshape(B, gh * gw, C * ph * pw)
        out = jnp.einsum('bnp,dp->bnd', patches, W) + b
        return out

    def _L0_attn_ref(x, Wq, Wk, Wv, u, v, Wo, bo):
        import jax, jax.numpy as jnp
        import numpy as np
        NUM_HEADS = 16

        def _sinusoid_rel_pos(seq_len, dim):
            pos = jnp.arange(seq_len - 1, -1, -1, dtype=jnp.float32)
            inv_freq = 1.0 / 10000.0 ** (jnp.arange(0, dim, 2, dtype=jnp.float32) / dim)
            ang = pos[:, None] * inv_freq[None, :]
            return jnp.concatenate([jnp.sin(ang), jnp.cos(ang)], axis=-1)

        def _rel_shift(x):
            B, H, S, L = x.shape
            x = jnp.pad(x, ((0, 0), (0, 0), (0, 0), (1, 0)))
            x = x.reshape(B, H, L + 1, S)
            return x[:, :, 1:S + 1, :]
        B, S, C = x.shape
        H = NUM_HEADS
        dk = Wq.shape[1] // H
        dv = Wv.shape[1] // H
        Q = (x @ Wq).reshape(B, S, H, dk).transpose(0, 2, 1, 3)
        K = (x @ Wk).reshape(B, S, H, dk).transpose(0, 2, 1, 3)
        V = (x @ Wv).reshape(B, S, H, dv).transpose(0, 2, 1, 3)
        r = _sinusoid_rel_pos(S, dk)
        term1 = jnp.einsum('bhqd,bhkd->bhqk', Q, K)
        term2 = jnp.einsum('bhqd,kd->bhqk', Q, r)
        term3 = jnp.einsum('hd,bhkd->bhk', u, K)[:, :, None, :]
        term4 = jnp.einsum('hd,kd->hk', v, r)[None, :, None, :]
        scores = (term1 + term3 + _rel_shift(term2 + term4)) / jnp.sqrt(jnp.asarray(dk, dtype=x.dtype))
        attn = jax.nn.softmax(scores, axis=-1)
        out = jnp.einsum('bhqk,bhkd->bqhd', attn, V).reshape(B, S, H * dv)
        return out @ Wo + bo

    def _L0_ffn_ref(x, proj_w, proj_b, expert_bias, fc1_w, fc1_b, fc2_w, fc2_b, sh1_w, sh1_b, sh2_w, sh2_b):
        import jax, jax.numpy as jnp
        import numpy as np
        import math
        B, T, C = (4, 512, 256)
        E, K = (8, 2)
        EH, SH = (512, 1024)
        CAP_FACTOR = 1.25
        SCALING = 1.0
        FC_MULT = 1.0

        def _capacity(N, k):
            avg = math.ceil(N * k / E)
            return max(int(math.ceil(avg * CAP_FACTOR)), 1)
        Bx, Tx, Cx = x.shape
        N = Bx * Tx
        xf = x.reshape(N, Cx)
        z = xf @ proj_w.T + proj_b
        s = jax.nn.sigmoid(z) + expert_bias
        logits = jnp.log(jnp.clip(s, 1e-12)) * SCALING
        probs = jax.nn.softmax(logits, axis=-1)
        topk_w, topk_idx = jax.lax.top_k(probs, K)
        topk_w = topk_w / jnp.clip(topk_w.sum(-1, keepdims=True), 1e-12)
        pair_e = topk_idx.reshape(-1)
        pair_w = topk_w.reshape(-1)
        pair_tok = jnp.repeat(jnp.arange(N), K)
        cap = _capacity(N, K)
        assigned = pair_e[None, :] == jnp.arange(E)[:, None]
        wmat = jnp.where(assigned, pair_w[None, :], -jnp.inf)
        kept_w, kept_pair = jax.lax.top_k(wmat, cap)
        valid = kept_w > -jnp.inf
        kept_w = jnp.where(valid, kept_w, 0.0)
        kept_tok = pair_tok[kept_pair]
        xe = xf[kept_tok]
        h = jax.nn.gelu(jnp.einsum('ecd,ehd->ech', xe, fc1_w) + fc1_b[:, None, :], approximate=False)
        oe = jnp.einsum('ech,edh->ecd', h, fc2_w) + fc2_b[:, None, :]
        contrib = oe * kept_w[..., None]
        y = jnp.zeros((N, Cx), x.dtype).at[kept_tok.reshape(-1)].add(contrib.reshape(-1, Cx))
        sh = jax.nn.gelu(xf @ sh1_w.T + sh1_b, approximate=False) @ sh2_w.T + sh2_b
        return ((sh + y) * FC_MULT).reshape(Bx, Tx, Cx)
    h = _L0_tok_ref(x, L0_tok_W, L0_tok_b)
    h = h + _L0_attn_ref(_layernorm(h, axis=-1), L0_attn_Wq, L0_attn_Wk, L0_attn_Wv, L0_attn_u, L0_attn_v, L0_attn_Wo, L0_attn_bo)
    h = h + _L0_ffn_ref(_layernorm(h, axis=-1), L0_ffn_proj_w, L0_ffn_proj_b, L0_ffn_expert_bias, L0_ffn_fc1_w, L0_ffn_fc1_b, L0_ffn_fc2_w, L0_ffn_fc2_b, L0_ffn_sh1_w, L0_ffn_sh1_b, L0_ffn_sh2_w, L0_ffn_sh2_b)
    return h

_drawn_inputs = setup_inputs


def setup_inputs(seed=0):
    import zlib

    import numpy as np

    out = dict(_drawn_inputs(seed))
    spreads = {'L0_attn_bo': (0.0, 0.1),
     'L0_ffn_proj_b': (0.0, 0.403),
     'L0_ffn_expert_bias': (0.0, 0.1),
     'L0_ffn_fc1_b': (0.0, 1.62),
     'L0_ffn_fc2_b': (0.0, 0.435),
     'L0_ffn_sh1_b': (0.0, 0.736),
     'L0_ffn_sh2_b': (0.0, 0.1)}
    factors = {'L0_tok_b': 4.731,
     'L0_attn_Wq': 8.0,
     'L0_attn_Wk': 8.0,
     'L0_attn_Wv': 5.963,
     'L0_attn_u': 8.0,
     'L0_attn_v': 8.0,
     'L0_attn_Wo': 6.119,
     'L0_ffn_fc1_w': 3.414}
    for name, (base, spread) in spreads.items():
        noise = np.random.default_rng([zlib.crc32(name.encode()), seed]).standard_normal(out[name].shape)
        drawn = base * np.exp(spread * noise) if base else spread * noise
        out[name] = jnp.asarray(drawn.astype(out[name].dtype))
    for name, factor in factors.items():
        out[name] = (out[name] * factor).astype(out[name].dtype)
    return out
```

```python
import concourse.bass as bass
from concourse import mybir
from contextlib import ExitStack, contextmanager

F32 = mybir.dt.float32
BF16 = mybir.dt.bfloat16
U32 = mybir.dt.uint32
ALU = mybir.AluOpType
ACT = mybir.ActivationFunctionType
AX = mybir.AxisListType

IMAGES, SIDE, PATCH, CHANNELS = 64, 224, 16, 3
GRID = SIDE // PATCH
S = GRID * GRID
T = IMAGES * S
C = 256
PD = CHANNELS * PATCH * PATCH
PC = PD // 128
HEADS, DK = 16, 16
TILE = S // 2
PAIR = 2 * S
PAIRS = T // PAIR
PAD = 8
EPS = 1e-5
NEVER = -1e28
QH, QL, AH, AL, BH, BL, KH, KL = range(8)
KINDS = 8


@contextmanager
def stage(nc):
    with ExitStack() as ctx:
        ctx.semaphores = []
        yield ctx
        for s in ctx.semaphores:
            nc.gpsimd.sem_clear(s)
        nc.all_engine_barrier()


def semaphore(nc, ctx, name):
    ctx.semaphores.append(ctx.enter_context(nc.semaphore(name)))
    return ctx.semaphores[-1]


class Signal:

    def __init__(self, nc, ctx, name, per=1):
        self.sem = semaphore(nc, ctx, name)
        self.per = per

    def open(self, eng):
        eng.sem_inc(self.sem, 2 * self.per)

    def at(self, n, k=None):
        return (n + 2) * self.per + (self.per if k is None else k)


class Transfers:

    def __init__(self, nc, ctx, name, per=1, pool=False):
        self.lead = 0 if pool else 16 * per
        self.sems = [semaphore(nc, ctx, f"{name}_{u}") for u in range(2)]
        self.per = per

    def open(self, eng):
        for s in self.sems:
            eng.sem_inc(s, 16 * self.per)

    def at(self, n, u):
        return (n - u) * (8 * self.per) + 16 * self.per + self.lead


def known(x, low, high):
    return not isinstance(x, int) or low <= x < high


def three_products(nc, out, operands, start=True, stop=True):
    last = None
    todo = [(a, b) for lh, ll, rh, rl in operands for a, b in ((lh, rh), (lh, rl), (ll, rh))]
    for k, (a, b) in enumerate(todo):
        last = nc.tensor.matmul(out, a, b, start=start and k == 0, stop=stop and k == len(todo) - 1)
    return last


def tiles_of(ap):
    return ap.rearrange("(t p) c -> p t c", p=TILE)


def project(nc, d):
    with stage(nc) as ctx:
        def sb(name, shape, dt=F32):
            return ctx.enter_context(nc.sbuf_tensor("p1_" + name, shape, dt))

        def pb(name, shape, dt=F32):
            return ctx.enter_context(nc.psum_tensor("p1_" + name, shape, dt))

        def signal(name, per=1):
            return Signal(nc, ctx, "p1_" + name, per)

        def transfers(name, per=1):
            return Transfers(nc, ctx, "p1_" + name, per)

        w32 = sb("w32", [128, PC, C])
        wh, wl = sb("wh", [128, PC, C], BF16), sb("wl", [128, PC, C], BF16)
        g32 = sb("g32", [128, 2, 4 * C])
        gh, gl = sb("gh", [128, 2, 4 * C], BF16), sb("gl", [128, 2, 4 * C], BF16)
        cols = sb("cols", [128, 2, 3])
        rot = sb("rot", [128, 4, PAIR])
        tokb = sb("tokb", [TILE, C])
        ident = sb("ident", [128, 128])
        blk8 = sb("blk8", [128, 8])
        x32 = [sb(f"x32{u}", [128, PC, PAIR]) for u in range(2)]
        xh = [sb(f"xh{u}", [128, PC, PAIR], BF16) for u in range(2)]
        xl = [sb(f"xl{u}", [128, PC, PAIR], BF16) for u in range(2)]
        h0 = [sb(f"h0{u}", [TILE, 4, C]) for u in range(2)]
        stats = sb("stats", [TILE, 4, 6])
        mv = sb("mv", [TILE, 4, 2])
        eps = sb("eps", [TILE, 1])
        std, rstd = sb("std", [TILE, 4]), sb("rstd", [TILE, 4])
        xn = sb("xn", [TILE, 4, C])
        nh, nl = sb("nh", [128, 2, PAIR], BF16), sb("nl", [128, 2, PAIR], BF16)
        k32 = sb("k32", [128, 2, PAIR + 1])
        prod = sb("prod", [128, 2, PAIR])
        rt = sb("rt", [128, 2, 4, PAIR])
        st = [sb(f"st{u}", [128, 2, KINDS, PAIR], BF16) for u in range(2)]
        v32 = [sb(f"v32{u}", [TILE, 4, C]) for u in range(2)]
        c32 = [sb(f"c32{u}", [TILE, 4, HEADS]) for u in range(2)]
        pad16 = sb("pad16", [128, KINDS, PAD], BF16)
        padv = sb("padv", [PAD, C])

        psH = pb("psH", [TILE, 4, C])
        psT = pb("psT", [128, 2, 512])
        psC = psT[0:TILE, 0, 448:512].rearrange("p (t h) -> p t h", t=4)
        psJ = [pb(f"psJ{j}", [128, 2, 512]) for j in range(2)]

        loaded = semaphore(nc, ctx, "p1_weights_loaded")
        passed, passed_sp = (semaphore(nc, ctx, "p1_passed_" + e) for e in ("dve", "sp"))
        w_hi, w_lo = (semaphore(nc, ctx, "p1_" + n) for n in ("weights_hi", "weights_lo"))
        pads_set = semaphore(nc, ctx, "p1_pads_set")
        pads_out = semaphore(nc, ctx, "p1_pads_stored")
        x_in = transfers("x_in")
        xh_ok, xl_ok = signal("xh"), signal("xl")
        h_ok, h0_ok = signal("h_in_psum"), signal("h0")
        stats_ok, mv_ok, std_ok = signal("stats"), signal("mv"), signal("std")
        rstd_ok, xn_ok = signal("rstd"), signal("xn")
        t_ok, nh_ok, nl_ok = signal("xnT_in_psum"), signal("nh"), signal("nl")
        jk_ok, jq_ok, jv_ok = signal("k_in_psum"), signal("q_in_psum", 2), signal("v_in_psum")
        kh_ok, kl_ok = signal("kh"), signal("kl")
        k32_ok, qh_ok, q_used = signal("k32"), signal("qh", 2), signal("q_read_by_dve", 2)
        ab_ok, abh_ok, abl_ok = signal("ab", 2), signal("ab_hi", 2), signal("ab_lo", 2)
        prods, prod_ok = signal("prods_written"), signal("prod")
        c_ok, c32_ok = signal("c_in_psum"), signal("c32")
        v_ok = signal("v32")
        h0_out, st_out = transfers("h0_stored"), transfers("stack_stored", 2)
        v_out, c_out = transfers("v_stored"), transfers("c_stored")

        def positions(eng, position):
            for n in (0, 1):
                position(n, n)
            with eng.Fori(1, PAIRS // 2 - 2) as i:
                for u in range(2):
                    position(i * 2 + u, u)
            for n in range(PAIRS - 4, PAIRS + 1):
                position(n, n % 2)

        with nc.Block() as block:
            @block.sync
            def _(sp):
                for s in (x_in, h0_out, st_out, v_out, c_out):
                    s.open(sp)
                for dst, src in ((w32[:], d["tok_w"]), (g32[:], d["qkv_w"]), (cols[:], d["cols"]),
                                 (rot[:], d["rot"]), (tokb[:], d["tok_b"]), (ident[:], d["ident"]),
                                 (blk8[:], d["blk8"])):
                    sp.dma_start(dst, src).then_inc(loaded, 16)

                def load(n, u):
                    sp.dma_start(x32[u][:], d["x"][:, :, bass.ds(n * PAIR, PAIR)]).then_inc(x_in.sems[u], 16)

                def store(n, u):
                    rows = bass.ds(n * PAIR, PAIR)
                    sp.wait_ge(h0_ok.sem, h0_ok.at(n))
                    sp.dma_start(tiles_of(d["h0"][rows, :]), h0[u][:]).then_inc(h0_out.sems[u], 16)
                    sp.wait_ge(v_ok.sem, v_ok.at(n))
                    sp.dma_start(tiles_of(d["v"][rows, :]), v32[u][:]).then_inc(v_out.sems[u], 16)
                    sp.wait_ge(c32_ok.sem, c32_ok.at(n))
                    sp.dma_start(tiles_of(d["c"][rows, :]), c32[u][:]).then_inc(c_out.sems[u], 16)
                    sp.wait_ge(kl_ok.sem, kl_ok.at(n))
                    sp.wait_ge(q_used.sem, q_used.at(n))
                    sp.wait_ge(abl_ok.sem, abl_ok.at(n))
                    sp.sem_inc(passed_sp, 1)
                    for m in range(2):
                        sp.dma_start(d["stack"][m, :, :, rows], st[u][:, m]).then_inc(st_out.sems[u], 16)

                def position(n, u):
                    if known(n, 0, PAIRS - 3):
                        sp.wait_ge(xh_ok.sem, xh_ok.at(n + 1))
                        sp.wait_ge(xl_ok.sem, xl_ok.at(n + 1))
                        sp.sem_inc(passed_sp, 1)
                        load(n + 3, 1 - u)
                    if known(n, 0, PAIRS):
                        store(n, u)

                load(0, 0)
                load(1, 1)
                sp.wait_ge(pads_set, 2)
                for m in range(2):
                    with nc.allow_non_contiguous_dma(reason="the stacks' pad columns, once"):
                        sp.dma_start(d["stack"][m, :, :, T:T + PAD], pad16[:]).then_inc(pads_out, 16)
                sp.dma_start(d["v"][T:T + PAD, :], padv[:]).then_inc(pads_out, 16)
                sp.wait_ge(xh_ok.sem, xh_ok.at(0))
                sp.wait_ge(xl_ok.sem, xl_ok.at(0))
                load(2, 0)
                positions(sp, position)
                for s in (h0_out, st_out, v_out, c_out):
                    sp.wait_ge(s.sems[0], s.at(PAIRS - 2, 0))
                    sp.wait_ge(s.sems[1], s.at(PAIRS - 1, 1))
                sp.wait_ge(pads_out, 48)

            @block.scalar
            def _(act):
                for s in (xh_ok, std_ok, nh_ok, k32_ok, kh_ok, qh_ok, abh_ok, v_ok):
                    s.open(act)
                act.wait_ge(loaded, 112)
                act.activation(wh[:], w32[:], ACT.Copy).then_inc(w_hi, 1)
                act.activation(gh[:], g32[:], ACT.Copy).then_inc(w_hi, 1)

                def split(n, u):
                    act.wait_ge(x_in.sems[u], x_in.at(n, u))
                    act.wait_ge(h_ok.sem, h_ok.at(n - 2))
                    act.activation(xh[u][:], x32[u][:], ACT.Copy).then_inc(xh_ok.sem, 1)

                def deviation(n):
                    act.wait_ge(mv_ok.sem, mv_ok.at(n))
                    act.wait_ge(rstd_ok.sem, rstd_ok.at(n - 1))
                    act.activation(std[:], mv[:, :, 1], ACT.Sqrt, bias=eps[:, 0:1]).then_inc(std_ok.sem, 1)

                def position(n, u):
                    if known(n, 0, PAIRS):
                        act.wait_ge(t_ok.sem, t_ok.at(n))
                        act.wait_ge(jq_ok.sem, jq_ok.at(n - 1))
                        act.wait_ge(nl_ok.sem, nl_ok.at(n - 1))
                        act.activation(nh[:], psT[:, :, 0:PAIR], ACT.Copy).then_inc(nh_ok.sem, 1)
                    if known(n, 0, PAIRS - 2):
                        split(n + 2, u)
                    if known(n, 1, PAIRS + 1):
                        for m in range(2):
                            act.wait_ge(ab_ok.sem, ab_ok.at(n - 1, m + 1))
                            act.activation(st[1 - u][:, m, AH:BH + 1:2, :], rt[:, m, 0:4:2, :], ACT.Copy).then_inc(abh_ok.sem, 1)
                    if known(n, 0, PAIRS - 1):
                        deviation(n + 1)
                    if known(n, 0, PAIRS):
                        act.wait_ge(jv_ok.sem, jv_ok.at(n))
                        act.wait_ge(v_out.sems[u], v_out.at(n - 2, u))
                        act.activation(v32[u][:].rearrange("p (b t) c -> p b (t c)", b=2), psJ[1][0:TILE, :, :],
                                       ACT.Copy).then_inc(v_ok.sem, 1)
                        act.wait_ge(jk_ok.sem, jk_ok.at(n))
                        act.wait_ge(st_out.sems[u], st_out.at(n - 2, u))
                        act.activation(st[u][:, :, KH, :], psJ[0][:, :, 0:PAIR], ACT.Copy).then_inc(kh_ok.sem, 1)
                        act.wait_ge(prod_ok.sem, prod_ok.at(n - 1))
                        act.wait_ge(kl_ok.sem, kl_ok.at(n - 1))
                        act.activation(k32[:, :, 0:PAIR], psJ[0][:, :, 0:PAIR], ACT.Copy).then_inc(k32_ok.sem, 1)
                        for m in range(2):
                            act.wait_ge(jq_ok.sem, jq_ok.at(n, m + 1))
                            act.activation(st[u][:, m, QH, :], psJ[(m + 1) % 2][:, 0, 0:PAIR], ACT.Identity,
                                           bias=cols[:, m, 0:1]).then_inc(qh_ok.sem, 1)

                act.wait_ge(pads_set, 2)
                split(0, 0)
                split(1, 1)
                deviation(0)
                positions(act, position)

            @block.vector
            def _(dve):
                for s in (xl_ok, h0_ok, stats_ok, mv_ok, rstd_ok, xn_ok, nl_ok, q_used, prods, prod_ok, c32_ok):
                    s.open(dve)
                nc.vector.memset(eps[:], EPS)
                nc.vector.memset(k32[:], 0.0)
                nc.vector.memset(pad16[:], 0.0).then_inc(pads_set, 1)
                nc.vector.memset(padv[:], 0.0).then_inc(pads_set, 1)
                dve.wait_ge(w_hi, 1)
                nc.vector.tensor_tensor(wl[:], w32[:], wh[:], ALU.subtract).then_inc(w_lo, 1)
                dve.wait_ge(w_hi, 2)
                nc.vector.tensor_tensor(gl[:], g32[:], gh[:], ALU.subtract).then_inc(w_lo, 1)

                def split(n, u):
                    dve.wait_ge(xh_ok.sem, xh_ok.at(n))
                    nc.vector.tensor_tensor(xl[u][:], x32[u][:], xh[u][:], ALU.subtract).then_inc(xl_ok.sem, 1)

                def normalise(n, u):
                    dve.wait_ge(h_ok.sem, h_ok.at(n))
                    dve.wait_ge(h0_out.sems[u], h0_out.at(n - 2, u))
                    nc.vector.tensor_tensor(h0[u][:], psH[:], tokb[:].unsqueeze(1).broadcast_to([TILE, 4, C]),
                                            ALU.add).then_inc(h0_ok.sem, 1)
                    dve.wait_ge(h0_ok.sem, h0_ok.at(n))
                    for t in range(4):
                        last = nc.vector.bn_stats(stats[:, t, :], h0[u][:, t, :])
                    last.then_inc(stats_ok.sem, 1)
                    dve.wait_ge(stats_ok.sem, stats_ok.at(n))
                    dve.wait_ge(std_ok.sem, std_ok.at(n - 1))
                    dve.sem_inc(passed, 1)
                    for t in range(4):
                        last = nc.vector.bn_aggr(mv[:, t, :], stats[:, t, :])
                    last.then_inc(mv_ok.sem, 1)
                    dve.wait_ge(std_ok.sem, std_ok.at(n))
                    nc.vector.reciprocal(rstd[:], std[:]).then_inc(rstd_ok.sem, 1)
                    dve.wait_ge(rstd_ok.sem, rstd_ok.at(n))
                    dve.wait_ge(t_ok.sem, t_ok.at(n - 1))
                    for t in range(4):
                        last = nc.vector.tensor_scalar(xn[:, t, :], h0[u][:, t, :], mv[:, t, 0:1], rstd[:, t:t + 1],
                                                       ALU.subtract, ALU.mult)
                    last.then_inc(xn_ok.sem, 1)

                def position(n, u):
                    if known(n, 0, PAIRS):
                        dve.wait_ge(nh_ok.sem, nh_ok.at(n))
                        nc.vector.tensor_tensor(nl[:], psT[:, :, 0:PAIR], nh[:], ALU.subtract).then_inc(nl_ok.sem, 1)
                    if known(n, 0, PAIRS - 2):
                        split(n + 2, u)
                    if known(n, 0, PAIRS - 1):
                        normalise(n + 1, 1 - u)
                    if known(n, 1, PAIRS + 1):
                        dve.wait_ge(c_ok.sem, c_ok.at(n - 1))
                        dve.wait_ge(c_out.sems[1 - u], c_out.at(n - 3, 1 - u))
                        nc.vector.tensor_copy(c32[1 - u][:], psC).then_inc(c32_ok.sem, 1)
                    if known(n, 0, PAIRS):
                        rotate(n, u)

                def rotate(n, u):
                    dve.wait_ge(k32_ok.sem, k32_ok.at(n))
                    dve.wait_ge(abl_ok.sem, abl_ok.at(n - 1))
                    dve.wait_ge(st_out.sems[u], st_out.at(n - 2, u))
                    for m in range(2):
                        qa, qb = psJ[(m + 1) % 2][:, 0, 0:PAIR], psJ[(m + 1) % 2][:, 1, 0:PAIR]
                        dve.wait_ge(jq_ok.sem, jq_ok.at(n, m + 1))

                        def term(r, q, col):
                            return nc.vector.scalar_tensor_tensor(rt[:, m, r, :], q, cols[:, m, col:col + 1], rot[:, r, :],
                                                                  ALU.add, ALU.mult)

                        term(1, qb, 2)
                        term(3, qb, 2)
                        dve.wait_ge(qh_ok.sem, qh_ok.at(n, m + 1))
                        term(0, qa, 1)
                        term(2, qa, 1)
                        last = nc.vector.scalar_tensor_tensor(prod[:, m, :], qa, cols[:, m, 0:1], k32[:, m, 1:PAIR + 1],
                                                              ALU.add, ALU.mult)
                        if m:
                            last.then_inc(prods.sem, 1)
                        nc.vector.scalar_tensor_tensor(st[u][:, m, QL, :], qa, cols[:, m, 0:1], st[u][:, m, QH, :],
                                                       ALU.add, ALU.subtract).then_inc(q_used.sem, 1)
                    dve.wait_ge(prods.sem, prods.at(n))
                    nc.vector.memset(prod[:, :, S - 1:PAIR:S], NEVER / DK).then_inc(prod_ok.sem, 1)

                split(0, 0)
                split(1, 1)
                normalise(0, 0)
                positions(dve, position)

            @block.gpsimd
            def _(pool):
                for s in (kl_ok, ab_ok, abl_ok):
                    s.open(pool)

                def step(n, u):
                    pool.wait_ge(kh_ok.sem, kh_ok.at(n))
                    pool.wait_ge(k32_ok.sem, k32_ok.at(n))
                    nc.gpsimd.tensor_tensor(st[u][:, :, KL, :], k32[:, :, 0:PAIR], st[u][:, :, KH, :], ALU.subtract).then_inc(kl_ok.sem, 1)
                    for m in range(2):
                        pool.wait_ge(q_used.sem, q_used.at(n, m + 1))
                        nc.gpsimd.tensor_tensor(rt[:, m, 0:4:2, :], rt[:, m, 0:4:2, :], rt[:, m, 1:4:2, :], ALU.add).then_inc(ab_ok.sem, 1)
                        pool.wait_ge(abh_ok.sem, abh_ok.at(n, m + 1))
                        nc.gpsimd.tensor_tensor(st[u][:, m, AL:BL + 1:2, :], rt[:, m, 0:4:2, :],
                                                          st[u][:, m, AH:BH + 1:2, :], ALU.subtract).then_inc(abl_ok.sem, 1)

                with pool.Fori(0, PAIRS // 2) as i:
                    step(i * 2, 0)
                    step(i * 2 + 1, 1)

            @block.tensor
            def _(pe):
                for s in (h_ok, t_ok, jk_ok, jq_ok, jv_ok, c_ok):
                    s.open(pe)
                pe.wait_ge(w_lo, 2)
                pe.wait_ge(pads_set, 2)

                def embed(n, u):
                    pe.wait_ge(xh_ok.sem, xh_ok.at(n))
                    pe.wait_ge(xl_ok.sem, xl_ok.at(n))
                    pe.wait_ge(h0_ok.sem, h0_ok.at(n - 1))
                    for t in range(4):
                        cut = slice(t * TILE, (t + 1) * TILE)
                        last = three_products(nc, psH[:, t, :], [
                            (xh[u][:, c, cut], xl[u][:, c, cut], wh[:, c, :], wl[:, c, :]) for c in range(PC)])
                    last.then_inc(h_ok.sem, 1)

                def rows(out, col):
                    return three_products(nc, out, [
                        (gh[:, c, col:col + 128], gl[:, c, col:col + 128], nh[:, c, :], nl[:, c, :]) for c in range(2)])

                def position(n, u):
                    if known(n, 0, PAIRS):
                        pe.wait_ge(xn_ok.sem, xn_ok.at(n))
                        pe.wait_ge(nl_ok.sem, nl_ok.at(n - 1))
                        pe.wait_ge(c32_ok.sem, c32_ok.at(n - 2))
                        for c in range(2):
                            for t in range(4):
                                last = nc.tensor.transpose(psT[:, c, t * TILE:(t + 1) * TILE], xn[:, t, c * 128:(c + 1) * 128],
                                                           ident[0:TILE, 0:TILE])
                        last.then_inc(t_ok.sem, 1)
                    if known(n, 0, PAIRS - 1):
                        embed(n + 1, 1 - u)
                    if known(n, 0, PAIRS):
                        pe.wait_ge(nl_ok.sem, nl_ok.at(n))
                    if known(n, 1, PAIRS + 1):
                        pe.wait_ge(prod_ok.sem, prod_ok.at(n - 1))
                        for t in range(4):
                            for m in range(2):
                                last = nc.tensor.matmul(psC[:, t, 8 * m:8 * m + 8], prod[:, m, t * TILE:(t + 1) * TILE],
                                                        blk8[:], start=True, stop=True)
                        last.then_inc(c_ok.sem, 1)
                    if known(n, 0, PAIRS):
                        pe.wait_ge(q_used.sem, q_used.at(n - 1, 1))
                        for t in range(4):
                            cut = slice(t * TILE, (t + 1) * TILE)
                            last = three_products(nc, psJ[1][0:TILE, t // 2, (t % 2) * C:(t % 2 + 1) * C], [
                                (nh[:, c, cut], nl[:, c, cut], gh[:, c, 3 * C:], gl[:, c, 3 * C:]) for c in range(2)])
                        last.then_inc(jv_ok.sem, 1)
                        pe.wait_ge(q_used.sem, q_used.at(n - 1))
                        for m in range(2):
                            last = rows(psJ[0][:, m, 0:PAIR], 2 * C + 128 * m)
                        last.then_inc(jk_ok.sem, 1)
                        pe.wait_ge(v_ok.sem, v_ok.at(n))
                        for m in range(2):
                            if m:
                                pe.wait_ge(k32_ok.sem, k32_ok.at(n))
                            ps = psJ[(m + 1) % 2]
                            rows(ps[:, 0, 0:PAIR], 128 * m)
                            rows(ps[:, 1, 0:PAIR], C + 128 * m).then_inc(jq_ok.sem, 1)

                embed(0, 0)
                positions(pe, position)


LAG = 6
QUADS = HEADS // 4
SLOTS = IMAGES * QUADS
BODY = 16
STACK = 96
ROWS = STACK + 2


NEVER_COLUMNS = 4 * (TILE + 1) + 4 * TILE


def attend(nc, d):
    with stage(nc) as ctx:
        def sb(name, shape, dt=F32):
            return ctx.enter_context(nc.sbuf_tensor("p2_" + name, shape, dt))

        def pb(name, shape, dt=F32):
            return ctx.enter_context(nc.psum_tensor("p2_" + name, shape, dt))

        def signal(name, per=1):
            return Signal(nc, ctx, "p2_" + name, per)

        def transfers(name, per=1):
            return Transfers(nc, ctx, "p2_" + name, per)

        L = [sb(f"L{u}", [ROWS, HEADS, PAIR], BF16) for u in range(2)]
        U = [sb(f"U{u}", [ROWS, HEADS, PAIR], BF16) for u in range(2)]
        K = [sb(f"K{u}", [ROWS, HEADS, PAIR], BF16) for u in range(2)]
        vraw = [sb(f"vraw{u}", [TILE, 4, C]) for u in range(2)]
        vnext = [sb(f"vnext{u}", [TILE, 4, C]) for u in range(2)]
        h0 = [sb(f"h0{u}", [TILE, 4, C]) for u in range(2)]
        cnext = [sb(f"cnext{u}", [TILE, 4, HEADS]) for u in range(2)]
        v32 = [sb(f"v32{u}", [TILE, 4, HEADS, 32]) for u in range(2)]
        ident = sb("ident", [128, 128])
        ident16 = sb("ident16", [TILE, TILE], BF16)
        never32, never = (sb(x, [TILE, NEVER_COLUMNS], dt) for x, dt in (("never32", F32), ("never", BF16)))
        neverS, neverE = (never[:, 2 * (TILE + 1) * x:2 * (TILE + 1) * (x + 1)].rearrange("p (h t) -> p h t", h=2)
                          for x in range(2))
        neverU = never[:, 4 * (TILE + 1):NEVER_COLUMNS]
        maskE = sb("maskE", [TILE, TILE], U32)
        wo, bo = sb("wo", [128, 2, C]), sb("bo", [TILE, C])
        mx = [sb(f"mx{g}", [TILE, 2, HEADS]) for g in range(2)]
        mxU = [sb(f"mxU{g}", [TILE, 2, HEADS]) for g in range(2)]
        ml, mf, mt, ea = (sb(x, [TILE, 2, HEADS]) for x in ("ml", "mf", "mt", "ea"))
        nm = sb("nm", [TILE, 2, 2, HEADS], BF16)
        mrow = [sb(f"mrow{g}", [2 * HEADS, S], BF16) for g in range(2)]
        en = [sb(f"en{g}", [TILE, 2, HEADS]) for g in range(2)]
        ev = [sb(f"ev{g}", [TILE, 2, HEADS, DK]) for g in range(2)]
        probs = [sb(f"probs{j}", [TILE, 2, PAIR]) for j in range(2)]
        ot = [sb(f"ot{g}", [128, QUADS, S]) for g in range(2)]
        den, rden = sb("den", [TILE, HEADS]), sb("rden", [TILE, HEADS])
        num = sb("num", [TILE, HEADS, DK])
        attn = sb("attn", [TILE, HEADS, DK])
        attnT = sb("attnT", [128, 2, TILE])
        h1 = [sb(f"h1{g}", [TILE, 2, C]) for g in range(2)]

        psS, psD = pb("psS", [TILE, 2, 512]), pb("psD", [TILE, 512])
        psE, psF = pb("psE", [TILE, 2, 512]), pb("psF", [TILE, 512])
        psO = pb("psO", [128, 512])
        psM = pb("psM", [128, 512])
        psM16 = psM[:].bitcast(BF16)

        passed = {e: semaphore(nc, ctx, "p2_passed_" + e) for e in ("dve", "pool", "sp")}
        setup = semaphore(nc, ctx, "p2_constants_loaded")
        made_v32 = semaphore(nc, ctx, "p2_v32_constants")
        made = semaphore(nc, ctx, "p2_constants_made")
        s_ok, s_max = signal("s_in_psum", 6), signal("row_max", 6)
        e_ok, e_sel, p_ok = signal("e_in_psum", 4), signal("e_selected", 4), signal("probs", 4)
        pv_ok, ot_ok = signal("pv", 2), signal("ot")
        mch, mtr, mrow_ok, en_ok = signal("max_chain", 6), signal("maxT_in_psum"), signal("mrow"), signal("en")
        ev_ok, v32_ok, hb_ok = signal("ev"), signal("v32", 2), signal("h0_with_bias", 2)
        ott_ok, nrm, num_ok, attn_ok = signal("otT_in_psum", 2), signal("den", 4), signal("num", 2), signal("attn", 2)
        at_ok, att_ok, wo_ok, h1_ok = signal("attnT_in_psum", 2), signal("attnT", 2), signal("wo", 2), signal("h1", 2)
        stacks = [transfers(f"stack_in{m}", 15) for m in range(2)]
        tokens_in, h0_in = transfers("tokens_in", 3), transfers("h0_in")
        m_in, h1_out = transfers("max_in", 4), transfers("h1_out")

        def where(i, r):
            return i * BODY + r, i * 4 + r // 4, i * 2 + r // 8, r % 4, r // 4 % 2, r // 8 % 2

        def positions(eng, position):
            for r in range(-LAG, 0):
                for c in range(2):
                    position(0, r, c)
            for i in (0, None, IMAGES // 4 - 1):
                if i is None:
                    with eng.Fori(1, IMAGES // 4 - 1) as j:
                        for r in range(BODY):
                            for c in range(2):
                                position(j, r, c)
                    continue
                for r in range(BODY):
                    for c in range(2):
                        position(i, r, c)
            for r in range(4):
                for c in range(2):
                    position(IMAGES // 4, r, c)

        TAIL = {1: ("ott", 0), 2: ("at", 0), 3: ("wo", 0), 4: ("ott", 1), 5: ("mtr", 0), 6: ("at", 1), 7: ("wo", 1)}

        with nc.Block() as block:
            @block.sync
            def _(sp):
                for s in (*stacks, tokens_in, h0_in, m_in, h1_out):
                    s.open(sp)
                for u in range(2):
                    sp.dma_start(K[u][48:ROWS], d["keyrows"]).then_inc(setup, 16)
                for dst, name in ((ident, "ident"), (never32, "never"), (maskE, "maskE"), (wo, "wo"), (bo, "bo")):
                    sp.dma_start(dst[:], d[name]).then_inc(setup, 16)

                def load_stacks(n, u, m):
                    sp.sem_inc(passed["sp"], 1)

                    def rows(dst, r, kind, shift=0):
                        src = d["stack"][m, :, kind, bass.ds(n * PAIR + shift, PAIR)]
                        sp.dma_start(dst[u][DK * r:DK * r + DK, 8 * m:8 * m + 8, :],
                                                  src.rearrange("(h d) t -> d h t", d=DK)).then_inc(stacks[m].sems[u], 16)
                    for r, (kl, ku, kk) in enumerate(((QH, QH, KH), (QH, QH, KL), (QL, QL, KH))):
                        rows(L, r, kl)
                        rows(K, r, kk)
                        rows(U, r, ku)
                    for r, (kl, ku) in enumerate(((AH, BH), (AH, BH), (AL, BL))):
                        rows(L, 3 + r, kl)
                        rows(U, 3 + r, ku, 1)

                def load_tokens(n, u):
                    sp.sem_inc(passed["sp"], 1)
                    for dst, name, shift in ((cnext, "c", 0), (vraw, "v", 0), (vnext, "v", 1)):
                        sp.dma_start(dst[u][:], tiles_of(d[name][bass.ds(n * PAIR + shift, PAIR), :])).then_inc(tokens_in.sems[u], 16)

                def load_h0(n, u):
                    sp.sem_inc(passed["sp"], 1)
                    sp.dma_start(h0[u][:], tiles_of(d["h0"][bass.ds(n * PAIR, PAIR), :])).then_inc(h0_in.sems[u], 16)

                for n in range(2):
                    for m in range(2):
                        load_stacks(n, n, m)
                    load_tokens(n, n)
                    load_h0(n, n)

                def store_h1(k, g):
                    sp.wait_ge(h1_ok.sem, h1_ok.at(k))
                    sp.sem_inc(passed["sp"], 1)
                    sp.dma_start(tiles_of(d["h1"][bass.ds(k * S, S), :]), h1[g][:]).then_inc(h1_out.sems[g], 16)

                def position(i, r, c):
                    s, k, n, q, g, u = where(i, r)
                    if c == 1 and q == 2 and known(k, -1, IMAGES - 1):
                        g1, u1 = (g + 1) % 2, (r + 4) // 8 % 2
                        sp.wait_ge(mrow_ok.sem, mrow_ok.at(k + 1))
                        for dst in (L, U):
                            for part in range(2):
                                sp.dma_start(dst[u1][STACK + part:STACK + part + 1, :, g1 * S:g1 * S + S],
                                                     mrow[g1][HEADS * part:HEADS * (part + 1), :]).then_inc(m_in.sems[g1], 16)
                    if c == 1 and q == 0 and known(k, 2, IMAGES + 1):
                        store_h1(k - 2, g)
                    if c == 0 and r % 8 == 0 and known(n, 1, PAIRS - 1):
                        sp.wait_ge(e_ok.sem, e_ok.at(s - 1))
                        load_stacks(n + 1, 1 - u, 1)
                        sp.wait_ge(ev_ok.sem, ev_ok.at(k - 1))
                        sp.sem_inc(passed["sp"], 1)
                        sp.wait_ge(v32_ok.sem, v32_ok.at(n - 1))
                        load_tokens(n + 1, 1 - u)
                    if c == 0 and r % 8 == 4 and known(n, 1, PAIRS - 1):
                        sp.wait_ge(h1_ok.sem, h1_ok.at(k - 2))
                        load_h0(n + 1, 1 - u)
                    if c == 1 and r % 8 == 6 and known(n, 0, PAIRS - 2):
                        sp.wait_ge(e_ok.sem, e_ok.at(s - 1))
                        load_stacks(n + 2, u, 0)

                positions(sp, position)
                store_h1(IMAGES - 1, 1)
                sp.wait_ge(h1_out.sems[0], h1_out.at(IMAGES - 2, 0))
                sp.wait_ge(h1_out.sems[1], h1_out.at(IMAGES - 1, 1))

            @block.gpsimd
            def _(pool):
                for s in (ev_ok, v32_ok, hb_ok, attn_ok):
                    s.open(pool)
                for u in range(2):
                    nc.gpsimd.memset(v32[u][:, :, :, DK:32], 0.0).then_inc(made_v32, 1)
                pool.wait_ge(made_v32, 2)
                for u in range(2):
                    nc.gpsimd.memset(v32[u][:, :, :, DK:DK + 1], 1.0).then_inc(made_v32, 1)

                def values(n, u, half):
                    pool.wait_ge(tokens_in.sems[u], tokens_in.at(n, u))
                    pool.sem_inc(passed["pool"], 1)
                    t = slice(2 * half, 2 * half + 2)
                    nc.gpsimd.tensor_copy(v32[u][:, t, :, 0:DK],
                                          vraw[u][:, t].rearrange("p t (h d) -> p t h d", d=DK)).then_inc(v32_ok.sem, 1)

                def bias(n, u, half):
                    pool.wait_ge(h0_in.sems[u], h0_in.at(n, u))
                    t = slice(2 * half, 2 * half + 2)
                    nc.gpsimd.tensor_tensor(h0[u][:, t], h0[u][:, t], bo[:].unsqueeze(1).broadcast_to([TILE, 2, C]),
                                            ALU.add).then_inc(hb_ok.sem, 1)

                def position(i, r, c):
                    s, k, n, q, g, u = where(i, r)
                    if c == 0 and r % 8 == 3 and known(n, 0, PAIRS - 1):
                        pool.wait_ge(pv_ok.sem, pv_ok.at(s - 4))
                        values(n + 1, 1 - u, 0)
                    if c == 0 and r % 8 == 5 and known(n, 0, PAIRS - 1):
                        values(n + 1, 1 - u, 1)
                    if c == 0 and r % 8 == 7 and known(n, 0, PAIRS - 1):
                        bias(n + 1, 1 - u, 0)
                    if c == 0 and r % 8 == 1 and known(n, 1, PAIRS):
                        bias(n, u, 1)
                    if c == 1 and q == 2 and known(k, -1, IMAGES - 1):
                        g1, u1 = (g + 1) % 2, (r + 4) // 8 % 2
                        pool.wait_ge(en_ok.sem, en_ok.at(k + 1))
                        pool.wait_ge(num_ok.sem, num_ok.at(k - 1))
                        nc.gpsimd.tensor_tensor(
                            ev[g1][:], vnext[u1][:, 2 * g1:2 * g1 + 2, :].rearrange("p t (h d) -> p t h d", d=DK),
                            en[g1][:].unsqueeze(3).broadcast_to([TILE, 2, HEADS, DK]), ALU.mult).then_inc(ev_ok.sem, 1)
                    what, t = TAIL.get(2 * q + c, (None, 0))
                    if what == "ott" and known(k, 1, IMAGES + 1):
                        pool.wait_ge(num_ok.sem, num_ok.at(k - 1, t + 1))
                        (pool.wait_ge(at_ok.sem, at_ok.at(k - 1, 1)) if t else pool.wait_ge(at_ok.sem, at_ok.at(k - 2)))
                        nc.gpsimd.tensor_tensor(attn[:], num[:], rden[:].unsqueeze(2).broadcast_to([TILE, HEADS, DK]),
                                                           ALU.mult).then_inc(attn_ok.sem, 1)

                pool.wait_ge(setup, 16 * 7)
                for half in range(2):
                    values(0, 0, half)
                    bias(0, 0, half)
                positions(pool, position)

            @block.scalar
            def _(act):
                for s in (p_ok, ot_ok, en_ok, att_ok):
                    s.open(act)

                def position(i, r, c):
                    s, k, n, q, g, u = where(i, r)
                    if known(s, 0, SLOTS):
                        act.wait_ge(pv_ok.sem, pv_ok.at(s - 1, c + 1))
                        for b in range(2):
                            act.wait_ge(e_sel.sem, e_sel.at(s, 2 * c + b + 1))
                            act.activation(probs[c][:, b, :], psE[:, b, 0:PAIR], ACT.Exp, scale=DK ** -0.5).then_inc(p_ok.sem, 1)
                    if c == 0 and known(s, 1, SLOTS + 1):
                        _, k0, _, q0, g0, _ = where(i, r - 1)
                        act.wait_ge(pv_ok.sem, pv_ok.at(s - 1))
                        act.wait_ge(ott_ok.sem, ott_ok.at(k0 - 2))
                        act.activation(ot[g0][:, q0, :], psO[:, 0:S], ACT.Copy).then_inc(ot_ok.sem, 1)
                    if c == 1 and q == 2 and known(k, -1, IMAGES - 1):
                        g1 = (g + 1) % 2
                        act.wait_ge(mch.sem, mch.at(k + 1))
                        act.wait_ge(ev_ok.sem, ev_ok.at(k - 1))
                        act.wait_ge(num_ok.sem, num_ok.at(k - 1))
                        act.activation(en[g1][:], ea[:], ACT.Exp, scale=DK ** -0.5).then_inc(en_ok.sem, 1)
                    what, t = TAIL.get(2 * q + c, (None, 0))
                    if what == "at" and known(k, 1, IMAGES + 1):
                        act.wait_ge(at_ok.sem, at_ok.at(k - 1, t + 1))
                        (act.wait_ge(wo_ok.sem, wo_ok.at(k - 1, 1)) if t else act.wait_ge(wo_ok.sem, wo_ok.at(k - 2)))
                        act.activation(attnT[:], psM[:, 0:2 * TILE].rearrange("p (h t) -> p h t", h=2), ACT.Copy).then_inc(att_ok.sem, 1)

                positions(act, position)

            @block.vector
            def _(dve):
                for s in (s_max, e_sel, mch, mrow_ok, nrm, num_ok, h1_ok):
                    s.open(dve)
                dve.wait_ge(setup, 16 * 7)
                nc.vector.tensor_copy(ident16[:], ident[0:TILE, 0:TILE]).then_inc(made, 1)
                nc.vector.tensor_copy(never[:], never32[:]).then_inc(made, 1)

                def select(b, cut):
                    out = psE[:, b, 0:PAIR].rearrange("p (h t) -> p h t", h=2)[:, :, cut]
                    data = psF[:, 2 * TILE * b:2 * TILE * (b + 1)].rearrange("p (h t) -> p h t", h=2)
                    return nc.vector.copy_predicated(out, maskE[:].unsqueeze(1).broadcast_to([TILE, 2, TILE]), data)

                def position(i, r, c):
                    s, k, n, q, g, u = where(i, r)
                    cut = slice(c * TILE, (c + 1) * TILE)
                    s1, k1, n1, q1, g1, u1 = where(i, r + LAG)
                    if known(s1, 0, SLOTS):
                        if q1 == 0 and c == 0:
                            dve.wait_ge(mch.sem, mch.at(k1 - 2))
                        for b in range(2):
                            dve.wait_ge(s_ok.sem, s_ok.at(s1, 3 * c + b + 1))
                            nc.vector.tensor_reduce(mx[g1][:, c, 4 * q1 + 2 * b:4 * q1 + 2 * b + 2],
                                                    psS[:, b, 0:PAIR].rearrange("p (h t) -> p h t", h=2),
                                                    AX.X, ALU.max).then_inc(s_max.sem, 1)
                        dve.wait_ge(s_ok.sem, s_ok.at(s1, 3 * c + 3))
                        nc.vector.tensor_reduce(mxU[g1][:, c, 4 * q1:4 * q1 + 4], psD[:, 0:4 * TILE].rearrange("p (h t) -> p h t", h=4),
                                                AX.X, ALU.max).then_inc(s_max.sem, 1)
                    if known(s, 0, SLOTS):
                        for b in range(2):
                            dve.wait_ge(e_ok.sem, e_ok.at(s, 2 * c + b + 1))
                            dve.sem_inc(passed["dve"], 1)
                            select(b, cut).then_inc(e_sel.sem, 1)
                    if q1 == 3 and c == 1 and known(k1, 0, IMAGES):
                        dve.wait_ge(tokens_in.sems[u1], tokens_in.at(n1, u1))
                        dve.wait_ge(s_max.sem, s_max.at(s1))
                        cn = cnext[u1][:, 2 * g1:2 * g1 + 2, :]
                        nc.vector.tensor_tensor(ml[:], mx[g1][:], mxU[g1][:], ALU.max).then_inc(mch.sem, 1)
                        dve.wait_ge(mch.sem, mch.at(k1, 1))
                        nc.vector.tensor_tensor(mf[:], ml[:], cn, ALU.max).then_inc(mch.sem, 1)
                        dve.wait_ge(mch.sem, mch.at(k1, 2))
                        dve.wait_ge(mtr.sem, mtr.at(k1 - 1))
                        nc.vector.tensor_scalar(nm[:, :, 0, :], mf[:], -1.0, None, ALU.mult).then_inc(mch.sem, 1)
                        dve.wait_ge(mch.sem, mch.at(k1, 3))
                        nc.vector.scalar_tensor_tensor(nm[:, :, 1, :], mf[:], -1.0, nm[:, :, 0, :], ALU.mult, ALU.subtract).then_inc(mch.sem, 1)
                        dve.wait_ge(mch.sem, mch.at(k1, 4))
                        nc.vector.tensor_tensor(mt[:], nm[:, :, 0, :], nm[:, :, 1, :], ALU.add).then_inc(mch.sem, 1)
                        dve.wait_ge(mch.sem, mch.at(k1, 5))
                        dve.wait_ge(en_ok.sem, en_ok.at(k1 - 1))
                        nc.vector.tensor_tensor(ea[:], cn, mt[:], ALU.add).then_inc(mch.sem, 1)
                    what, t = TAIL.get(2 * q + c, (None, 0))
                    if what == "mtr" and known(k, -1, IMAGES - 1):
                        dve.wait_ge(mtr.sem, mtr.at(k + 1))
                        dve.wait_ge(m_in.sems[(g + 1) % 2], m_in.at(k - 1, (g + 1) % 2))
                        nc.vector.tensor_copy(mrow[(g + 1) % 2][:], psM16[0:2 * HEADS, 0:S]).then_inc(mrow_ok.sem, 1)
                    if what == "ott" and known(k, 1, IMAGES + 1):
                        o = psM[0:TILE, :].rearrange("p (h e) -> p h e", e=32)
                        e = en[1 - g][:, t, :]
                        dve.wait_ge(ott_ok.sem, ott_ok.at(k - 1, t + 1))
                        dve.wait_ge(en_ok.sem, en_ok.at(k - 1))
                        (dve.wait_ge(attn_ok.sem, attn_ok.at(k - 1, 1)) if t else dve.wait_ge(attn_ok.sem, attn_ok.at(k - 2)))
                        nc.vector.tensor_tensor(den[:], o[:, :, DK], e, ALU.add).then_inc(nrm.sem, 1)
                        dve.wait_ge(nrm.sem, nrm.at(k - 1, 2 * t + 1))
                        nc.vector.reciprocal(rden[:], den[:]).then_inc(nrm.sem, 1)
                        dve.wait_ge(ev_ok.sem, ev_ok.at(k - 1))
                        nc.vector.tensor_tensor(num[:], o[:, :, 0:DK], ev[1 - g][:, t], ALU.add).then_inc(num_ok.sem, 1)
                    if what == "wo" and known(k, 1, IMAGES + 1):
                        _, _, n0, _, g0, u0 = where(i, r - 4)
                        dve.wait_ge(wo_ok.sem, wo_ok.at(k - 1, t + 1))
                        dve.wait_ge(hb_ok.sem, hb_ok.at(n0))
                        dve.wait_ge(h1_out.sems[g0], h1_out.at(k - 3, g0))
                        nc.vector.tensor_tensor(h1[g0][:, t, :], psM[0:TILE, 0:C], h0[u0][:, 2 * g0 + t, :], ALU.add).then_inc(h1_ok.sem, 1)

                positions(dve, position)

            @block.tensor
            def _(pe):
                for s in (s_ok, e_ok, pv_ok, mtr, ott_ok, at_ok, wo_ok):
                    s.open(pe)
                pe.wait_ge(made, 2)
                pe.wait_ge(made_v32, 4)
                pe.wait_ge(setup, 16 * 7)

                def stage_s(s, q, g, u, c, n):
                    if q % 2 == 0 and g == 0 and c == 0:
                        pe.wait_ge(stacks[q // 2].sems[u], stacks[q // 2].at(n, u))
                    mid, first, second = slice(g * S + c * TILE, g * S + (c + 1) * TILE), g * S, g * S + TILE
                    for b in range(2):
                        pe.wait_ge(s_max.sem, s_max.at(s, b + 1) if c else s_max.at(s - 1, 3 + b + 1))
                        for j in range(2):
                            h = 4 * q + 2 * b + j
                            low, up, key = L[u][0:STACK, h], U[u][0:STACK, h], K[u][0:STACK, h]
                            out = psS[:, b, j * S:(j + 1) * S]
                            if c == 0:
                                nc.tensor.matmul(out[:, 0:TILE], low[:, mid], key[:, first:second], start=(j == 0), stop=False)
                                nc.tensor.matmul(out[:, TILE:S], up[:, mid], key[:, second:second + TILE], start=False, stop=False)
                            else:
                                nc.tensor.matmul(out, low[:, mid], key[:, first:first + S], start=(j == 0), stop=False)
                        pair = psS[:, b, 0:PAIR].rearrange("p (h t) -> p h t", h=2)
                        if c == 0:
                            last = nc.tensor.matmul(pair[:, :, 0:TILE + 1], ident16[:], neverS, start=False, stop=True)
                        else:
                            last = nc.tensor.matmul(pair[:, :, TILE:S], ident16[:], neverS[:, :, 0:TILE], start=False, stop=True)
                        last.then_inc(s_ok.sem, 1)
                    pe.wait_ge(s_max.sem, s_max.at(s, 3) if c else s_max.at(s - 1))
                    for j in range(4):
                        h = 4 * q + j
                        nc.tensor.matmul(psD[:, j * TILE:(j + 1) * TILE], U[u][0:STACK, h][:, mid], K[u][0:STACK, h][:, mid],
                                         start=(j == 0), stop=False)
                    nc.tensor.matmul(psD[:, 0:4 * TILE], ident16[:], neverU, start=False, stop=True).then_inc(s_ok.sem, 1)

                def stage_e(s, k, q, g, u, c):
                    if q == 0 and c == 0:
                        pe.wait_ge(m_in.sems[g], m_in.at(k, g))
                    mid, first, second = slice(g * S + c * TILE, g * S + (c + 1) * TILE), g * S, g * S + TILE
                    pe.wait_ge(e_sel.sem, e_sel.at(s, 2) if c else e_sel.at(s - 1))
                    for j in range(4):
                        h = 4 * q + j
                        nc.tensor.matmul(psF[:, j * TILE:(j + 1) * TILE], K[u][:, h][:, mid], U[u][:, h][:, mid], start=True, stop=True)
                    for b in range(2):
                        pe.wait_ge(p_ok.sem, p_ok.at(s, b + 1) if c else p_ok.at(s - 1, 2 + b + 1))
                        for j in range(2):
                            h = 4 * q + 2 * b + j
                            low, up, key = L[u][:, h], U[u][:, h], K[u][:, h]
                            out = psE[:, b, j * S:(j + 1) * S]
                            if c == 0:
                                nc.tensor.matmul(out, key[:, mid], low[:, first:first + S], start=(j == 0), stop=False)
                            else:
                                nc.tensor.matmul(out[:, 0:TILE], key[:, mid], up[:, first:second], start=(j == 0), stop=False)
                                nc.tensor.matmul(out[:, TILE:S], key[:, mid], low[:, second:second + TILE], start=False, stop=False)
                        pair = psE[:, b, 0:PAIR].rearrange("p (h t) -> p h t", h=2)
                        if c == 0:
                            last = nc.tensor.matmul(pair[:, :, 0:TILE], ident16[:], neverE[:, :, 1:TILE + 1], start=False, stop=True)
                        else:
                            last = nc.tensor.matmul(pair[:, :, TILE - 1:S], ident16[:], neverE, start=False, stop=True)
                        last.then_inc(e_ok.sem, 1)

                def stage_v(s, n, q, g, u, c):
                    pe.wait_ge(p_ok.sem, p_ok.at(s, 2 * c + 2))
                    if c == 0:
                        pe.wait_ge(v32_ok.sem, v32_ok.at(n))
                        pe.wait_ge(ot_ok.sem, ot_ok.at(s - 1))
                    for j in range(4):
                        last = nc.tensor.matmul(psO[32 * j:32 * j + 32, 0:S], v32[u][:, 2 * g + c, 4 * q + j, :],
                                                probs[c][:, j // 2, (j % 2) * S:(j % 2 + 1) * S],
                                                start=(c == 0), stop=(c == 1))
                    last.then_inc(pv_ok.sem, 1)

                def position(i, r, c):
                    s, k, n, q, g, u = where(i, r)
                    s1, k1, n1, q1, g1, u1 = where(i, r + LAG)
                    if known(s1, 0, SLOTS):
                        stage_s(s1, q1, g1, u1, c, n1)
                    if known(s, 0, SLOTS):
                        stage_e(s, k, q, g, u, c)
                    sv, kv, nv, qv, gv, uv = where(i, r if c else r - 1)
                    if known(sv, 0, SLOTS):
                        stage_v(sv, nv, qv, gv, uv, 1 - c)
                    what, t = TAIL.get(2 * q + c, (None, 0))
                    g0 = (g + 1) % 2
                    if what == "mtr" and known(k, -1, IMAGES - 1):
                        pe.wait_ge(num_ok.sem, num_ok.at(k - 1))
                        pe.wait_ge(mch.sem, mch.at(k + 1))
                        for h in range(2):
                            last = nc.tensor.transpose(psM16[0:2 * HEADS, h * TILE:(h + 1) * TILE],
                                                       nm[:, h].rearrange("p l h -> p (l h)"), ident16[:])
                        last.then_inc(mtr.sem, 1)
                    if known(k, 1, IMAGES + 1):
                        if what == "ott":
                            (pe.wait_ge(h1_ok.sem, h1_ok.at(k - 1, 1)) if t else pe.wait_ge(h1_ok.sem, h1_ok.at(k - 2)))
                            pe.wait_ge(ot_ok.sem, ot_ok.at(s - 3 if t else s - 1))
                            for j in range(QUADS):
                                last = nc.tensor.transpose(psM[0:TILE, 128 * j:128 * j + 128],
                                                           ot[g0][:, j, t * TILE:(t + 1) * TILE], ident[:])
                            last.then_inc(ott_ok.sem, 1)
                        if what == "at":
                            pe.wait_ge(attn_ok.sem, attn_ok.at(k - 1, t + 1))
                            if t and known(k, -1, IMAGES - 1):
                                pe.wait_ge(mrow_ok.sem, mrow_ok.at(k + 1))
                            a = attn[:].rearrange("p h d -> p (h d)")
                            for j in range(2):
                                last = nc.tensor.transpose(psM[:, j * TILE:(j + 1) * TILE], a[:, 128 * j:128 * j + 128],
                                                           ident[0:TILE, 0:TILE])
                            last.then_inc(at_ok.sem, 1)
                        if what == "wo":
                            pe.wait_ge(att_ok.sem, att_ok.at(k - 1, t + 1))
                            for j in range(2):
                                last = nc.tensor.matmul(psM[0:TILE, 0:C], attnT[:, j, :], wo[:, j, :],
                                                        start=(j == 0), stop=(j == 1))
                            last.then_inc(wo_ok.sem, 1)

                positions(pe, position)


EXPERTS, CHOICES = 8, 2
EXPERT_HIDDEN, SHARED_HIDDEN = 512, 1024
CAP = -(-(-(-T * CHOICES // EXPERTS)) * 5 // 4)
BLOCK = 4
BLOCKS = T // (BLOCK * TILE)


def feed_forward(nc, d, name, x, y_dram, tiles, hidden, steps, body, experts):
    chunks = hidden // 128
    N = tiles * TILE
    banks = -(-tiles // 2)
    sets = min(experts, 2)
    per_expert = steps // experts
    ahead = 4
    with stage(nc) as ctx:
        def sb(x, shape, dt=F32):
            return ctx.enter_context(nc.sbuf_tensor(name + x, shape, dt))

        def pb(x, shape, dt=F32):
            return ctx.enter_context(nc.psum_tensor(name + x, shape, dt))

        def signal(x, per=1):
            return Signal(nc, ctx, name + x, per)

        def transfers(x, per=1):
            return Transfers(nc, ctx, name + x, per)

        xin = [sb(f"xin{u}", [TILE, tiles, C]) for u in range(2)]
        xh = [sb(f"xh{u}", [128, 2, N], BF16) for u in range(2)]
        xl = [sb(f"xl{u}", [128, 2, N], BF16) for u in range(2)]
        raw1, raw2 = sb("raw1", [128, 2, hidden]), sb("raw2", [128, chunks, C])
        rawb1, rawb2 = sb("rawb1", [128, chunks]), sb("rawb2", [TILE, C])
        w1h = [sb(f"w1h{w}", [128, 2, hidden], BF16) for w in range(sets)]
        w1l = [sb(f"w1l{w}", [128, 2, hidden], BF16) for w in range(sets)]
        w2h = [sb(f"w2h{w}", [128, chunks, C], BF16) for w in range(sets)]
        w2l = [sb(f"w2l{w}", [128, chunks, C], BF16) for w in range(sets)]
        b1 = [sb(f"b1{w}", [128, chunks]) for w in range(sets)]
        b2 = [sb(f"b2{w}", [TILE, C]) for w in range(sets)]
        g32 = sb("g32", [128, chunks, N])
        gh = [sb(f"gh{u}", [128, chunks, N], BF16) for u in range(2)]
        gl = [sb(f"gl{u}", [128, chunks, N], BF16) for u in range(2)]
        y = [sb(f"y{u}", [TILE, tiles, C]) for u in range(2)]
        ident = sb("ident", [128, 128])

        psT = pb("psT", [128, 2, 512])
        psG = [pb(f"psG{j}", [128, 512]) for j in range(ahead)]
        psY = [pb(f"psY{j}", [TILE, 2, C]) for j in range(2)]

        setup = semaphore(nc, ctx, name + "constants_loaded")
        x_in, y_out, w_in = transfers("x_in"), transfers("y_out"), transfers("weights_in", 4)
        t_ok, xh_ok, xl_ok = signal("xT_in_psum"), signal("xh"), signal("xl")
        g_ok, gelu_ok, split_ok = signal("h_in_psum", chunks), signal("gelu", chunks), signal("g_split", chunks)
        gh_ok = signal("gh", chunks)
        y_ok, yev_ok = signal("y_in_psum", banks), signal("y", banks)
        wh_ok, wl_ok = signal("weights_hi", 2), signal("weights_lo", 4)
        passed = {e: semaphore(nc, ctx, name + "passed_" + e) for e in ("sp", "dve")}

        def positions(eng, position):
            for r in range(-2, 0):
                position(0, r)
            for r in range(body):
                position(0, r)
            with eng.Fori(1, steps // body - 1) as j:
                for r in range(body):
                    position(j, r)
            for r in range(body):
                position(steps // body - 1, r)

        def weights_at(i, r):
            if experts == 1:
                return 0, 0
            return i * (body // per_expert) + r // per_expert, r // per_expert % 2

        def reused(signal, n, m):
            return signal.at(n, m - ahead + 1) if m >= ahead else signal.at(n - 1, chunks - ahead + m + 1)

        def new_weights(i, r):
            if experts == 1 or r % per_expert != 1:
                return None
            e, w = weights_at(i, r)
            return (e + 1, 1 - w) if known(e, 0, experts - 1) else None

        with nc.Block() as block:
            @block.sync
            def _(sp):
                for s in (x_in, y_out, w_in):
                    s.open(sp)
                sp.dma_start(ident[:], d["ident"]).then_inc(setup, 16)

                def load_weights(e, w):
                    for dst, src in ((raw1, "w1"), (raw2, "w2"), (rawb1, "b1"), (rawb2, "b2")):
                        sp.dma_start(dst[:], d[name + src][bass.ds(e, 1)].squeeze(0)).then_inc(w_in.sems[w], 16)

                def load_x(n, u):
                    sp.dma_start(xin[u][:], tiles_of(x[bass.ds(n * N, N), :])).then_inc(x_in.sems[u], 16)

                load_weights(0, 0)
                load_x(0, 0)
                load_x(1, 1)
                if experts > 1:
                    sp.wait_ge(wl_ok.sem, wl_ok.at(0))
                    sp.wait_ge(wh_ok.sem, wh_ok.at(0))
                    load_weights(1, 1)

                def position(i, r):
                    n, u = i * body + r, r % 2
                    if known(n, -2, steps - 4):
                        sp.wait_ge(t_ok.sem, t_ok.at(n + 2))
                        sp.sem_inc(passed["sp"], 1)
                        load_x(n + 4, u)
                    new = new_weights(i, r)
                    if new is not None and known(new[0], 0, experts - 1):
                        sp.wait_ge(wl_ok.sem, wl_ok.at(new[0]))
                        sp.sem_inc(passed["sp"], 1)
                        sp.wait_ge(wh_ok.sem, wh_ok.at(new[0]))
                        sp.sem_inc(passed["sp"], 1)
                        load_weights(new[0] + 1, 1 - new[1])
                    if known(n, 0, steps):
                        sp.wait_ge(yev_ok.sem, yev_ok.at(n))
                        sp.sem_inc(passed["sp"], 1)
                        sp.dma_start(tiles_of(y_dram[bass.ds(n * N, N), :]), y[u][:]).then_inc(y_out.sems[u], 16)

                positions(sp, position)
                sp.wait_ge(y_out.sems[0], y_out.at(steps - 2, 0))
                sp.wait_ge(y_out.sems[1], y_out.at(steps - 1, 1))

            @block.scalar
            def _(act):
                for s in (xh_ok, gelu_ok, wh_ok):
                    s.open(act)

                def split_weights(e, w):
                    act.wait_ge(w_in.sems[w], w_in.at(e, w))
                    act.wait_ge(y_ok.sem, y_ok.at((e - 1) * per_expert - 1))
                    act.activation(w1h[w][:], raw1[:], ACT.Copy).then_inc(wh_ok.sem, 1)
                    act.activation(w2h[w][:], raw2[:], ACT.Copy).then_inc(wh_ok.sem, 1)

                def position(i, r):
                    n, u = i * body + r, r % 2
                    if known(n, -1, steps - 1):
                        _, w = weights_at(i, r + 1)
                        for m in range(chunks):
                            act.wait_ge(g_ok.sem, g_ok.at(n + 1, m + 1))
                            if m == 0:
                                act.wait_ge(wl_ok.sem, wl_ok.at(weights_at(i, r + 1)[0]))
                            act.wait_ge(split_ok.sem, split_ok.at(n, m + 1))
                            act.activation(g32[:, m, :], psG[m % ahead][:, 0:N], ACT.Gelu, bias=b1[w][:, m:m + 1]).then_inc(gelu_ok.sem, 1)
                    if known(n, -2, steps - 2):
                        act.wait_ge(t_ok.sem, t_ok.at(n + 2))
                        act.wait_ge(g_ok.sem, g_ok.at(n))
                        act.activation(xh[u][:], psT[:, :, 0:N], ACT.Copy).then_inc(xh_ok.sem, 1)
                    new = new_weights(i, r)
                    if new is not None:
                        split_weights(*new)

                act.wait_ge(w_in.sems[0], w_in.at(0, 0))
                act.activation(w1h[0][:], raw1[:], ACT.Copy).then_inc(wh_ok.sem, 1)
                act.activation(w2h[0][:], raw2[:], ACT.Copy).then_inc(wh_ok.sem, 1)
                positions(act, position)

            @block.vector
            def _(dve):
                for s in (xl_ok, gh_ok, split_ok, yev_ok, wl_ok):
                    s.open(dve)

                def split_weights(e, w):
                    dve.wait_ge(wh_ok.sem, wh_ok.at(e))
                    nc.vector.tensor_tensor(w1l[w][:], raw1[:], w1h[w][:], ALU.subtract).then_inc(wl_ok.sem, 1)
                    nc.vector.tensor_tensor(w2l[w][:], raw2[:], w2h[w][:], ALU.subtract).then_inc(wl_ok.sem, 1)
                    nc.vector.tensor_copy(b1[w][:], rawb1[:]).then_inc(wl_ok.sem, 1)
                    nc.vector.tensor_copy(b2[w][:], rawb2[:]).then_inc(wl_ok.sem, 1)

                def position(i, r):
                    n, u = i * body + r, r % 2
                    if known(n, -1, steps - 1):
                        v = 1 - u
                        dve.wait_ge(y_ok.sem, y_ok.at(n - 1))
                        for m in range(chunks):
                            dve.wait_ge(gelu_ok.sem, gelu_ok.at(n + 1, m + 1))
                            nc.vector.tensor_copy(gh[v][:, m, :], g32[:, m, :]).then_inc(gh_ok.sem, 1)
                            dve.wait_ge(gh_ok.sem, gh_ok.at(n + 1, m + 1))
                            nc.vector.tensor_tensor(gl[v][:, m, :], g32[:, m, :], gh[v][:, m, :], ALU.subtract).then_inc(split_ok.sem, 1)
                    if known(n, -2, steps - 2):
                        dve.wait_ge(xh_ok.sem, xh_ok.at(n + 2))
                        nc.vector.tensor_tensor(xl[u][:], psT[:, :, 0:N], xh[u][:], ALU.subtract).then_inc(xl_ok.sem, 1)
                    new = new_weights(i, r)
                    if new is not None:
                        split_weights(*new)
                    if known(n, 0, steps):
                        _, w = weights_at(i, r)
                        dve.wait_ge(y_out.sems[u], y_out.at(n - 2, u))
                        for b in range(banks):
                            here = min(2, tiles - 2 * b)
                            dve.wait_ge(y_ok.sem, y_ok.at(n, b + 1))
                            nc.vector.tensor_tensor(y[u][:, 2 * b:2 * b + here, :], psY[b % 2][:, 0:here, :],
                                                              b2[w][:].unsqueeze(1).broadcast_to([TILE, here, C]), ALU.add).then_inc(yev_ok.sem, 1)

                split_weights(0, 0)
                positions(dve, position)

            @block.tensor
            def _(pe):
                for s in (t_ok, g_ok, y_ok):
                    s.open(pe)
                pe.wait_ge(setup, 16)

                def position(i, r):
                    n, u = i * body + r, r % 2
                    if known(n, -1, steps - 1):
                        v = 1 - u
                        e, w = weights_at(i, r + 1)
                        pe.wait_ge(wl_ok.sem, wl_ok.at(e))
                        pe.wait_ge(xl_ok.sem, xl_ok.at(n + 1))
                        for m in range(chunks):
                            pe.wait_ge(gelu_ok.sem, reused(gelu_ok, n + 1, m))
                            rows = slice(128 * m, 128 * m + 128)
                            three_products(nc, psG[m % ahead][:, 0:N], [
                                (w1h[w][:, c, rows], w1l[w][:, c, rows], xh[v][:, c, :], xl[v][:, c, :]) for c in range(2)]).then_inc(g_ok.sem, 1)
                    if known(n, -2, steps - 2):
                        pe.wait_ge(x_in.sems[u], x_in.at(n + 2, u))
                        pe.wait_ge(xl_ok.sem, xl_ok.at(n + 1))
                        for c in range(2):
                            for t in range(tiles):
                                last = nc.tensor.transpose(psT[:, c, t * TILE:(t + 1) * TILE], xin[u][:, t, c * 128:(c + 1) * 128],
                                                           ident[0:TILE, 0:TILE])
                        last.then_inc(t_ok.sem, 1)
                    if known(n, 0, steps):
                        _, w = weights_at(i, r)
                        pe.wait_ge(split_ok.sem, split_ok.at(n))
                        for b in range(banks):
                            if b >= 2:
                                pe.wait_ge(yev_ok.sem, yev_ok.at(n, b - 1))
                            else:
                                pe.wait_ge(yev_ok.sem, yev_ok.at(n - 1, max(j for j in range(banks) if j % 2 == b) + 1))
                            for t in range(2 * b, min(2 * b + 2, tiles)):
                                cut = slice(t * TILE, (t + 1) * TILE)
                                last = three_products(nc, psY[b % 2][:, t % 2, :], [
                                    (gh[u][:, m, cut], gl[u][:, m, cut], w2h[w][:, m, :], w2l[w][:, m, :]) for m in range(chunks)])
                            last.then_inc(y_ok.sem, 1)

                positions(pe, position)


TILES = T // TILE
ROWS_ALL = EXPERTS * CAP
NOWHERE = 4 * ROWS_ALL
BITS = 30


def route(nc, d):
    with stage(nc) as ctx:
        def sb(x, shape, dt=F32):
            return ctx.enter_context(nc.sbuf_tensor("p3_" + x, shape, dt))

        def pb(x, shape, dt=F32):
            return ctx.enter_context(nc.psum_tensor("p3_" + x, shape, dt))

        def signal(x, per=1):
            return Signal(nc, ctx, "p3_" + x, per)

        def transfers(x, per=1):
            return Transfers(nc, ctx, "p3_" + x, per)

        def plain(x):
            return semaphore(nc, ctx, "p3_" + x)

        N = BLOCK * TILE
        wide = [TILE, TILES, EXPERTS]
        ident, eps = sb("ident", [128, 128]), sb("eps", [TILE, 1])
        wz, bz, eb = sb("wz", [128, 2, EXPERTS]), sb("bz", [TILE, EXPERTS]), sb("eb", [TILE, EXPERTS])
        iota, rows0 = sb("iota", [TILE, EXPERTS]), sb("rows0", [TILE, EXPERTS])
        tri32, ones32 = sb("tri32", [TILE, TILE]), sb("ones32", [TILE, TILE])
        tri, ones = sb("tri", [TILE, TILE], BF16), sb("ones", [TILE, TILE], BF16)
        zero = sb("zero", [TILE, C])
        hin = [sb(f"hin{u}", [TILE, BLOCK, C]) for u in range(2)]
        xf = [sb(f"xf{u}", [TILE, BLOCK, C]) for u in range(2)]
        stats, mv = sb("stats", [TILE, BLOCK, 6]), sb("mv", [TILE, BLOCK, 2])
        std, rstd = sb("std", [TILE, BLOCK]), sb("rstd", [TILE, BLOCK])
        xT, zT = sb("xT", [128, 2, N]), sb("zT", [EXPERTS, N])
        z, c, key, oh1, oh2, c2, w, t1, t2 = (sb(x, wide) for x in
                                             ("z", "c", "key", "oh1", "oh2", "c2", "w", "t1", "t2"))
        m16 = sb("m16", wide, BF16)
        m1, m2, i1, r1, w1, w2 = (sb(x, [TILE, TILES]) for x in ("m1", "m2", "i1", "r1", "w1", "w2"))
        onesrow = sb("onesrow", [TILE, TILES])
        cur, cand, bit, take = (sb(x, [TILE, EXPERTS], U32) for x in ("cur", "cand", "bit", "take"))
        bitf = sb("bitf", [TILE, 1])
        part, more = sb("part", [TILE, EXPERTS]), sb("more", [TILE, EXPERTS])
        sidx, gidx = sb("sidx", [TILE, TILES, 2], U32), sb("gidx", [TILE, TILES, 2], U32)
        gw = sb("gw", [TILE, TILES, 2])
        idx = [sb(f"idx{u}", [TILE, BLOCK, 2], U32) for u in range(2)]

        psT = pb("psT", [128, 2, 512])
        psZ, psB, psC = pb("psZ", [EXPERTS, 512]), pb("psB", [TILE, BLOCK, EXPERTS]), pb("psC", [TILE, EXPERTS])
        psR = psT[0:TILE].rearrange("p b x -> p (b x)").rearrange("p (t e) -> p t e", e=EXPERTS)
        psU = pb("psU", [TILE, 2, 512])
        psUw = psU[:].rearrange("p b x -> p (b x)").rearrange("p (t e) -> p t e", e=EXPERTS)

        setup, made = plain("constants_loaded"), plain("constants_made")
        zeroed, rinsed = plain("zero_ready"), plain("rows_zeroed")
        h_in, xf_out = transfers("h1_in"), transfers("xf_out")
        stats_ok, mv_ok, std_ok, rstd_ok, xf_ok = (signal(x) for x in ("stats", "mv", "std", "rstd", "xf"))
        t_ok, xT_ok, z_ok, zT_ok, zz_ok, zw_ok = (signal(x) for x in
                                                 ("xT_in_psum", "xT", "z_in_psum", "zT", "z_transposed", "z"))
        sig_ok = plain("sigmoid")
        search, counted = signal("search", 8), signal("counted")
        chain, asked, ranked = plain("chain"), plain("mask_ready"), plain("ranks_in_psum")
        tables_out = plain("tables_stored")
        x_in, idx_ok, sent = transfers("xf_in"), signal("idx"), Transfers(nc, ctx, "p3_rows_sent", 8, pool=True)
        passed = {e: plain("passed_" + e) for e in ("sp", "pool", "dve", "pe")}

        def positions(eng, position):
            for n in (-2, -1, 0, 1):
                position(n, n % 2)
            with eng.Fori(1, BLOCKS // 2 - 2) as j:
                for u in range(2):
                    position(j * 2 + u, u)
            for n in range(BLOCKS - 4, BLOCKS):
                position(n, n % 2)

        with nc.Block() as block:
            @block.sync
            def _(sp):
                for s in (h_in, xf_out, x_in):
                    s.open(sp)

                def load(n, u):
                    sp.dma_start(hin[u][:], tiles_of(d["h1"][bass.ds(n * N, N), :])).then_inc(h_in.sems[u], 16)

                load(0, 0)
                load(1, 1)
                for dst, name in ((ident, "ident"), (wz, "proj_w"), (bz, "proj_b"), (eb, "expert_bias"), (iota, "iota"),
                                  (rows0, "rows0"), (tri32, "tri")):
                    sp.dma_start(dst[:], d[name]).then_inc(setup, 16)
                sp.wait_ge(zeroed, 1)
                each = ROWS_ALL // TILE
                sp.dma_start(d["xe"].rearrange("(p r) c -> p r c", r=each),
                             zero[:].unsqueeze(1).broadcast_to([TILE, each, C])).then_inc(rinsed, 16)

                def position(n, u):
                    if known(n, -2, BLOCKS - 2):
                        sp.wait_ge(xf_ok.sem, xf_ok.at(n + 2))
                        sp.sem_inc(passed["sp"], 1)
                        if known(n, -2, BLOCKS - 4):
                            load(n + 4, u)
                        sp.dma_start(tiles_of(d["xf"][bass.ds((n + 2) * N, N), :]), xf[u][:]).then_inc(xf_out.sems[u], 16)

                positions(sp, position)
                sp.wait_ge(xf_out.sems[0], xf_out.at(BLOCKS - 2, 0))
                sp.wait_ge(xf_out.sems[1], xf_out.at(BLOCKS - 1, 1))

                def load_x(n, u):
                    sp.dma_start(xf[u][:], tiles_of(d["xf"][bass.ds(n * N, N), :])).then_inc(x_in.sems[u], 16)

                sp.wait_ge(t_ok.sem, t_ok.at(BLOCKS - 1))
                load_x(0, 0)
                load_x(1, 1)
                sp.wait_ge(asked, 3)
                for name, src in (("gidx", gidx), ("gw", gw)):
                    sp.dma_start(d[name], src[:]).then_inc(tables_out, 16)
                with sp.Fori(0, BLOCKS // 2 - 1) as j:
                    for u in range(2):
                        sp.wait_ge(sent.sems[u], sent.at(j * 2 + u, u))
                        sp.sem_inc(passed["sp"], 1)
                        load_x(j * 2 + u + 2, u)
                sp.wait_ge(tables_out, 32)

            @block.gpsimd
            def _(pool):
                pool.wait_ge(rinsed, 16)
                with pool.Fori(0, BLOCKS // 2) as j:
                    for u in range(2):
                        n = j * 2 + u
                        pool.wait_ge(x_in.sems[u], x_in.at(n, u))
                        pool.sem_inc(passed["pool"], 1)
                        pool.wait_ge(idx_ok.sem, idx_ok.at(n))
                        pool.sem_inc(passed["pool"], 1)
                        for t in range(BLOCK):
                            for k in range(2):
                                nc.gpsimd.indirect_dma_start(
                                    out=d["xe"], out_offset=bass.IndirectOffsetOnAxis(ap=idx[u][:, t, k:k + 1], axis=0),
                                    in_=xf[u][:, t, :], in_offset=None, bounds_check=ROWS_ALL - 1, oob_is_err=False).then_inc(sent.sems[u], 16)
                pool.wait_ge(sent.sems[0], sent.at(BLOCKS - 2, 0))
                pool.wait_ge(sent.sems[1], sent.at(BLOCKS - 1, 1))

            @block.scalar
            def _(act):
                for s in (std_ok, xT_ok, zT_ok):
                    s.open(act)
                act.wait_ge(made, 1)

                def position(n, u):
                    if known(n, -2, BLOCKS - 2):
                        act.wait_ge(mv_ok.sem, mv_ok.at(n + 2))
                        act.wait_ge(rstd_ok.sem, rstd_ok.at(n + 1))
                        act.activation(std[:], mv[:, :, 1], ACT.Sqrt, bias=eps[:, 0:1]).then_inc(std_ok.sem, 1)
                        act.wait_ge(t_ok.sem, t_ok.at(n + 2))
                        act.wait_ge(z_ok.sem, z_ok.at(n + 1))
                        act.activation(xT[:], psT[:, :, 0:N], ACT.Copy).then_inc(xT_ok.sem, 1)
                    if known(n, -1, BLOCKS - 1):
                        act.wait_ge(z_ok.sem, z_ok.at(n + 1))
                        act.wait_ge(zz_ok.sem, zz_ok.at(n))
                        act.activation(zT[:], psZ[:, 0:N], ACT.Copy).then_inc(zT_ok.sem, 1)

                positions(act, position)
                act.wait_ge(zw_ok.sem, zw_ok.at(BLOCKS - 1))
                act.activation(c[:], z[:], ACT.Sigmoid).then_inc(sig_ok, 1)

            @block.vector
            def _(dve):
                for s in (stats_ok, mv_ok, rstd_ok, xf_ok, zw_ok, search, idx_ok):
                    s.open(dve)
                nc.vector.memset(eps[:], EPS).then_inc(made, 1)
                nc.vector.memset(zero[:], 0.0).then_inc(zeroed, 1)
                nc.vector.memset(ones[:], 1.0)
                nc.vector.memset(ones32[:], 1.0)
                nc.vector.memset(onesrow[:], 1.0)
                nc.vector.memset(cur[:], 0)
                nc.vector.memset(bitf[:], 2.0 ** (BITS - 1)).then_inc(made, 1)
                dve.wait_ge(setup, 16 * 7)
                nc.vector.tensor_copy(tri[:], tri32[:]).then_inc(made, 1)

                def position(n, u):
                    if known(n, -2, BLOCKS - 2):
                        dve.wait_ge(h_in.sems[u], h_in.at(n + 2, u))
                        for t in range(BLOCK):
                            last = nc.vector.bn_stats(stats[:, t, :], hin[u][:, t, :])
                        last.then_inc(stats_ok.sem, 1)
                        dve.wait_ge(stats_ok.sem, stats_ok.at(n + 2))
                        dve.wait_ge(std_ok.sem, std_ok.at(n + 1))
                        dve.sem_inc(passed["dve"], 1)
                        for t in range(BLOCK):
                            last = nc.vector.bn_aggr(mv[:, t, :], stats[:, t, :])
                        last.then_inc(mv_ok.sem, 1)
                        dve.wait_ge(std_ok.sem, std_ok.at(n + 2))
                        nc.vector.reciprocal(rstd[:], std[:]).then_inc(rstd_ok.sem, 1)
                        dve.wait_ge(rstd_ok.sem, rstd_ok.at(n + 2))
                        dve.wait_ge(xf_out.sems[u], xf_out.at(n, u))
                        dve.wait_ge(t_ok.sem, t_ok.at(n))
                        for t in range(BLOCK):
                            last = nc.vector.tensor_scalar(xf[u][:, t, :], hin[u][:, t, :], mv[:, t, 0:1], rstd[:, t:t + 1],
                                                           ALU.subtract, ALU.mult)
                        last.then_inc(xf_ok.sem, 1)
                    if known(n, 0, BLOCKS):
                        dve.wait_ge(zz_ok.sem, zz_ok.at(n))
                        nc.vector.tensor_tensor(z[:, bass.ds(n * BLOCK, BLOCK), :], psB[:],
                                                         bz[:].unsqueeze(1).broadcast_to([TILE, BLOCK, EXPERTS]), ALU.add).then_inc(zw_ok.sem, 1)

                positions(dve, position)

                def links():
                    count[0] += 1
                    return count[0]

                count = [0]

                def over_tiles(a):
                    return a.unsqueeze(1).broadcast_to(wide)

                def over_experts(a):
                    return a.unsqueeze(2).broadcast_to(wide)

                tt, ts, stt = nc.vector.tensor_tensor, nc.vector.tensor_scalar, nc.vector.scalar_tensor_tensor

                def top(scores, best, one_hot):
                    nc.vector.tensor_reduce(best[:], scores[:], AX.X, ALU.max).then_inc(chain, 1)
                    dve.wait_ge(chain, links())
                    tt(key[:], scores[:], over_experts(best[:]), ALU.is_lt).then_inc(chain, 1)
                    dve.wait_ge(chain, links())
                    stt(key[:], key[:], float(EXPERTS), over_tiles(iota[:]), ALU.mult, ALU.add).then_inc(chain, 1)
                    dve.wait_ge(chain, links())
                    nc.vector.tensor_reduce(i1[:], key[:], AX.X, ALU.min).then_inc(chain, 1)
                    dve.wait_ge(chain, links())
                    tt(one_hot[:], over_tiles(iota[:]), over_experts(i1[:]), ALU.is_equal).then_inc(chain, 1)
                    dve.wait_ge(chain, links())

                dve.wait_ge(sig_ok, 1)
                tt(c[:], c[:], over_tiles(eb[:]), ALU.add).then_inc(chain, 1)
                dve.wait_ge(chain, links())
                ts(c[:], c[:], 1e-12, None, ALU.max).then_inc(chain, 1)
                dve.wait_ge(chain, links())
                top(c, m1, oh1)
                stt(c2[:], oh1[:], -1e30, c[:], ALU.mult, ALU.add).then_inc(chain, 1)
                dve.wait_ge(chain, links())
                top(c2, m2, oh2)
                tt(r1[:], m1[:], m2[:], ALU.add).then_inc(chain, 1)
                dve.wait_ge(chain, links())
                nc.vector.reciprocal(r1[:], r1[:]).then_inc(chain, 1)
                dve.wait_ge(chain, links())
                tt(w1[:], m1[:], r1[:], ALU.mult).then_inc(chain, 1)
                dve.wait_ge(chain, links())
                tt(w2[:], m2[:], r1[:], ALU.mult).then_inc(chain, 1)
                dve.wait_ge(chain, links())
                tt(w[:], oh1[:], over_experts(w1[:]), ALU.mult).then_inc(chain, 1)
                dve.wait_ge(chain, links())
                tt(t1[:], oh2[:], over_experts(w2[:]), ALU.mult).then_inc(chain, 1)
                dve.wait_ge(chain, links())
                tt(w[:], w[:], t1[:], ALU.add).then_inc(chain, 1)
                dve.wait_ge(chain, links())

                def per_expert(a):
                    return a[:].rearrange("p t e -> p e t")

                def above(threshold, op, out):
                    tt(t1[:], w[:], over_tiles(threshold.bitcast(F32)), op).then_inc(chain, 1)
                    dve.wait_ge(chain, links())
                    nc.vector.tensor_reduce(out, per_expert(t1), AX.X, ALU.add).then_inc(chain, 1)
                    dve.wait_ge(chain, links())

                with dve.Fori(0, BITS) as b:
                    steps = iter(range(1, 9))
                    nc.vector.tensor_copy(bit[:], bitf[:].broadcast_to([TILE, EXPERTS])).then_inc(search.sem, 1)
                    dve.wait_ge(search.sem, search.at(b, next(steps)))
                    tt(cand[:], cur[:], bit[:], ALU.bitwise_or).then_inc(search.sem, 1)
                    dve.wait_ge(search.sem, search.at(b, next(steps)))
                    tt(t1[:], w[:], over_tiles(cand[:].bitcast(F32)), ALU.is_ge).then_inc(search.sem, 1)
                    dve.wait_ge(search.sem, search.at(b, next(steps)))
                    nc.vector.tensor_reduce(part[:], per_expert(t1), AX.X, ALU.add).then_inc(search.sem, 1)
                    dve.wait_ge(search.sem, search.at(b, next(steps)))
                    dve.wait_ge(counted.sem, counted.at(b))
                    ts(take[:], psC[:], float(CAP), bitf[:, 0:1], ALU.is_ge, ALU.mult).then_inc(search.sem, 1)
                    dve.wait_ge(search.sem, search.at(b, next(steps)))
                    tt(cur[:], cur[:], take[:], ALU.bitwise_or).then_inc(search.sem, 1)
                    dve.wait_ge(search.sem, search.at(b, next(steps)))
                    ts(bitf[:], bitf[:], 0.5, None, ALU.mult).then_inc(search.sem, 1)
                    dve.wait_ge(search.sem, search.at(b, next(steps)))
                    nc.vector.tensor_copy(more[:], part[:]).then_inc(search.sem, 1)
                    dve.wait_ge(search.sem, search.at(b, next(steps)))

                tt(c2[:], w[:], over_tiles(cur[:].bitcast(F32)), ALU.is_gt).then_inc(chain, 1)
                dve.wait_ge(chain, links())
                nc.vector.tensor_reduce(part[:], per_expert(c2), AX.X, ALU.add).then_inc(chain, 1)
                dve.wait_ge(chain, links())
                tt(t1[:], oh1[:], oh2[:], ALU.add).then_inc(chain, 1)
                dve.wait_ge(chain, links())
                tt(t2[:], w[:], over_tiles(cur[:].bitcast(F32)), ALU.is_equal).then_inc(chain, 1)
                dve.wait_ge(chain, links())
                tt(t2[:], t2[:], t1[:], ALU.mult).then_inc(chain, 1)
                dve.wait_ge(chain, links())
                nc.vector.tensor_copy(m16[:], t2[:]).then_inc(asked, 1)

                def ranks(out, n):
                    dve.wait_ge(ranked, n)
                    for e in range(EXPERTS):
                        last = nc.vector.tensor_tensor_scan(key[:, :, e], onesrow[:], psUw[:, :, e], 0.0, ALU.mult, ALU.add)
                    last.then_inc(chain, 1)
                    dve.wait_ge(chain, links())
                    tt(out[:], key[:], psUw, ALU.subtract).then_inc(chain, 1)
                    dve.wait_ge(chain, links())
                    tt(out[:], out[:], psR, ALU.add).then_inc(chain, 1)
                    dve.wait_ge(chain, links())

                ranks(t1, 1)
                ts(more[:], psC[:], -1.0, float(CAP), ALU.mult, ALU.add).then_inc(chain, 1)
                dve.wait_ge(chain, links())
                tt(t1[:], t1[:], over_tiles(more[:]), ALU.is_lt).then_inc(chain, 1)
                dve.wait_ge(chain, links())
                tt(t1[:], t1[:], t2[:], ALU.mult).then_inc(chain, 1)
                dve.wait_ge(chain, links())
                tt(c2[:], c2[:], t1[:], ALU.add).then_inc(chain, 1)
                dve.wait_ge(chain, links())
                nc.vector.tensor_copy(m16[:], c2[:]).then_inc(asked, 1)
                ranks(t1, 2)
                tt(t1[:], t1[:], over_tiles(rows0[:]), ALU.add).then_inc(chain, 1)
                dve.wait_ge(chain, links())
                for k, (one_hot, weight) in enumerate(((oh1, w1), (oh2, w2))):
                    tt(t2[:], one_hot[:], t1[:], ALU.mult).then_inc(chain, 1)
                    dve.wait_ge(chain, links())
                    nc.vector.tensor_reduce(m1[:], t2[:], AX.X, ALU.add).then_inc(chain, 1)
                    dve.wait_ge(chain, links())
                    tt(t2[:], one_hot[:], c2[:], ALU.mult).then_inc(chain, 1)
                    dve.wait_ge(chain, links())
                    nc.vector.tensor_reduce(m2[:], t2[:], AX.X, ALU.add).then_inc(chain, 1)
                    dve.wait_ge(chain, links())
                    tt(gw[:, :, k], weight[:], m2[:], ALU.mult).then_inc(chain, 1)
                    dve.wait_ge(chain, links())
                    tt(i1[:], m1[:], m2[:], ALU.mult).then_inc(chain, 1)
                    dve.wait_ge(chain, links())
                    nc.vector.tensor_copy(gidx[:, :, k], i1[:]).then_inc(chain, 1)
                    dve.wait_ge(chain, links())
                    ts(m2[:], m2[:], -float(NOWHERE), float(NOWHERE), ALU.mult, ALU.add).then_inc(chain, 1)
                    dve.wait_ge(chain, links())
                    tt(m1[:], m1[:], m2[:], ALU.add).then_inc(chain, 1)
                    dve.wait_ge(chain, links())
                    nc.vector.tensor_copy(sidx[:, :, k], m1[:]).then_inc(chain, 1)
                    dve.wait_ge(chain, links())
                dve.sem_inc(asked, 1)
                for u in range(2):
                    nc.vector.tensor_copy(idx[u][:], sidx[:, BLOCK * u:BLOCK * (u + 1), :]).then_inc(idx_ok.sem, 1)
                with dve.Fori(1, BLOCKS // 2) as j:
                    for u in range(2):
                        n = j * 2 + u
                        dve.wait_ge(sent.sems[u], sent.at(n - 2, u))
                        nc.vector.tensor_copy(idx[u][:], sidx[:, bass.ds(n * BLOCK, BLOCK), :]).then_inc(idx_ok.sem, 1)

            @block.tensor
            def _(pe):
                for s in (t_ok, z_ok, zz_ok, counted):
                    s.open(pe)
                pe.wait_ge(setup, 16 * 7)
                pe.wait_ge(made, 3)

                def position(n, u):
                    if known(n, -2, BLOCKS - 2):
                        pe.wait_ge(xf_ok.sem, xf_ok.at(n + 2))
                        pe.wait_ge(xT_ok.sem, xT_ok.at(n + 1))
                        for h in range(2):
                            for t in range(BLOCK):
                                last = nc.tensor.transpose(psT[:, h, t * TILE:(t + 1) * TILE], xf[u][:, t, h * 128:(h + 1) * 128],
                                                           ident[0:TILE, 0:TILE])
                        last.then_inc(t_ok.sem, 1)
                    if known(n, -1, BLOCKS - 1):
                        pe.wait_ge(xT_ok.sem, xT_ok.at(n + 1))
                        pe.wait_ge(zT_ok.sem, zT_ok.at(n))
                        for h in range(2):
                            last = nc.tensor.matmul(psZ[:, 0:N], wz[:, h, :], xT[:, h, :], start=(h == 0), stop=(h == 1))
                        last.then_inc(z_ok.sem, 1)
                    if known(n, 0, BLOCKS):
                        pe.wait_ge(zT_ok.sem, zT_ok.at(n))
                        pe.wait_ge(zw_ok.sem, zw_ok.at(n - 1))
                        pe.sem_inc(passed["pe"], 1)
                        for t in range(BLOCK):
                            last = nc.tensor.transpose(psB[:, t, :], zT[:, t * TILE:(t + 1) * TILE], ident[0:EXPERTS, 0:EXPERTS])
                        last.then_inc(zz_ok.sem, 1)

                positions(pe, position)
                with pe.Fori(0, BITS) as b:
                    pe.wait_ge(search.sem, search.at(b, 4))
                    pe.wait_ge(search.sem, search.at(b - 1, 5))
                    nc.tensor.matmul(psC[:], ones32[:], part[:], start=True, stop=True).then_inc(counted.sem, 1)
                for n in range(2):
                    pe.wait_ge(asked, n + 1)
                    if n == 0:
                        nc.tensor.matmul(psC[:], ones32[:], part[:], start=True, stop=True)
                    m = m16[:].rearrange("p t e -> p (t e)")
                    for h in range(2):
                        nc.tensor.matmul(psT[0:TILE, h, :], tri[:], m[:, 512 * h:512 * h + 512], start=True, stop=True)
                        last = nc.tensor.matmul(psU[:, h, :], ones[:], m[:, 512 * h:512 * h + 512], start=True, stop=True)
                    last.then_inc(ranked, 1)


def combine(nc, d):
    with stage(nc) as ctx:
        def sb(x, shape, dt=F32):
            return ctx.enter_context(nc.sbuf_tensor("p6_" + x, shape, dt))

        def signal(x, per=1):
            return Signal(nc, ctx, "p6_" + x, per)

        def transfers(x, per=1):
            return Transfers(nc, ctx, "p6_" + x, per)

        N = BLOCK * TILE
        gidx, gw = sb("gidx", [TILE, TILES, 2], U32), sb("gw", [TILE, TILES, 2])
        idx = [sb(f"idx{u}", [TILE, BLOCK, 2], U32) for u in range(2)]
        wt = [sb(f"wt{u}", [TILE, BLOCK, 2]) for u in range(2)]
        h1 = [sb(f"h1{u}", [TILE, BLOCK, C]) for u in range(2)]
        ys = [sb(f"ys{u}", [TILE, BLOCK, C]) for u in range(2)]
        ye = [sb(f"ye{u}", [TILE, BLOCK, 2, C]) for u in range(2)]
        out = [sb(f"out{u}", [TILE, BLOCK, C]) for u in range(2)]
        setup = semaphore(nc, ctx, "p6_tables_loaded")
        tok_in, out_ok = transfers("tokens_in", 2), transfers("out_stored")
        ye_in = Transfers(nc, ctx, "p6_ye_in", 8, pool=True)
        idx_ok, wt_ok, sum_ok, done = signal("idx"), signal("weights"), signal("sums", 2), signal("out")
        passed = {e: semaphore(nc, ctx, "p6_passed_" + e) for e in ("sp", "pool")}
        with nc.Block() as block:
            @block.sync
            def _(sp):
                for s in (tok_in, out_ok):
                    s.open(sp)
                for dst, name in ((gidx, "gidx"), (gw, "gw")):
                    sp.dma_start(dst[:], d[name]).then_inc(setup, 16)

                def load(n, u):
                    for dst, name in ((h1, "h1"), (ys, "ys")):
                        sp.dma_start(dst[u][:], tiles_of(d[name][bass.ds(n * N, N), :])).then_inc(tok_in.sems[u], 16)

                def store(n, u):
                    sp.dma_start(tiles_of(d["out"][bass.ds(n * N, N), :]), out[u][:]).then_inc(out_ok.sems[u], 16)

                load(0, 0)
                load(1, 1)
                with sp.Fori(0, BLOCKS // 2 - 1) as j:
                    for u in range(2):
                        n = j * 2 + u
                        sp.wait_ge(done.sem, done.at(n))
                        sp.sem_inc(passed["sp"], 1)
                        load(n + 2, u)
                        store(n, u)
                for n in (BLOCKS - 2, BLOCKS - 1):
                    sp.wait_ge(done.sem, done.at(n))
                    store(n, n % 2)
                sp.wait_ge(out_ok.sems[0], out_ok.at(BLOCKS - 2, 0))
                sp.wait_ge(out_ok.sems[1], out_ok.at(BLOCKS - 1, 1))

            @block.gpsimd
            def _(pool):
                with pool.Fori(0, BLOCKS // 2) as j:
                    for u in range(2):
                        n = j * 2 + u
                        pool.wait_ge(idx_ok.sem, idx_ok.at(n))
                        pool.sem_inc(passed["pool"], 1)
                        pool.wait_ge(done.sem, done.at(n - 2))
                        pool.sem_inc(passed["pool"], 1)
                        for t in range(BLOCK):
                            for k in range(2):
                                nc.gpsimd.indirect_dma_start(
                                    out=ye[u][:, t, k, :], out_offset=None, in_=d["ye"],
                                    in_offset=bass.IndirectOffsetOnAxis(ap=idx[u][:, t, k:k + 1], axis=0)).then_inc(ye_in.sems[u], 16)

            @block.vector
            def _(dve):
                for s in (idx_ok, wt_ok, sum_ok, done):
                    s.open(dve)
                dve.wait_ge(setup, 32)

                def indices(n, u):
                    nc.vector.tensor_copy(idx[u][:], gidx[:, bass.ds(n * BLOCK, BLOCK), :]).then_inc(idx_ok.sem, 1)
                    nc.vector.tensor_copy(wt[u][:], gw[:, bass.ds(n * BLOCK, BLOCK), :]).then_inc(wt_ok.sem, 1)

                def step(n, u, more):
                    dve.wait_ge(tok_in.sems[u], tok_in.at(n, u))
                    dve.wait_ge(out_ok.sems[u], out_ok.at(n - 2, u))
                    nc.vector.tensor_tensor(out[u][:], h1[u][:], ys[u][:], ALU.add).then_inc(sum_ok.sem, 1)
                    dve.wait_ge(sum_ok.sem, sum_ok.at(n, 1))
                    dve.wait_ge(ye_in.sems[u], ye_in.at(n, u))
                    dve.wait_ge(wt_ok.sem, wt_ok.at(n))
                    for k in range(2):
                        for t in range(BLOCK):
                            last = nc.vector.scalar_tensor_tensor(out[u][:, t, :], ye[u][:, t, k, :], wt[u][:, t, k:k + 1],
                                                                  out[u][:, t, :], ALU.mult, ALU.add)
                        if k == 0:
                            last.then_inc(sum_ok.sem, 1)
                            dve.wait_ge(sum_ok.sem, sum_ok.at(n, 2))
                    last.then_inc(done.sem, 1)
                    if more:
                        dve.wait_ge(done.sem, done.at(n))
                        indices(n + 2, u)

                indices(0, 0)
                indices(1, 1)
                with dve.Fori(0, BLOCKS // 2 - 1) as j:
                    for u in range(2):
                        step(j * 2 + u, u, True)
                step(BLOCKS - 2, 0, False)
                step(BLOCKS - 1, 1, False)


def constants():
    import numpy as np
    bfloat16 = mybir.dt.np(BF16)
    half = DK // 2
    freq = 1.0 / 10000.0 ** (np.arange(0, DK, 2, dtype=np.float64) / DK)
    comp = np.arange(128) % DK
    f = freq[comp % half][:, None]
    is_cos = comp[:, None] < half
    out = {}
    rot = []
    for shift in (0, S):
        angle = (np.tile(np.arange(S), 2)[None, :] + shift) * f
        rot += [np.sin(angle), np.where(is_cos, 1.0, -1.0) * np.cos(angle)]
    out["rot"] = np.stack(rot, 1).astype(np.float32)
    angle = np.arange(S)[None, :] * np.concatenate([freq, freq])[:, None]
    t = np.where(np.arange(DK)[:, None] < half, np.cos(angle), np.sin(angle))
    th = t.astype(np.float32).astype(bfloat16)
    tl = (t - th.astype(np.float64)).astype(np.float32).astype(bfloat16)
    out["keyrows"] = np.concatenate([th, tl, th, np.ones((2, S), bfloat16)], 0)
    out["keyrows"] = np.broadcast_to(np.tile(out["keyrows"], (1, 2))[:, None, :], (DK * 3 + 2, HEADS, PAIR))
    one, other = np.arange(TILE)[:, None], np.arange(TILE)[None, :]
    key = np.arange(TILE + 1)[None, :]
    never = [np.where(key < TILE, key > one, one == TILE - 1)] * 2
    never += [one == key] * 2
    never += [other < one + 2] * 4
    out["never"] = np.concatenate([np.where(x, NEVER, 0.0) for x in never], 1).astype(np.float32)
    out["maskE"] = (one >= other + 2).astype(np.uint32)
    out["tri"] = (one < other).astype(np.float32)
    out["iota"] = np.broadcast_to(np.arange(EXPERTS, dtype=np.float32), (TILE, EXPERTS))
    out["rows0"] = np.broadcast_to(np.arange(EXPERTS, dtype=np.float32) * CAP, (TILE, EXPERTS))
    out["ident"] = np.eye(128, dtype=np.float32)
    out["blk8"] = (np.arange(128)[:, None] // DK == np.arange(8)[None, :]).astype(np.float32)
    return out


def lay_out(i):
    import numpy as np
    a = {k: np.asarray(v) for k, v in i.items()}
    x = a["x"].reshape(IMAGES, CHANNELS, GRID, PATCH, GRID, PATCH).transpose(1, 3, 5, 0, 2, 4)
    swap = (np.arange(C) // DK) * DK + (np.arange(C) % DK + DK // 2) % DK

    def chunks(w):
        return w.reshape(-1, 128, w.shape[-1]).transpose(1, 0, 2)

    u, v = a["L0_attn_u"].reshape(C), a["L0_attn_v"].reshape(C)
    out = {
        "x": x.reshape(PC, 128, T).transpose(1, 0, 2),
        "tok_w": chunks(a["L0_tok_W"].T),
        "tok_b": np.broadcast_to(a["L0_tok_b"], (TILE, C)),
        "qkv_w": chunks(np.concatenate([a["L0_attn_Wq"], a["L0_attn_Wq"][:, swap], a["L0_attn_Wk"], a["L0_attn_Wv"]], 1)),
        "cols": np.stack([u, v, v[swap]], 1).reshape(2, 128, 3).transpose(1, 0, 2),
    }
    out["wo"] = chunks(a["L0_attn_Wo"])
    out["bo"] = np.broadcast_to(a["L0_attn_bo"], (TILE, C))
    def transposed(w):
        return w.transpose(0, 2, 1).reshape(w.shape[0], -1, 128, w.shape[1]).transpose(0, 2, 1, 3)

    for name, kind in (("ex_", "fc"), ("sh_", "sh")):
        w1, b1, w2, b2 = (a[f"L0_ffn_{kind}{x}"] for x in ("1_w", "1_b", "2_w", "2_b"))
        if kind == "sh":
            w1, b1, w2, b2 = w1[None], b1[None], w2[None], b2[None]
        out[name + "w1"], out[name + "w2"] = transposed(w1), transposed(w2)
        out[name + "b1"] = b1.reshape(len(b1), -1, 128).transpose(0, 2, 1)
        out[name + "b2"] = np.broadcast_to(b2[:, None, :], (len(b2), TILE, C))
    out["proj_w"] = chunks(a["L0_ffn_proj_w"].T)
    out["proj_b"] = np.broadcast_to(a["L0_ffn_proj_b"], (TILE, EXPERTS))
    out["expert_bias"] = np.broadcast_to(a["L0_ffn_expert_bias"], (TILE, EXPERTS))
    out.update(constants())
    return {k: np.ascontiguousarray(v) for k, v in out.items()}


SCRATCH = {"h1": ([T, C], F32), "h0": ([T, C], F32), "v": ([T + PAD, C], F32), "c": ([T, HEADS], F32),
           "stack": ([2, 128, KINDS, T + PAD], BF16)}
SCRATCH.update(xf=([T, C], F32), xe=([ROWS_ALL, C], F32), ye=([ROWS_ALL, C], F32), ys=([T, C], F32),
               gidx=([TILE, TILES, 2], U32), gw=([TILE, TILES, 2], F32))


def tower(nc, d):
    project(nc, d)
    attend(nc, d)
    route(nc, d)
    feed_forward(nc, d, "ex_", d["xe"], d["ye"], 5, EXPERT_HIDDEN, ROWS_ALL // (5 * TILE), 16, EXPERTS)
    feed_forward(nc, d, "sh_", d["xf"], d["ys"], BLOCK, SHARED_HIDDEN, BLOCKS, 4, 1)
    combine(nc, d)


def kernel(**inputs):
    import concourse.bacc as bacc
    from concourse.bass_utils import run_bass_kernel_spmd

    nc = bacc.Bacc("TRN2", target_bir_lowering=False, num_devices=1)
    arrays = lay_out(inputs)
    d = {k: nc.dram_tensor("in_" + k, a.shape, mybir.dt.from_np(a.dtype), kind="ExternalInput").ap()
         for k, a in arrays.items()}
    for k, (shape, dt) in SCRATCH.items():
        d[k] = nc.dram_tensor("scratch_" + k, shape, dt, kind="Internal").ap()
    d["out"] = nc.dram_tensor("out", [T, C], F32, kind="ExternalOutput").ap()
    tower(nc, d)
    r = run_bass_kernel_spmd(nc, [{"in_" + k: a for k, a in arrays.items()}], core_ids=[0])
    return r.results[0]["out"].reshape(IMAGES, S, C)
```

```python
import concourse.bass as bass
from concourse import mybir
from contextlib import ExitStack, contextmanager

F32 = mybir.dt.float32
BF16 = mybir.dt.bfloat16
U32 = mybir.dt.uint32
ALU = mybir.AluOpType
ACT = mybir.ActivationFunctionType
AX = mybir.AxisListType

IMAGES, SIDE, PATCH, CHANNELS = 64, 224, 16, 3
GRID = SIDE // PATCH
S = GRID * GRID
T = IMAGES * S
C = 256
PD = CHANNELS * PATCH * PATCH
PC = PD // 128
HEADS, DK = 16, 16
TILE = S // 2
PAIR = 2 * S
PAIRS = T // PAIR
PAD = 8
EPS = 1e-5
NEVER = -1e28
QH, QL, AH, AL, BH, BL, KH, KL = range(8)
KINDS = 8


@contextmanager
def stage(nc):
    with ExitStack() as ctx:
        ctx.semaphores = []
        yield ctx
        for s in ctx.semaphores:
            nc.gpsimd.sem_clear(s)
        nc.all_engine_barrier()


def semaphore(nc, ctx, name):
    ctx.semaphores.append(ctx.enter_context(nc.semaphore(name)))
    return ctx.semaphores[-1]


class Signal:

    def __init__(self, nc, ctx, name, per=1):
        self.sem = semaphore(nc, ctx, name)
        self.per = per

    def open(self, eng):
        eng.sem_inc(self.sem, 2 * self.per)

    def at(self, n, k=None):
        return (n + 2) * self.per + (self.per if k is None else k)


class Transfers:

    def __init__(self, nc, ctx, name, per=1, pool=False):
        self.lead = 0 if pool else 16 * per
        self.sems = [semaphore(nc, ctx, f"{name}_{u}") for u in range(2)]
        self.per = per

    def open(self, eng):
        for s in self.sems:
            eng.sem_inc(s, 16 * self.per)

    def at(self, n, u):
        return (n - u) * (8 * self.per) + 16 * self.per + self.lead


def known(x, low, high):
    return not isinstance(x, int) or low <= x < high


def three_products(nc, out, operands, start=True, stop=True):
    last = None
    todo = [(a, b) for lh, ll, rh, rl in operands for a, b in ((lh, rh), (lh, rl), (ll, rh))]
    for k, (a, b) in enumerate(todo):
        last = nc.tensor.matmul(out, a, b, start=start and k == 0, stop=stop and k == len(todo) - 1)
    return last


def tiles_of(ap, rows=TILE):
    return ap.rearrange("(t p) c -> p t c", p=rows)


def project(nc, d):
    with stage(nc) as ctx:
        def sb(name, shape, dt=F32):
            return ctx.enter_context(nc.sbuf_tensor("p1_" + name, shape, dt))

        def pb(name, shape, dt=F32):
            return ctx.enter_context(nc.psum_tensor("p1_" + name, shape, dt))

        def signal(name, per=1):
            return Signal(nc, ctx, "p1_" + name, per)

        def transfers(name, per=1):
            return Transfers(nc, ctx, "p1_" + name, per)

        w32 = sb("w32", [128, PC, C])
        wh, wl = sb("wh", [128, PC, C], BF16), sb("wl", [128, PC, C], BF16)
        g32 = sb("g32", [128, 2, 4 * C])
        gh, gl = sb("gh", [128, 2, 4 * C], BF16), sb("gl", [128, 2, 4 * C], BF16)
        cols = sb("cols", [128, 2, 3])
        rot = sb("rot", [128, 4, PAIR])
        tokb = sb("tokb", [TILE, C])
        ident = sb("ident", [128, 128])
        blk8 = sb("blk8", [128, 8])
        x32 = [sb(f"x32{u}", [128, PC, PAIR]) for u in range(2)]
        xh = [sb(f"xh{u}", [128, PC, PAIR], BF16) for u in range(2)]
        xl = [sb(f"xl{u}", [128, PC, PAIR], BF16) for u in range(2)]
        h0 = [sb(f"h0{u}", [TILE, 4, C]) for u in range(2)]
        stats = sb("stats", [TILE, 4, 6])
        mv = sb("mv", [TILE, 4, 2])
        eps = sb("eps", [TILE, 1])
        std, rstd = sb("std", [TILE, 4]), sb("rstd", [TILE, 4])
        xn = sb("xn", [TILE, 4, C])
        nh, nl = sb("nh", [128, 2, PAIR], BF16), sb("nl", [128, 2, PAIR], BF16)
        k32 = sb("k32", [128, 2, PAIR + 1])
        prod = sb("prod", [128, 2, PAIR])
        rt = sb("rt", [128, 2, 4, PAIR])
        st = [sb(f"st{u}", [128, 2, KINDS, PAIR], BF16) for u in range(2)]
        v32 = [sb(f"v32{u}", [TILE, 4, C]) for u in range(2)]
        c32 = [sb(f"c32{u}", [TILE, 4, HEADS]) for u in range(2)]
        pad16 = sb("pad16", [128, KINDS, PAD], BF16)
        padv = sb("padv", [PAD, C])

        psH = pb("psH", [TILE, 4, C])
        psT = pb("psT", [128, 2, 512])
        psC = psT[0:TILE, 0, 448:512].rearrange("p (t h) -> p t h", t=4)
        psJ = [pb(f"psJ{j}", [128, 2, 512]) for j in range(2)]

        loaded = semaphore(nc, ctx, "p1_weights_loaded")
        passed, passed_sp = (semaphore(nc, ctx, "p1_passed_" + e) for e in ("dve", "sp"))
        w_hi, w_lo = (semaphore(nc, ctx, "p1_" + n) for n in ("weights_hi", "weights_lo"))
        pads_set = semaphore(nc, ctx, "p1_pads_set")
        pads_out = semaphore(nc, ctx, "p1_pads_stored")
        x_in = transfers("x_in")
        xh_ok, xl_ok = signal("xh"), signal("xl")
        h_ok, h0_ok = signal("h_in_psum"), signal("h0")
        stats_ok, mv_ok, std_ok = signal("stats"), signal("mv"), signal("std")
        rstd_ok, xn_ok = signal("rstd"), signal("xn")
        t_ok, nh_ok, nl_ok = signal("xnT_in_psum"), signal("nh"), signal("nl")
        jk_ok, jq_ok, jv_ok = signal("k_in_psum"), signal("q_in_psum", 2), signal("v_in_psum")
        kh_ok, kl_ok = signal("kh"), signal("kl")
        k32_ok, qh_ok, q_used = signal("k32"), signal("qh", 2), signal("q_read_by_dve", 2)
        ab_ok, abh_ok, abl_ok = signal("ab", 2), signal("ab_hi", 2), signal("ab_lo", 2)
        prods, prod_ok = signal("prods_written"), signal("prod")
        c_ok, c32_ok = signal("c_in_psum"), signal("c32")
        v_ok = signal("v32")
        h0_out, st_out = transfers("h0_stored"), transfers("stack_stored", 2)
        v_out, c_out = transfers("v_stored"), transfers("c_stored")

        def positions(eng, position):
            for n in (0, 1):
                position(n, n)
            with eng.Fori(1, PAIRS // 2 - 2) as i:
                for u in range(2):
                    position(i * 2 + u, u)
            for n in range(PAIRS - 4, PAIRS + 1):
                position(n, n % 2)

        with nc.Block() as block:
            @block.sync
            def _(sp):
                for s in (x_in, h0_out, st_out, v_out, c_out):
                    s.open(sp)
                for dst, src in ((w32[:], d["tok_w"]), (g32[:], d["qkv_w"]), (cols[:], d["cols"]),
                                 (rot[:], d["rot"]), (tokb[:], d["tok_b"]), (ident[:], d["ident"]),
                                 (blk8[:], d["blk8"])):
                    sp.dma_start(dst, src).then_inc(loaded, 16)

                def load(n, u):
                    sp.dma_start(x32[u][:], d["x"][:, :, bass.ds(n * PAIR, PAIR)]).then_inc(x_in.sems[u], 16)

                def reload(n, u):
                    sp.wait_ge(xh_ok.sem, xh_ok.at(n - 2))
                    sp.wait_ge(xl_ok.sem, xl_ok.at(n - 2))
                    sp.sem_inc(passed_sp, 1)
                    load(n, u)

                def position(n, u):
                    if not known(n, 0, PAIRS):
                        return
                    rows = bass.ds(n * PAIR, PAIR)
                    sp.wait_ge(h0_ok.sem, h0_ok.at(n))
                    sp.dma_start(tiles_of(d["h0"][rows, :]), h0[u][:]).then_inc(h0_out.sems[u], 16)
                    sp.wait_ge(v_ok.sem, v_ok.at(n))
                    sp.dma_start(tiles_of(d["v"][rows, :]), v32[u][:]).then_inc(v_out.sems[u], 16)
                    if known(n, 0, PAIRS - 4):
                        reload(n + 4, u)
                    sp.wait_ge(c32_ok.sem, c32_ok.at(n))
                    sp.dma_start(tiles_of(d["c"][rows, :]), c32[u][:]).then_inc(c_out.sems[u], 16)
                    sp.wait_ge(kl_ok.sem, kl_ok.at(n))
                    sp.wait_ge(q_used.sem, q_used.at(n))
                    sp.wait_ge(abl_ok.sem, abl_ok.at(n))
                    sp.sem_inc(passed_sp, 1)
                    for m in range(2):
                        sp.dma_start(d["stack"][m, :, :, rows], st[u][:, m]).then_inc(st_out.sems[u], 16)

                load(0, 0)
                load(1, 1)
                sp.wait_ge(pads_set, 2)
                for m in range(2):
                    with nc.allow_non_contiguous_dma(reason="the stacks' pad columns, once"):
                        sp.dma_start(d["stack"][m, :, :, T:T + PAD], pad16[:]).then_inc(pads_out, 16)
                sp.dma_start(d["v"][T:T + PAD, :], padv[:]).then_inc(pads_out, 16)
                reload(2, 0)
                reload(3, 1)
                positions(sp, position)
                for s in (h0_out, st_out, v_out, c_out):
                    sp.wait_ge(s.sems[0], s.at(PAIRS - 2, 0))
                    sp.wait_ge(s.sems[1], s.at(PAIRS - 1, 1))
                sp.wait_ge(pads_out, 48)

            @block.scalar
            def _(act):
                for s in (xh_ok, std_ok, nh_ok, k32_ok, kh_ok, qh_ok, abh_ok, v_ok):
                    s.open(act)
                act.wait_ge(loaded, 112)
                act.activation(wh[:], w32[:], ACT.Copy).then_inc(w_hi, 1)
                act.activation(gh[:], g32[:], ACT.Copy).then_inc(w_hi, 1)

                def split(n, u):
                    act.wait_ge(x_in.sems[u], x_in.at(n, u))
                    act.wait_ge(h_ok.sem, h_ok.at(n - 2))
                    act.activation(xh[u][:], x32[u][:], ACT.Copy).then_inc(xh_ok.sem, 1)

                def deviation(n):
                    act.wait_ge(mv_ok.sem, mv_ok.at(n))
                    act.wait_ge(rstd_ok.sem, rstd_ok.at(n - 1))
                    act.activation(std[:], mv[:, :, 1], ACT.Sqrt, bias=eps[:, 0:1]).then_inc(std_ok.sem, 1)

                def position(n, u):
                    if known(n, 0, PAIRS):
                        act.wait_ge(t_ok.sem, t_ok.at(n))
                        act.wait_ge(jq_ok.sem, jq_ok.at(n - 1))
                        act.wait_ge(nl_ok.sem, nl_ok.at(n - 1))
                        act.activation(nh[:], psT[:, :, 0:PAIR], ACT.Copy).then_inc(nh_ok.sem, 1)
                    if known(n, 0, PAIRS - 2):
                        split(n + 2, u)
                    def halves(m):
                        if known(n, 1, PAIRS + 1):
                            act.wait_ge(ab_ok.sem, ab_ok.at(n - 1, m + 1))
                            act.activation(st[1 - u][:, m, AH:BH + 1:2, :], rt[:, m, 0:4:2, :], ACT.Copy).then_inc(abh_ok.sem, 1)

                    halves(0)
                    if known(n, 0, PAIRS):
                        act.wait_ge(jv_ok.sem, jv_ok.at(n))
                        act.wait_ge(v_out.sems[u], v_out.at(n - 2, u))
                        act.activation(v32[u][:].rearrange("p (b t) c -> p b (t c)", b=2), psJ[1][0:TILE, :, :],
                                       ACT.Copy).then_inc(v_ok.sem, 1)
                    halves(1)
                    if known(n, 0, PAIRS):
                        act.wait_ge(jk_ok.sem, jk_ok.at(n))
                        act.wait_ge(st_out.sems[u], st_out.at(n - 2, u))
                        act.activation(st[u][:, :, KH, :], psJ[0][:, :, 0:PAIR], ACT.Copy).then_inc(kh_ok.sem, 1)
                    if known(n, 0, PAIRS - 1):
                        deviation(n + 1)
                    if known(n, 0, PAIRS):
                        act.wait_ge(prod_ok.sem, prod_ok.at(n - 1))
                        act.wait_ge(kl_ok.sem, kl_ok.at(n - 1))
                        act.activation(k32[:, :, 0:PAIR], psJ[0][:, :, 0:PAIR], ACT.Copy).then_inc(k32_ok.sem, 1)
                        for m in range(2):
                            act.wait_ge(jq_ok.sem, jq_ok.at(n, m + 1))
                            act.activation(st[u][:, m, QH, :], psJ[(m + 1) % 2][:, 0, 0:PAIR], ACT.Identity,
                                           bias=cols[:, m, 0:1]).then_inc(qh_ok.sem, 1)

                act.wait_ge(pads_set, 2)
                split(0, 0)
                split(1, 1)
                deviation(0)
                positions(act, position)

            @block.vector
            def _(dve):
                for s in (xl_ok, h0_ok, stats_ok, mv_ok, rstd_ok, xn_ok, nl_ok, q_used, prods, prod_ok, c32_ok):
                    s.open(dve)
                nc.vector.memset(eps[:], EPS)
                nc.vector.memset(k32[:], 0.0)
                nc.vector.memset(pad16[:], 0.0).then_inc(pads_set, 1)
                nc.vector.memset(padv[:], 0.0).then_inc(pads_set, 1)
                dve.wait_ge(w_hi, 1)
                nc.vector.tensor_tensor(wl[:], w32[:], wh[:], ALU.subtract).then_inc(w_lo, 1)
                dve.wait_ge(w_hi, 2)
                nc.vector.tensor_tensor(gl[:], g32[:], gh[:], ALU.subtract).then_inc(w_lo, 1)

                def split(n, u):
                    dve.wait_ge(xh_ok.sem, xh_ok.at(n))
                    nc.vector.tensor_tensor(xl[u][:], x32[u][:], xh[u][:], ALU.subtract).then_inc(xl_ok.sem, 1)

                def normalise(n, u):
                    dve.wait_ge(h_ok.sem, h_ok.at(n))
                    dve.wait_ge(h0_out.sems[u], h0_out.at(n - 2, u))
                    nc.vector.tensor_tensor(h0[u][:], psH[:], tokb[:].unsqueeze(1).broadcast_to([TILE, 4, C]),
                                            ALU.add).then_inc(h0_ok.sem, 1)
                    dve.wait_ge(h0_ok.sem, h0_ok.at(n))
                    for t in range(4):
                        last = nc.vector.bn_stats(stats[:, t, :], h0[u][:, t, :])
                    last.then_inc(stats_ok.sem, 1)
                    dve.wait_ge(stats_ok.sem, stats_ok.at(n))
                    dve.wait_ge(std_ok.sem, std_ok.at(n - 1))
                    dve.sem_inc(passed, 1)
                    for t in range(4):
                        last = nc.vector.bn_aggr(mv[:, t, :], stats[:, t, :])
                    last.then_inc(mv_ok.sem, 1)
                    dve.wait_ge(std_ok.sem, std_ok.at(n))
                    nc.vector.reciprocal(rstd[:], std[:]).then_inc(rstd_ok.sem, 1)
                    dve.wait_ge(rstd_ok.sem, rstd_ok.at(n))
                    dve.wait_ge(t_ok.sem, t_ok.at(n - 1))
                    for t in range(4):
                        last = nc.vector.tensor_scalar(xn[:, t, :], h0[u][:, t, :], mv[:, t, 0:1], rstd[:, t:t + 1],
                                                       ALU.subtract, ALU.mult)
                    last.then_inc(xn_ok.sem, 1)

                def position(n, u):
                    if known(n, 0, PAIRS):
                        dve.wait_ge(nh_ok.sem, nh_ok.at(n))
                        nc.vector.tensor_tensor(nl[:], psT[:, :, 0:PAIR], nh[:], ALU.subtract).then_inc(nl_ok.sem, 1)
                    if known(n, 0, PAIRS - 2):
                        split(n + 2, u)
                    if known(n, 0, PAIRS - 1):
                        normalise(n + 1, 1 - u)
                    if known(n, 1, PAIRS + 1):
                        dve.wait_ge(c_ok.sem, c_ok.at(n - 1))
                        dve.wait_ge(c_out.sems[1 - u], c_out.at(n - 3, 1 - u))
                        nc.vector.tensor_copy(c32[1 - u][:], psC).then_inc(c32_ok.sem, 1)
                    if known(n, 0, PAIRS):
                        rotate(n, u)

                def rotate(n, u):
                    dve.wait_ge(k32_ok.sem, k32_ok.at(n))
                    dve.wait_ge(abl_ok.sem, abl_ok.at(n - 1))
                    dve.wait_ge(st_out.sems[u], st_out.at(n - 2, u))
                    for m in range(2):
                        qa, qb = psJ[(m + 1) % 2][:, 0, 0:PAIR], psJ[(m + 1) % 2][:, 1, 0:PAIR]
                        dve.wait_ge(jq_ok.sem, jq_ok.at(n, m + 1))

                        def term(r, q, col):
                            return nc.vector.scalar_tensor_tensor(rt[:, m, r, :], q, cols[:, m, col:col + 1], rot[:, r, :],
                                                                  ALU.add, ALU.mult)

                        term(1, qb, 2)
                        term(3, qb, 2)
                        dve.wait_ge(qh_ok.sem, qh_ok.at(n, m + 1))
                        term(0, qa, 1)
                        term(2, qa, 1)
                        last = nc.vector.scalar_tensor_tensor(prod[:, m, :], qa, cols[:, m, 0:1], k32[:, m, 1:PAIR + 1],
                                                              ALU.add, ALU.mult)
                        if m:
                            last.then_inc(prods.sem, 1)
                        nc.vector.scalar_tensor_tensor(st[u][:, m, QL, :], qa, cols[:, m, 0:1], st[u][:, m, QH, :],
                                                       ALU.add, ALU.subtract).then_inc(q_used.sem, 1)
                    dve.wait_ge(prods.sem, prods.at(n))
                    nc.vector.memset(prod[:, :, S - 1:PAIR:S], NEVER / DK).then_inc(prod_ok.sem, 1)

                split(0, 0)
                split(1, 1)
                normalise(0, 0)
                positions(dve, position)

            @block.gpsimd
            def _(pool):
                for s in (kl_ok, ab_ok, abl_ok):
                    s.open(pool)

                def step(n, u):
                    pool.wait_ge(kh_ok.sem, kh_ok.at(n))
                    pool.wait_ge(k32_ok.sem, k32_ok.at(n))
                    nc.gpsimd.tensor_tensor(st[u][:, :, KL, :], k32[:, :, 0:PAIR], st[u][:, :, KH, :], ALU.subtract).then_inc(kl_ok.sem, 1)
                    for m in range(2):
                        pool.wait_ge(q_used.sem, q_used.at(n, m + 1))
                        nc.gpsimd.tensor_tensor(rt[:, m, 0:4:2, :], rt[:, m, 0:4:2, :], rt[:, m, 1:4:2, :], ALU.add).then_inc(ab_ok.sem, 1)
                        pool.wait_ge(abh_ok.sem, abh_ok.at(n, m + 1))
                        nc.gpsimd.tensor_tensor(st[u][:, m, AL:BL + 1:2, :], rt[:, m, 0:4:2, :],
                                                          st[u][:, m, AH:BH + 1:2, :], ALU.subtract).then_inc(abl_ok.sem, 1)

                with pool.Fori(0, PAIRS // 2) as i:
                    step(i * 2, 0)
                    step(i * 2 + 1, 1)

            @block.tensor
            def _(pe):
                for s in (h_ok, t_ok, jk_ok, jq_ok, jv_ok, c_ok):
                    s.open(pe)
                pe.wait_ge(w_lo, 2)
                pe.wait_ge(pads_set, 2)

                def embed(n, u):
                    pe.wait_ge(xh_ok.sem, xh_ok.at(n))
                    pe.wait_ge(xl_ok.sem, xl_ok.at(n))
                    pe.wait_ge(h0_ok.sem, h0_ok.at(n - 1))
                    for t in range(4):
                        cut = slice(t * TILE, (t + 1) * TILE)
                        last = three_products(nc, psH[:, t, :], [
                            (xh[u][:, c, cut], xl[u][:, c, cut], wh[:, c, :], wl[:, c, :]) for c in range(PC)])
                    last.then_inc(h_ok.sem, 1)

                def rows(out, col):
                    return three_products(nc, out, [
                        (gh[:, c, col:col + 128], gl[:, c, col:col + 128], nh[:, c, :], nl[:, c, :]) for c in range(2)])

                def position(n, u):
                    if known(n, 0, PAIRS):
                        pe.wait_ge(xn_ok.sem, xn_ok.at(n))
                        pe.wait_ge(nl_ok.sem, nl_ok.at(n - 1))
                        pe.wait_ge(c32_ok.sem, c32_ok.at(n - 2))
                        for c in range(2):
                            for t in range(4):
                                last = nc.tensor.transpose(psT[:, c, t * TILE:(t + 1) * TILE], xn[:, t, c * 128:(c + 1) * 128],
                                                           ident[0:TILE, 0:TILE])
                        last.then_inc(t_ok.sem, 1)
                    if known(n, 0, PAIRS - 1):
                        embed(n + 1, 1 - u)
                    if known(n, 0, PAIRS):
                        pe.wait_ge(nl_ok.sem, nl_ok.at(n))
                    if known(n, 1, PAIRS + 1):
                        pe.wait_ge(prod_ok.sem, prod_ok.at(n - 1))
                        for t in range(4):
                            for m in range(2):
                                last = nc.tensor.matmul(psC[:, t, 8 * m:8 * m + 8], prod[:, m, t * TILE:(t + 1) * TILE],
                                                        blk8[:], start=True, stop=True)
                        last.then_inc(c_ok.sem, 1)
                    if known(n, 0, PAIRS):
                        pe.wait_ge(q_used.sem, q_used.at(n - 1, 1))
                        for t in range(4):
                            cut = slice(t * TILE, (t + 1) * TILE)
                            last = three_products(nc, psJ[1][0:TILE, t // 2, (t % 2) * C:(t % 2 + 1) * C], [
                                (nh[:, c, cut], nl[:, c, cut], gh[:, c, 3 * C:], gl[:, c, 3 * C:]) for c in range(2)])
                        last.then_inc(jv_ok.sem, 1)
                        pe.wait_ge(q_used.sem, q_used.at(n - 1))
                        for m in range(2):
                            last = rows(psJ[0][:, m, 0:PAIR], 2 * C + 128 * m)
                        last.then_inc(jk_ok.sem, 1)
                        pe.wait_ge(v_ok.sem, v_ok.at(n))
                        for m in range(2):
                            if m:
                                pe.wait_ge(k32_ok.sem, k32_ok.at(n))
                            ps = psJ[(m + 1) % 2]
                            rows(ps[:, 0, 0:PAIR], 128 * m)
                            rows(ps[:, 1, 0:PAIR], C + 128 * m).then_inc(jq_ok.sem, 1)

                embed(0, 0)
                positions(pe, position)


LAG = 6
QUADS = HEADS // 4
SLOTS = IMAGES * QUADS
BODY = 16
STACK = 96
ROWS = STACK + 2


NEVER_COLUMNS = 4 * (TILE + 1) + 4 * TILE


def attend(nc, d):
    with stage(nc) as ctx:
        def sb(name, shape, dt=F32):
            return ctx.enter_context(nc.sbuf_tensor("p2_" + name, shape, dt))

        def pb(name, shape, dt=F32):
            return ctx.enter_context(nc.psum_tensor("p2_" + name, shape, dt))

        def signal(name, per=1):
            return Signal(nc, ctx, "p2_" + name, per)

        def transfers(name, per=1):
            return Transfers(nc, ctx, "p2_" + name, per)

        L = [sb(f"L{u}", [ROWS, HEADS, PAIR], BF16) for u in range(2)]
        U = [sb(f"U{u}", [ROWS, HEADS, PAIR], BF16) for u in range(2)]
        K = [sb(f"K{u}", [ROWS, HEADS, PAIR], BF16) for u in range(2)]
        vraw = [sb(f"vraw{u}", [TILE, 4, C]) for u in range(2)]
        vnext = [sb(f"vnext{u}", [TILE, 4, C]) for u in range(2)]
        h0 = [sb(f"h0{u}", [TILE, 4, C]) for u in range(2)]
        cnext = [sb(f"cnext{u}", [TILE, 4, HEADS]) for u in range(2)]
        v32 = [sb(f"v32{u}", [TILE, 4, HEADS, 32]) for u in range(2)]
        ident = sb("ident", [128, 128])
        ident16 = sb("ident16", [TILE, TILE], BF16)
        never32, never = (sb(x, [TILE, NEVER_COLUMNS], dt) for x, dt in (("never32", F32), ("never", BF16)))
        neverS, neverE = (never[:, 2 * (TILE + 1) * x:2 * (TILE + 1) * (x + 1)].rearrange("p (h t) -> p h t", h=2)
                          for x in range(2))
        neverU = never[:, 4 * (TILE + 1):NEVER_COLUMNS]
        maskE = sb("maskE", [TILE, TILE], U32)
        wo, bo = sb("wo", [128, 2, C]), sb("bo", [TILE, C])
        mx = [sb(f"mx{g}", [TILE, 2, HEADS]) for g in range(2)]
        mxU = [sb(f"mxU{g}", [TILE, 2, HEADS]) for g in range(2)]
        ml, mf, mt, ea = (sb(x, [TILE, 2, HEADS]) for x in ("ml", "mf", "mt", "ea"))
        nm = sb("nm", [TILE, 2, 2, HEADS], BF16)
        mrow = [sb(f"mrow{g}", [2 * HEADS, S], BF16) for g in range(2)]
        en = [sb(f"en{g}", [TILE, 2, HEADS]) for g in range(2)]
        ev = [sb(f"ev{g}", [TILE, 2, HEADS, DK]) for g in range(2)]
        probs = [sb(f"probs{j}", [TILE, 2, PAIR]) for j in range(2)]
        ot = [sb(f"ot{g}", [128, QUADS, S]) for g in range(2)]
        den, rden = sb("den", [TILE, HEADS]), sb("rden", [TILE, HEADS])
        num = sb("num", [TILE, HEADS, DK])
        attn = sb("attn", [TILE, HEADS, DK])
        attnT = sb("attnT", [128, 2, TILE])
        h1 = [sb(f"h1{g}", [TILE, 2, C]) for g in range(2)]
        zero = sb("zero", [128, C])

        psS, psD = pb("psS", [TILE, 2, 512]), pb("psD", [TILE, 512])
        psE, psF = pb("psE", [TILE, 2, 512]), pb("psF", [TILE, 512])
        psO = pb("psO", [128, 512])
        psM = pb("psM", [128, 512])
        psM16 = psM[:].bitcast(BF16)

        passed = {e: semaphore(nc, ctx, "p2_passed_" + e) for e in ("dve", "pool", "sp")}
        setup = semaphore(nc, ctx, "p2_constants_loaded")
        zeroed = semaphore(nc, ctx, "p2_zero_ready")
        made_v32 = semaphore(nc, ctx, "p2_v32_constants")
        made = semaphore(nc, ctx, "p2_constants_made")
        s_ok, s_max = signal("s_in_psum", 6), signal("row_max", 6)
        e_ok, e_sel, p_ok = signal("e_in_psum", 4), signal("e_selected", 4), signal("probs", 4)
        pv_ok, ot_ok = signal("pv", 2), signal("ot")
        mch, mtr, mrow_ok, en_ok = signal("max_chain", 6), signal("maxT_in_psum"), signal("mrow"), signal("en")
        ev_ok, v32_ok, hb_ok = signal("ev"), signal("v32", 2), signal("h0_with_bias", 2)
        ott_ok, nrm, num_ok, attn_ok = signal("otT_in_psum", 2), signal("den", 4), signal("num", 2), signal("attn", 2)
        at_ok, att_ok, wo_ok, h1_ok = signal("attnT_in_psum", 2), signal("attnT", 2), signal("wo", 2), signal("h1", 2)
        stacks = [transfers(f"stack_in{m}", 15) for m in range(2)]
        tokens_in, h0_in = transfers("tokens_in", 3), transfers("h0_in")
        m_in, h1_out = transfers("max_in", 4), transfers("h1_out")
        rinsed = transfers("expert_rows_zeroed")

        def where(i, r):
            return i * BODY + r, i * 4 + r // 4, i * 2 + r // 8, r % 4, r // 4 % 2, r // 8 % 2

        def positions(eng, position):
            for r in range(-LAG, 0):
                for c in range(2):
                    position(0, r, c)
            for i in (0, None, IMAGES // 4 - 1):
                if i is None:
                    with eng.Fori(1, IMAGES // 4 - 1) as j:
                        for r in range(BODY):
                            for c in range(2):
                                position(j, r, c)
                    continue
                for r in range(BODY):
                    for c in range(2):
                        position(i, r, c)
            for r in range(4):
                for c in range(2):
                    position(IMAGES // 4, r, c)

        TAIL = {1: ("ott", 0), 2: ("at", 0), 3: ("wo", 0), 4: ("ott", 1), 5: ("mtr", 0), 6: ("at", 1), 7: ("wo", 1)}

        with nc.Block() as block:
            @block.sync
            def _(sp):
                for s in (*stacks, tokens_in, h0_in, m_in, h1_out, rinsed):
                    s.open(sp)
                for u in range(2):
                    sp.dma_start(K[u][48:ROWS], d["keyrows"]).then_inc(setup, 16)
                for dst, name in ((ident, "ident"), (never32, "never"), (maskE, "maskE"), (wo, "wo"), (bo, "bo")):
                    sp.dma_start(dst[:], d[name]).then_inc(setup, 16)

                def load_stacks(n, u, m):
                    sp.sem_inc(passed["sp"], 1)

                    def rows(dst, r, kind, shift=0):
                        src = d["stack"][m, :, kind, bass.ds(n * PAIR + shift, PAIR)]
                        sp.dma_start(dst[u][DK * r:DK * r + DK, 8 * m:8 * m + 8, :],
                                                  src.rearrange("(h d) t -> d h t", d=DK)).then_inc(stacks[m].sems[u], 16)
                    for r, (kl, ku, kk) in enumerate(((QH, QH, KH), (QH, QH, KL), (QL, QL, KH))):
                        rows(L, r, kl)
                        rows(K, r, kk)
                        rows(U, r, ku)
                    for r, (kl, ku) in enumerate(((AH, BH), (AH, BH), (AL, BL))):
                        rows(L, 3 + r, kl)
                        rows(U, 3 + r, ku, 1)

                def load_tokens(n, u):
                    sp.sem_inc(passed["sp"], 1)
                    for dst, name, shift in ((cnext, "c", 0), (vraw, "v", 0), (vnext, "v", 1)):
                        sp.dma_start(dst[u][:], tiles_of(d[name][bass.ds(n * PAIR + shift, PAIR), :])).then_inc(tokens_in.sems[u], 16)

                def load_h0(n, u):
                    sp.sem_inc(passed["sp"], 1)
                    sp.dma_start(h0[u][:], tiles_of(d["h0"][bass.ds(n * PAIR, PAIR), :])).then_inc(h0_in.sems[u], 16)

                for n in range(2):
                    for m in range(2):
                        load_stacks(n, n, m)
                    load_tokens(n, n)
                    load_h0(n, n)

                def store_h1(k, g):
                    sp.wait_ge(h1_ok.sem, h1_ok.at(k))
                    sp.sem_inc(passed["sp"], 1)
                    sp.dma_start(tiles_of(d["h1"][bass.ds(k * S, S), :]), h1[g][:]).then_inc(h1_out.sems[g], 16)

                sp.wait_ge(zeroed, 1)
                each = ROWS_ALL // PAIRS // 128

                def position(i, r, c):
                    s, k, n, q, g, u = where(i, r)
                    if c == 0 and r % 8 == 3 and known(n, 0, PAIRS):
                        sp.dma_start(d["xe"][bass.ds(n * (each * 128), each * 128), :].rearrange("(p r) c -> p r c", r=each),
                                     zero[:].unsqueeze(1).broadcast_to([128, each, C])).then_inc(rinsed.sems[u], 16)
                    if c == 1 and q == 2 and known(k, -1, IMAGES - 1):
                        g1, u1 = (g + 1) % 2, (r + 4) // 8 % 2
                        sp.wait_ge(mrow_ok.sem, mrow_ok.at(k + 1))
                        for dst in (L, U):
                            for part in range(2):
                                sp.dma_start(dst[u1][STACK + part:STACK + part + 1, :, g1 * S:g1 * S + S],
                                                     mrow[g1][HEADS * part:HEADS * (part + 1), :]).then_inc(m_in.sems[g1], 16)
                    if c == 1 and q == 0 and known(k, 2, IMAGES + 1):
                        store_h1(k - 2, g)
                    if c == 0 and r % 8 == 0 and known(n, 1, PAIRS - 1):
                        sp.wait_ge(e_ok.sem, e_ok.at(s - 1))
                        load_stacks(n + 1, 1 - u, 1)
                        sp.wait_ge(ev_ok.sem, ev_ok.at(k - 1))
                        sp.sem_inc(passed["sp"], 1)
                        sp.wait_ge(v32_ok.sem, v32_ok.at(n - 1))
                        load_tokens(n + 1, 1 - u)
                    if c == 0 and r % 8 == 4 and known(n, 1, PAIRS - 1):
                        sp.wait_ge(h1_ok.sem, h1_ok.at(k - 2))
                        load_h0(n + 1, 1 - u)
                    if c == 1 and r % 8 == 6 and known(n, 0, PAIRS - 2):
                        sp.wait_ge(e_ok.sem, e_ok.at(s - 1))
                        load_stacks(n + 2, u, 0)

                positions(sp, position)
                store_h1(IMAGES - 1, 1)
                sp.wait_ge(h1_out.sems[0], h1_out.at(IMAGES - 2, 0))
                sp.wait_ge(h1_out.sems[1], h1_out.at(IMAGES - 1, 1))
                for u in range(2):
                    sp.wait_ge(rinsed.sems[u], rinsed.at(PAIRS - 2 + u, u))

            @block.gpsimd
            def _(pool):
                for s in (ev_ok, v32_ok, hb_ok, attn_ok):
                    s.open(pool)
                nc.gpsimd.memset(zero[:], 0.0).then_inc(zeroed, 1)
                for u in range(2):
                    nc.gpsimd.memset(v32[u][:, :, :, DK:32], 0.0).then_inc(made_v32, 1)
                pool.wait_ge(made_v32, 2)
                for u in range(2):
                    nc.gpsimd.memset(v32[u][:, :, :, DK:DK + 1], 1.0).then_inc(made_v32, 1)

                def values(n, u, half):
                    pool.wait_ge(tokens_in.sems[u], tokens_in.at(n, u))
                    pool.sem_inc(passed["pool"], 1)
                    t = slice(2 * half, 2 * half + 2)
                    nc.gpsimd.tensor_copy(v32[u][:, t, :, 0:DK],
                                          vraw[u][:, t].rearrange("p t (h d) -> p t h d", d=DK)).then_inc(v32_ok.sem, 1)

                def bias(n, u, half):
                    pool.wait_ge(h0_in.sems[u], h0_in.at(n, u))
                    t = slice(2 * half, 2 * half + 2)
                    nc.gpsimd.tensor_tensor(h0[u][:, t], h0[u][:, t], bo[:].unsqueeze(1).broadcast_to([TILE, 2, C]),
                                            ALU.add).then_inc(hb_ok.sem, 1)

                def position(i, r, c):
                    s, k, n, q, g, u = where(i, r)
                    if c == 0 and r % 8 == 3 and known(n, 0, PAIRS - 1):
                        pool.wait_ge(pv_ok.sem, pv_ok.at(s - 4))
                        values(n + 1, 1 - u, 0)
                    if c == 0 and r % 8 == 5 and known(n, 0, PAIRS - 1):
                        values(n + 1, 1 - u, 1)
                    if c == 0 and r % 8 == 7 and known(n, 0, PAIRS - 1):
                        bias(n + 1, 1 - u, 0)
                    if c == 0 and r % 8 == 1 and known(n, 1, PAIRS):
                        bias(n, u, 1)
                    if c == 1 and q == 2 and known(k, -1, IMAGES - 1):
                        g1, u1 = (g + 1) % 2, (r + 4) // 8 % 2
                        pool.wait_ge(en_ok.sem, en_ok.at(k + 1))
                        pool.wait_ge(num_ok.sem, num_ok.at(k - 1))
                        nc.gpsimd.tensor_tensor(
                            ev[g1][:], vnext[u1][:, 2 * g1:2 * g1 + 2, :].rearrange("p t (h d) -> p t h d", d=DK),
                            en[g1][:].unsqueeze(3).broadcast_to([TILE, 2, HEADS, DK]), ALU.mult).then_inc(ev_ok.sem, 1)
                    what, t = TAIL.get(2 * q + c, (None, 0))
                    if what == "ott" and known(k, 1, IMAGES + 1):
                        pool.wait_ge(num_ok.sem, num_ok.at(k - 1, t + 1))
                        pool.wait_ge(at_ok.sem, at_ok.at(k - 1, 1) if t else at_ok.at(k - 2))
                        nc.gpsimd.tensor_tensor(attn[:], num[:], rden[:].unsqueeze(2).broadcast_to([TILE, HEADS, DK]),
                                                           ALU.mult).then_inc(attn_ok.sem, 1)

                pool.wait_ge(setup, 16 * 7)
                for half in range(2):
                    values(0, 0, half)
                    bias(0, 0, half)
                positions(pool, position)

            @block.scalar
            def _(act):
                for s in (p_ok, ot_ok, en_ok, att_ok):
                    s.open(act)

                def position(i, r, c):
                    s, k, n, q, g, u = where(i, r)
                    if known(s, 0, SLOTS):
                        act.wait_ge(pv_ok.sem, pv_ok.at(s - 1, c + 1))
                        for b in range(2):
                            act.wait_ge(e_sel.sem, e_sel.at(s, 2 * c + b + 1))
                            act.activation(probs[c][:, b, :], psE[:, b, 0:PAIR], ACT.Exp, scale=DK ** -0.5).then_inc(p_ok.sem, 1)
                    if c == 0 and known(s, 1, SLOTS + 1):
                        _, k0, _, q0, g0, _ = where(i, r - 1)
                        act.wait_ge(pv_ok.sem, pv_ok.at(s - 1))
                        act.wait_ge(ott_ok.sem, ott_ok.at(k0 - 2))
                        act.activation(ot[g0][:, q0, :], psO[:, 0:S], ACT.Copy).then_inc(ot_ok.sem, 1)
                    if c == 1 and q == 2 and known(k, -1, IMAGES - 1):
                        g1 = (g + 1) % 2
                        act.wait_ge(mch.sem, mch.at(k + 1))
                        act.wait_ge(ev_ok.sem, ev_ok.at(k - 1))
                        act.wait_ge(num_ok.sem, num_ok.at(k - 1))
                        act.activation(en[g1][:], ea[:], ACT.Exp, scale=DK ** -0.5).then_inc(en_ok.sem, 1)
                    what, t = TAIL.get(2 * q + c, (None, 0))
                    if what == "at" and known(k, 1, IMAGES + 1):
                        act.wait_ge(at_ok.sem, at_ok.at(k - 1, t + 1))
                        act.wait_ge(wo_ok.sem, wo_ok.at(k - 1, 1) if t else wo_ok.at(k - 2))
                        act.activation(attnT[:], psM[:, 0:2 * TILE].rearrange("p (h t) -> p h t", h=2), ACT.Copy).then_inc(att_ok.sem, 1)

                positions(act, position)

            @block.vector
            def _(dve):
                for s in (s_max, e_sel, mch, mrow_ok, nrm, num_ok, h1_ok):
                    s.open(dve)
                dve.wait_ge(setup, 16 * 7)
                nc.vector.tensor_copy(ident16[:], ident[0:TILE, 0:TILE]).then_inc(made, 1)
                nc.vector.tensor_copy(never[:], never32[:]).then_inc(made, 1)

                def select(b, cut):
                    out = psE[:, b, 0:PAIR].rearrange("p (h t) -> p h t", h=2)[:, :, cut]
                    data = psF[:, 2 * TILE * b:2 * TILE * (b + 1)].rearrange("p (h t) -> p h t", h=2)
                    return nc.vector.copy_predicated(out, maskE[:].unsqueeze(1).broadcast_to([TILE, 2, TILE]), data)

                def position(i, r, c):
                    s, k, n, q, g, u = where(i, r)
                    cut = slice(c * TILE, (c + 1) * TILE)
                    s1, k1, n1, q1, g1, u1 = where(i, r + LAG)
                    if known(s1, 0, SLOTS):
                        if q1 == 0 and c == 0:
                            dve.wait_ge(mch.sem, mch.at(k1 - 2))
                        for b in range(2):
                            dve.wait_ge(s_ok.sem, s_ok.at(s1, 3 * c + b + 1))
                            nc.vector.tensor_reduce(mx[g1][:, c, 4 * q1 + 2 * b:4 * q1 + 2 * b + 2],
                                                    psS[:, b, 0:PAIR].rearrange("p (h t) -> p h t", h=2),
                                                    AX.X, ALU.max).then_inc(s_max.sem, 1)
                        dve.wait_ge(s_ok.sem, s_ok.at(s1, 3 * c + 3))
                        nc.vector.tensor_reduce(mxU[g1][:, c, 4 * q1:4 * q1 + 4], psD[:, 0:4 * TILE].rearrange("p (h t) -> p h t", h=4),
                                                AX.X, ALU.max).then_inc(s_max.sem, 1)
                    if known(s, 0, SLOTS):
                        for b in range(2):
                            dve.wait_ge(e_ok.sem, e_ok.at(s, 2 * c + b + 1))
                            dve.sem_inc(passed["dve"], 1)
                            select(b, cut).then_inc(e_sel.sem, 1)
                    if q1 == 3 and c == 1 and known(k1, 0, IMAGES):
                        dve.wait_ge(tokens_in.sems[u1], tokens_in.at(n1, u1))
                        dve.wait_ge(s_max.sem, s_max.at(s1))
                        cn = cnext[u1][:, 2 * g1:2 * g1 + 2, :]
                        nc.vector.tensor_tensor(ml[:], mx[g1][:], mxU[g1][:], ALU.max).then_inc(mch.sem, 1)
                        dve.wait_ge(mch.sem, mch.at(k1, 1))
                        nc.vector.tensor_tensor(mf[:], ml[:], cn, ALU.max).then_inc(mch.sem, 1)
                        dve.wait_ge(mch.sem, mch.at(k1, 2))
                        dve.wait_ge(mtr.sem, mtr.at(k1 - 1))
                        nc.vector.tensor_scalar(nm[:, :, 0, :], mf[:], -1.0, None, ALU.mult).then_inc(mch.sem, 1)
                        dve.wait_ge(mch.sem, mch.at(k1, 3))
                        nc.vector.scalar_tensor_tensor(nm[:, :, 1, :], mf[:], -1.0, nm[:, :, 0, :], ALU.mult, ALU.subtract).then_inc(mch.sem, 1)
                        dve.wait_ge(mch.sem, mch.at(k1, 4))
                        nc.vector.tensor_tensor(mt[:], nm[:, :, 0, :], nm[:, :, 1, :], ALU.add).then_inc(mch.sem, 1)
                        dve.wait_ge(mch.sem, mch.at(k1, 5))
                        dve.wait_ge(en_ok.sem, en_ok.at(k1 - 1))
                        nc.vector.tensor_tensor(ea[:], cn, mt[:], ALU.add).then_inc(mch.sem, 1)
                    what, t = TAIL.get(2 * q + c, (None, 0))
                    if what == "mtr" and known(k, -1, IMAGES - 1):
                        dve.wait_ge(mtr.sem, mtr.at(k + 1))
                        dve.wait_ge(m_in.sems[(g + 1) % 2], m_in.at(k - 1, (g + 1) % 2))
                        nc.vector.tensor_copy(mrow[(g + 1) % 2][:], psM16[0:2 * HEADS, 0:S]).then_inc(mrow_ok.sem, 1)
                    if what == "ott" and known(k, 1, IMAGES + 1):
                        o = psM[0:TILE, :].rearrange("p (h e) -> p h e", e=32)
                        e = en[1 - g][:, t, :]
                        dve.wait_ge(ott_ok.sem, ott_ok.at(k - 1, t + 1))
                        dve.wait_ge(en_ok.sem, en_ok.at(k - 1))
                        dve.wait_ge(attn_ok.sem, attn_ok.at(k - 1, 1) if t else attn_ok.at(k - 2))
                        nc.vector.tensor_tensor(den[:], o[:, :, DK], e, ALU.add).then_inc(nrm.sem, 1)
                        dve.wait_ge(nrm.sem, nrm.at(k - 1, 2 * t + 1))
                        nc.vector.reciprocal(rden[:], den[:]).then_inc(nrm.sem, 1)
                        dve.wait_ge(ev_ok.sem, ev_ok.at(k - 1))
                        nc.vector.tensor_tensor(num[:], o[:, :, 0:DK], ev[1 - g][:, t], ALU.add).then_inc(num_ok.sem, 1)
                    if what == "wo" and known(k, 1, IMAGES + 1):
                        _, _, n0, _, g0, u0 = where(i, r - 4)
                        dve.wait_ge(wo_ok.sem, wo_ok.at(k - 1, t + 1))
                        dve.wait_ge(hb_ok.sem, hb_ok.at(n0))
                        dve.wait_ge(h1_out.sems[g0], h1_out.at(k - 3, g0))
                        nc.vector.tensor_tensor(h1[g0][:, t, :], psM[0:TILE, 0:C], h0[u0][:, 2 * g0 + t, :], ALU.add).then_inc(h1_ok.sem, 1)

                positions(dve, position)

            @block.tensor
            def _(pe):
                for s in (s_ok, e_ok, pv_ok, mtr, ott_ok, at_ok, wo_ok):
                    s.open(pe)
                pe.wait_ge(made, 2)
                pe.wait_ge(made_v32, 4)
                pe.wait_ge(setup, 16 * 7)

                def stage_s(s, q, g, u, c, n):
                    if q % 2 == 0 and g == 0 and c == 0:
                        pe.wait_ge(stacks[q // 2].sems[u], stacks[q // 2].at(n, u))
                    mid, first, second = slice(g * S + c * TILE, g * S + (c + 1) * TILE), g * S, g * S + TILE
                    for b in range(2):
                        pe.wait_ge(s_max.sem, s_max.at(s, b + 1) if c else s_max.at(s - 1, 3 + b + 1))
                        for j in range(2):
                            h = 4 * q + 2 * b + j
                            low, up, key = L[u][0:STACK, h], U[u][0:STACK, h], K[u][0:STACK, h]
                            out = psS[:, b, j * S:(j + 1) * S]
                            if c == 0:
                                nc.tensor.matmul(out[:, 0:TILE], low[:, mid], key[:, first:second], start=(j == 0), stop=False)
                                nc.tensor.matmul(out[:, TILE:S], up[:, mid], key[:, second:second + TILE], start=False, stop=False)
                            else:
                                nc.tensor.matmul(out, low[:, mid], key[:, first:first + S], start=(j == 0), stop=False)
                        pair = psS[:, b, 0:PAIR].rearrange("p (h t) -> p h t", h=2)
                        if c == 0:
                            last = nc.tensor.matmul(pair[:, :, 0:TILE + 1], ident16[:], neverS, start=False, stop=True)
                        else:
                            last = nc.tensor.matmul(pair[:, :, TILE:S], ident16[:], neverS[:, :, 0:TILE], start=False, stop=True)
                        last.then_inc(s_ok.sem, 1)
                    pe.wait_ge(s_max.sem, s_max.at(s, 3) if c else s_max.at(s - 1))
                    for j in range(4):
                        h = 4 * q + j
                        nc.tensor.matmul(psD[:, j * TILE:(j + 1) * TILE], U[u][0:STACK, h][:, mid], K[u][0:STACK, h][:, mid],
                                         start=(j == 0), stop=False)
                    nc.tensor.matmul(psD[:, 0:4 * TILE], ident16[:], neverU, start=False, stop=True).then_inc(s_ok.sem, 1)

                def stage_e(s, k, q, g, u, c):
                    if q == 0 and c == 0:
                        pe.wait_ge(m_in.sems[g], m_in.at(k, g))
                    mid, first, second = slice(g * S + c * TILE, g * S + (c + 1) * TILE), g * S, g * S + TILE
                    pe.wait_ge(e_sel.sem, e_sel.at(s, 2) if c else e_sel.at(s - 1))
                    for j in range(4):
                        h = 4 * q + j
                        nc.tensor.matmul(psF[:, j * TILE:(j + 1) * TILE], K[u][:, h][:, mid], U[u][:, h][:, mid], start=True, stop=True)
                    for b in range(2):
                        pe.wait_ge(p_ok.sem, p_ok.at(s, b + 1) if c else p_ok.at(s - 1, 2 + b + 1))
                        for j in range(2):
                            h = 4 * q + 2 * b + j
                            low, up, key = L[u][:, h], U[u][:, h], K[u][:, h]
                            out = psE[:, b, j * S:(j + 1) * S]
                            if c == 0:
                                nc.tensor.matmul(out, key[:, mid], low[:, first:first + S], start=(j == 0), stop=False)
                            else:
                                nc.tensor.matmul(out[:, 0:TILE], key[:, mid], up[:, first:second], start=(j == 0), stop=False)
                                nc.tensor.matmul(out[:, TILE:S], key[:, mid], low[:, second:second + TILE], start=False, stop=False)
                        pair = psE[:, b, 0:PAIR].rearrange("p (h t) -> p h t", h=2)
                        if c == 0:
                            last = nc.tensor.matmul(pair[:, :, 0:TILE], ident16[:], neverE[:, :, 1:TILE + 1], start=False, stop=True)
                        else:
                            last = nc.tensor.matmul(pair[:, :, TILE - 1:S], ident16[:], neverE, start=False, stop=True)
                        last.then_inc(e_ok.sem, 1)

                def stage_v(s, n, q, g, u, c):
                    pe.wait_ge(p_ok.sem, p_ok.at(s, 2 * c + 2))
                    if c == 0:
                        pe.wait_ge(v32_ok.sem, v32_ok.at(n))
                        pe.wait_ge(ot_ok.sem, ot_ok.at(s - 1))
                    for j in range(4):
                        last = nc.tensor.matmul(psO[32 * j:32 * j + 32, 0:S], v32[u][:, 2 * g + c, 4 * q + j, :],
                                                probs[c][:, j // 2, (j % 2) * S:(j % 2 + 1) * S],
                                                start=(c == 0), stop=(c == 1))
                    last.then_inc(pv_ok.sem, 1)

                def position(i, r, c):
                    s, k, n, q, g, u = where(i, r)
                    s1, k1, n1, q1, g1, u1 = where(i, r + LAG)
                    if known(s1, 0, SLOTS):
                        stage_s(s1, q1, g1, u1, c, n1)
                    if known(s, 0, SLOTS):
                        stage_e(s, k, q, g, u, c)
                    sv, _, nv, qv, gv, uv = where(i, r if c else r - 1)
                    if known(sv, 0, SLOTS):
                        stage_v(sv, nv, qv, gv, uv, 1 - c)
                    what, t = TAIL.get(2 * q + c, (None, 0))
                    g0 = (g + 1) % 2
                    if what == "mtr" and known(k, -1, IMAGES - 1):
                        pe.wait_ge(num_ok.sem, num_ok.at(k - 1))
                        pe.wait_ge(mch.sem, mch.at(k + 1))
                        for h in range(2):
                            last = nc.tensor.transpose(psM16[0:2 * HEADS, h * TILE:(h + 1) * TILE],
                                                       nm[:, h].rearrange("p l h -> p (l h)"), ident16[:])
                        last.then_inc(mtr.sem, 1)
                    if known(k, 1, IMAGES + 1):
                        if what == "ott":
                            pe.wait_ge(h1_ok.sem, h1_ok.at(k - 1, 1) if t else h1_ok.at(k - 2))
                            pe.wait_ge(ot_ok.sem, ot_ok.at(s - 3 if t else s - 1))
                            for j in range(QUADS):
                                last = nc.tensor.transpose(psM[0:TILE, 128 * j:128 * j + 128],
                                                           ot[g0][:, j, t * TILE:(t + 1) * TILE], ident[:])
                            last.then_inc(ott_ok.sem, 1)
                        if what == "at":
                            pe.wait_ge(attn_ok.sem, attn_ok.at(k - 1, t + 1))
                            if t and known(k, -1, IMAGES - 1):
                                pe.wait_ge(mrow_ok.sem, mrow_ok.at(k + 1))
                            a = attn[:].rearrange("p h d -> p (h d)")
                            for j in range(2):
                                last = nc.tensor.transpose(psM[:, j * TILE:(j + 1) * TILE], a[:, 128 * j:128 * j + 128],
                                                           ident[0:TILE, 0:TILE])
                            last.then_inc(at_ok.sem, 1)
                        if what == "wo":
                            pe.wait_ge(att_ok.sem, att_ok.at(k - 1, t + 1))
                            for j in range(2):
                                last = nc.tensor.matmul(psM[0:TILE, 0:C], attnT[:, j, :], wo[:, j, :],
                                                        start=(j == 0), stop=(j == 1))
                            last.then_inc(wo_ok.sem, 1)

                positions(pe, position)


EXPERTS, CHOICES = 8, 2
EXPERT_HIDDEN, SHARED_HIDDEN = 512, 1024
CAP = -(-(-(-T * CHOICES // EXPERTS)) * 5 // 4)
GROUP = 112
TILES = T // GROUP
BLOCK = 4
BLOCKS = TILES // BLOCK
ROOM = -(-CAP // 512) * 512


class Weights:

    def __init__(self, nc, ctx, source, tile, hidden):
        def sb(x, shape, dt=F32):
            return ctx.enter_context(nc.sbuf_tensor(source + x, shape, dt))

        self.source, self.hidden = source, hidden
        self.w1h, self.w1l = (sb(x, [128, 2, hidden], BF16) for x in ("first_w1h", "first_w1l"))
        self.w2h, self.w2l = (sb(x, [128, hidden // 128, C], BF16) for x in ("first_w2h", "first_w2l"))
        self.b1, self.b2 = sb("first_b1", [128, hidden // 128]), sb("first_b2", [tile, C])


def feed_forward(nc, d, name, ready, x, y_dram, tile, tiles, first, steps, body, experts, beside=None):
    send, collect = beside == "send", beside == "collect"
    weights, hidden = ready.source, ready.hidden
    chunks = hidden // 128
    N = tiles * tile
    banks = -(-tiles // 2)
    sets = min(experts, 2)
    per_expert = steps // experts
    ahead = 4
    with stage(nc) as ctx:
        def sb(x, shape, dt=F32):
            return ctx.enter_context(nc.sbuf_tensor(name + x, shape, dt))

        def pb(x, shape, dt=F32):
            return ctx.enter_context(nc.psum_tensor(name + x, shape, dt))

        def signal(x, per=1):
            return Signal(nc, ctx, name + x, per)

        def transfers(x, per=1):
            return Transfers(nc, ctx, name + x, per)

        xin = [sb(f"xin{u}", [tile, tiles, C]) for u in range(2)]
        xh = [sb(f"xh{u}", [128, 2, N], BF16) for u in range(2)]
        xl = [sb(f"xl{u}", [128, 2, N], BF16) for u in range(2)]
        if experts > 1:
            raw1, raw2 = sb("raw1", [128, 2, hidden]), sb("raw2", [128, chunks, C])
            rawb1, rawb2 = sb("rawb1", [128, chunks]), sb("rawb2", [tile, C])
        w1h = [ready.w1h] + [sb(f"w1h{w}", [128, 2, hidden], BF16) for w in range(1, sets)]
        w1l = [ready.w1l] + [sb(f"w1l{w}", [128, 2, hidden], BF16) for w in range(1, sets)]
        w2h = [ready.w2h] + [sb(f"w2h{w}", [128, chunks, C], BF16) for w in range(1, sets)]
        w2l = [ready.w2l] + [sb(f"w2l{w}", [128, chunks, C], BF16) for w in range(1, sets)]
        b1 = [ready.b1] + [sb(f"b1{w}", [128, chunks]) for w in range(1, sets)]
        b2 = [ready.b2] + [sb(f"b2{w}", [tile, C]) for w in range(1, sets)]
        g32 = sb("g32", [128, chunks, N])
        gh = [sb(f"gh{u}", [128, chunks, N], BF16) for u in range(2)]
        gl = [sb(f"gl{u}", [128, chunks, N], BF16) for u in range(2)]
        y = [sb(f"y{u}", [tile, tiles, C]) for u in range(2)]
        ident = sb("ident", [128, 128])
        if send or collect:
            table = sb("table", [tile, TILES, 2], U32)
        if send:
            xs = [sb(f"xs{v}", [tile, BLOCK, C]) for v in range(2)]
            idx = [sb(f"idx{v}", [tile, BLOCK, 2], U32) for v in range(2)]
        if collect:
            gw = sb("gw", [tile, TILES, 2])
            ya = [sb(f"ya{u}", [tile, BLOCK, C]) for u in range(2)]
            total = (ya, y)
            h1 = [[sb(f"h1{v}{u}", [tile, BLOCK, C]) for u in range(2)] for v in range(2)]
            ye = [[sb(f"ye{v}{u}", [tile, BLOCK, 2, C]) for u in range(2)] for v in range(2)]
            idx = [[sb(f"idx{v}{u}", [tile, BLOCK, 2], U32) for u in range(2)] for v in range(2)]
            wt = [[sb(f"wt{v}{u}", [tile, BLOCK, 2]) for u in range(2)] for v in range(2)]

        psT = pb("psT", [128, 2, 512])
        psG = [pb(f"psG{j}", [128, 512]) for j in range(ahead)]
        psY = [pb(f"psY{j}", [tile, 2, C]) for j in range(2)]

        setup = semaphore(nc, ctx, name + "constants_loaded")
        x_in, y_out, w_in = transfers("x_in"), transfers("y_out"), transfers("weights_in", 4)
        t_ok, xh_ok, xl_ok = signal("xT_in_psum"), signal("xh"), signal("xl")
        g_ok, gelu_ok, split_ok = signal("h_in_psum", chunks), signal("gelu", chunks), signal("g_split", chunks)
        gh_ok = signal("gh", chunks)
        y_ok, yev_ok = signal("y_in_psum", banks), signal("y", banks)
        wh_ok, wl_ok = signal("weights_hi", 2), signal("weights_lo", 4)
        tables_in = semaphore(nc, ctx, name + "tables_loaded")
        if send:
            xs_in, sent = transfers("rows_in"), Transfers(nc, ctx, name + "rows_sent", 8, pool=True)
            idx_ok = signal("idx", 2)
        if collect:
            ya_in, ya_out = transfers("ya_and_h1_in", 2), transfers("ya_out")
            h1_in = transfers("h1_in")
            ye_in = [Transfers(nc, ctx, name + f"ye{v}_in", 8, pool=True) for v in range(2)]
            idx_ok, wt_ok = [signal(f"idx{v}") for v in range(2)], [signal(f"weights{v}") for v in range(2)]
            sums, done = [signal(f"sums{v}", 2) for v in range(2)], [signal(f"total{v}") for v in range(2)]
        passed = {e: semaphore(nc, ctx, name + "passed_" + e) for e in ("sp", "dve", "pool")}

        def positions(eng, position):
            for r in range(-2, 0):
                position(0, r)
            for r in range(body):
                position(0, r)
            last = -(-4 // body)
            with eng.Fori(1, steps // body - last) as j:
                for r in range(body):
                    position(j, r)
            for i in range(steps // body - last, steps // body):
                for r in range(body):
                    position(i, r)

        def weights_at(i, r):
            if experts == 1:
                return 0, 0
            return i * (body // per_expert) + r // per_expert, r // per_expert % 2

        def reused(signal, n, m):
            return signal.at(n, m - ahead + 1) if m >= ahead else signal.at(n - 1, chunks - ahead + m + 1)

        def new_weights(i, r):
            if experts == 1 or r % per_expert != 1:
                return None
            e, w = weights_at(i, r)
            return (e + 1, 1 - w) if known(e, 0, experts - 1) else None

        with nc.Block() as block:
            @block.sync
            def _(sp):
                for s in (x_in, y_out, w_in):
                    s.open(sp)
                if send:
                    xs_in.open(sp)
                    sp.dma_start(table[:], d["sidx"]).then_inc(tables_in, 16)
                if collect:
                    for s in (ya_in, ya_out, h1_in):
                        s.open(sp)
                    sp.dma_start(table[:], d["gidx"]).then_inc(tables_in, 16)
                    sp.dma_start(gw[:], d["gw"]).then_inc(tables_in, 16)
                sp.dma_start(ident[:], d["ident"]).then_inc(setup, 16)

                def load_weights(e, w):
                    for dst, src in ((raw1, "w1"), (raw2, "w2"), (rawb1, "b1"), (rawb2, "b2")):
                        sp.dma_start(dst[:], d[weights + src][bass.ds(e, 1)].squeeze(0)).then_inc(w_in.sems[w], 16)

                def load_x(n, u):
                    sp.dma_start(xin[u][:], tiles_of(x[bass.ds((n + first) * N, N), :], tile)).then_inc(x_in.sems[u], 16)

                def load_rows(b, v):
                    sp.dma_start(xs[v][:], tiles_of(d["xf"][bass.ds(b * N, N), :], tile)).then_inc(xs_in.sems[v], 16)

                def load_ya(n, u):
                    sp.dma_start(ya[u][:], tiles_of(d["ys"][bass.ds(n * N, N), :], tile)).then_inc(ya_in.sems[u], 16)
                    sp.dma_start(h1[0][u][:], tiles_of(d["h1"][bass.ds(n * N, N), :], tile)).then_inc(ya_in.sems[u], 16)

                def load_h1(n, u):
                    sp.dma_start(h1[1][u][:], tiles_of(d["h1"][bass.ds((n + first) * N, N), :], tile)).then_inc(h1_in.sems[u], 16)

                def store_y(n, u):
                    sp.dma_start(tiles_of(y_dram[bass.ds((n + first) * N, N), :], tile), y[u][:]).then_inc(y_out.sems[u], 16)

                sp.sem_inc(w_in.sems[0], 16 * w_in.per)
                load_x(0, 0)
                load_x(1, 1)
                if send:
                    for v in range(2):
                        load_rows(v, v)
                if collect:
                    load_ya(0, 0)
                    load_h1(0, 0)
                if experts > 1:
                    sp.wait_ge(wl_ok.sem, wl_ok.at(0))
                    sp.wait_ge(wh_ok.sem, wh_ok.at(0))
                    load_weights(1, 1)

                def position(i, r):
                    n, u = i * body + r, r % 2
                    if known(n, -2, steps - 4):
                        sp.wait_ge(t_ok.sem, t_ok.at(n + 2))
                        sp.sem_inc(passed["sp"], 1)
                        load_x(n + 4, u)
                    new = new_weights(i, r)
                    if new is not None and known(new[0], 0, experts - 1):
                        sp.wait_ge(wl_ok.sem, wl_ok.at(new[0]))
                        sp.sem_inc(passed["sp"], 1)
                        sp.wait_ge(wh_ok.sem, wh_ok.at(new[0]))
                        sp.sem_inc(passed["sp"], 1)
                        load_weights(new[0] + 1, 1 - new[1])
                    if collect and known(n, 0, steps - 1):
                        sp.wait_ge(ya_out.sems[1 - u], ya_out.at(n - 1, 1 - u))
                        sp.sem_inc(passed["sp"], 1)
                        load_ya(n + 1, 1 - u)
                    if collect and known(n, 0, steps):
                        sp.wait_ge(done[0].sem, done[0].at(n))
                        sp.sem_inc(passed["sp"], 1)
                        sp.dma_start(tiles_of(y_dram[bass.ds(n * N, N), :], tile), ya[u][:]).then_inc(ya_out.sems[u], 16)
                    if collect and known(n, 1, steps):
                        sp.wait_ge(done[1].sem, done[1].at(n - 1))
                        sp.sem_inc(passed["sp"], 1)
                        store_y(n - 1, 1 - u)
                    if collect and known(n, 0, steps - 1):
                        load_h1(n + 1, 1 - u)
                    if not collect and known(n, 0, steps):
                        sp.wait_ge(yev_ok.sem, yev_ok.at(n))
                        sp.sem_inc(passed["sp"], 1)
                        store_y(n, u)
                    if send and known(n, 0, steps - 1):
                        for v in range(2):
                            b = n * 2 + v
                            sp.wait_ge(sent.sems[v], sent.at(b, v))
                            sp.sem_inc(passed["sp"], 1)
                            load_rows(b + 2, v)

                positions(sp, position)
                if collect:
                    sp.wait_ge(done[1].sem, done[1].at(steps - 1))
                    store_y(steps - 1, 1)
                    sp.wait_ge(ya_out.sems[0], ya_out.at(steps - 2, 0))
                    sp.wait_ge(ya_out.sems[1], ya_out.at(steps - 1, 1))
                sp.wait_ge(y_out.sems[0], y_out.at(steps - 2, 0))
                sp.wait_ge(y_out.sems[1], y_out.at(steps - 1, 1))

            @block.gpsimd
            def _(pool):
                if send:
                    idx_ok.open(pool)
                if collect:
                    for v in range(2):
                        idx_ok[v].open(pool)
                        wt_ok[v].open(pool)
                if send or collect:
                    pool.wait_ge(tables_in, 16 if send else 32)

                def send_rows(n, v):
                    b = n * 2 + v
                    if known(n, 1, steps):
                        pool.wait_ge(sent.sems[v], sent.at(b - 2, v))
                        pool.sem_inc(passed["pool"], 1)
                    nc.gpsimd.tensor_copy(idx[v][:], table[:, bass.ds(b * BLOCK, BLOCK), :]).then_inc(idx_ok.sem, 1)
                    pool.wait_ge(idx_ok.sem, idx_ok.at(n, v + 1))
                    pool.sem_inc(passed["pool"], 1)
                    pool.wait_ge(xs_in.sems[v], xs_in.at(b, v))
                    pool.sem_inc(passed["pool"], 1)
                    for t in range(BLOCK):
                        for k in range(2):
                            nc.gpsimd.indirect_dma_start(
                                out=d["xe"], out_offset=bass.IndirectOffsetOnAxis(ap=idx[v][:, t, k:k + 1], axis=0),
                                in_=xs[v][:, t, :], in_offset=None, bounds_check=ROWS_ALL - 1,
                                oob_is_err=False).then_inc(sent.sems[v], 16)

                def gather(n, v, u):
                    at = bass.ds((n + v * first) * BLOCK, BLOCK)
                    pool.wait_ge(done[v].sem, done[v].at(n - 2))
                    pool.sem_inc(passed["pool"], 1)
                    nc.gpsimd.tensor_copy(wt[v][u][:], gw[:, at, :]).then_inc(wt_ok[v].sem, 1)
                    nc.gpsimd.tensor_copy(idx[v][u][:], table[:, at, :]).then_inc(idx_ok[v].sem, 1)
                    pool.wait_ge(idx_ok[v].sem, idx_ok[v].at(n))
                    pool.sem_inc(passed["pool"], 1)
                    for t in range(BLOCK):
                        for k in range(2):
                            nc.gpsimd.indirect_dma_start(
                                out=ye[v][u][:, t, k, :], out_offset=None, in_=d["ye"],
                                in_offset=bass.IndirectOffsetOnAxis(ap=idx[v][u][:, t, k:k + 1], axis=0)).then_inc(ye_in[v].sems[u], 16)

                def position(i, r):
                    n, u = i * body + r, r % 2
                    if known(n, 0, steps):
                        for v in range(2):
                            if send:
                                send_rows(n, v)
                            if collect:
                                gather(n, v, u)

                if send or collect:
                    positions(pool, position)
                if send:
                    for v in range(2):
                        pool.wait_ge(sent.sems[v], sent.at(2 * steps - 2 + v, v))

            @block.scalar
            def _(act):
                for s in (xh_ok, gelu_ok, wh_ok):
                    s.open(act)

                def split_weights(e, w):
                    act.wait_ge(w_in.sems[w], w_in.at(e, w))
                    act.wait_ge(y_ok.sem, y_ok.at((e - 1) * per_expert - 1))
                    act.activation(w1h[w][:], raw1[:], ACT.Copy).then_inc(wh_ok.sem, 1)
                    act.activation(w2h[w][:], raw2[:], ACT.Copy).then_inc(wh_ok.sem, 1)

                def position(i, r):
                    n, u = i * body + r, r % 2
                    if known(n, -1, steps - 1):
                        _, w = weights_at(i, r + 1)
                        for m in range(chunks):
                            act.wait_ge(g_ok.sem, g_ok.at(n + 1, m + 1))
                            if m == 0:
                                act.wait_ge(wl_ok.sem, wl_ok.at(weights_at(i, r + 1)[0]))
                            act.wait_ge(split_ok.sem, split_ok.at(n, m + 1))
                            act.activation(g32[:, m, :], psG[m % ahead][:, 0:N], ACT.Gelu, bias=b1[w][:, m:m + 1]).then_inc(gelu_ok.sem, 1)
                    if known(n, -2, steps - 2):
                        act.wait_ge(t_ok.sem, t_ok.at(n + 2))
                        act.wait_ge(g_ok.sem, g_ok.at(n))
                        act.activation(xh[u][:], psT[:, :, 0:N], ACT.Copy).then_inc(xh_ok.sem, 1)
                    new = new_weights(i, r)
                    if new is not None:
                        split_weights(*new)

                act.sem_inc(wh_ok.sem, wh_ok.per)
                positions(act, position)

            @block.vector
            def _(dve):
                for s in (xl_ok, gh_ok, split_ok, yev_ok, wl_ok) + ((*sums, *done) if collect else ()):
                    s.open(dve)

                def split_weights(e, w):
                    dve.wait_ge(wh_ok.sem, wh_ok.at(e))
                    nc.vector.tensor_tensor(w1l[w][:], raw1[:], w1h[w][:], ALU.subtract).then_inc(wl_ok.sem, 1)
                    nc.vector.tensor_tensor(w2l[w][:], raw2[:], w2h[w][:], ALU.subtract).then_inc(wl_ok.sem, 1)
                    nc.vector.tensor_copy(b1[w][:], rawb1[:]).then_inc(wl_ok.sem, 1)
                    nc.vector.tensor_copy(b2[w][:], rawb2[:]).then_inc(wl_ok.sem, 1)

                def add(v, n, u, part):
                    if part == 0:
                        if v:
                            dve.wait_ge(yev_ok.sem, yev_ok.at(n))
                            dve.wait_ge(h1_in.sems[u], h1_in.at(n, u))
                        else:
                            dve.wait_ge(ya_in.sems[u], ya_in.at(n, u))
                        nc.vector.tensor_tensor(total[v][u][:], total[v][u][:], h1[v][u][:], ALU.add).then_inc(sums[v].sem, 1)
                        return
                    k = part - 1
                    if k == 0:
                        dve.wait_ge(ye_in[v].sems[u], ye_in[v].at(n, u))
                        dve.wait_ge(wt_ok[v].sem, wt_ok[v].at(n))
                    dve.wait_ge(sums[v].sem, sums[v].at(n, part))
                    for t in range(BLOCK):
                        last = nc.vector.scalar_tensor_tensor(total[v][u][:, t, :], ye[v][u][:, t, k, :], wt[v][u][:, t, k:k + 1],
                                                              total[v][u][:, t, :], ALU.mult, ALU.add)
                    last.then_inc(done[v].sem if k else sums[v].sem, 1)

                def beside_chunk(n, u, m):
                    if m < 6 and m % 2 == 0 and known(n, 0, steps):
                        add(0, n, u, m // 2)
                    if m < 6 and m % 2 == 1 and known(n, 1, steps + 1):
                        add(1, n - 1, 1 - u, m // 2)

                def position(i, r):
                    n, u = i * body + r, r % 2
                    if collect and not known(n, -2, steps - 1):
                        for m in range(chunks):
                            beside_chunk(n, u, m)
                    if known(n, -1, steps - 1):
                        v = 1 - u
                        dve.wait_ge(y_ok.sem, y_ok.at(n - 1))
                        for m in range(chunks):
                            if collect:
                                beside_chunk(n, u, m)
                            dve.wait_ge(gelu_ok.sem, gelu_ok.at(n + 1, m + 1))
                            nc.vector.tensor_copy(gh[v][:, m, :], g32[:, m, :]).then_inc(gh_ok.sem, 1)
                            dve.wait_ge(gh_ok.sem, gh_ok.at(n + 1, m + 1))
                            nc.vector.tensor_tensor(gl[v][:, m, :], g32[:, m, :], gh[v][:, m, :], ALU.subtract).then_inc(split_ok.sem, 1)
                    if known(n, -2, steps - 2):
                        dve.wait_ge(xh_ok.sem, xh_ok.at(n + 2))
                        nc.vector.tensor_tensor(xl[u][:], psT[:, :, 0:N], xh[u][:], ALU.subtract).then_inc(xl_ok.sem, 1)
                    new = new_weights(i, r)
                    if new is not None:
                        split_weights(*new)
                    if known(n, 0, steps):
                        _, w = weights_at(i, r)
                        dve.wait_ge(y_out.sems[u], y_out.at(n - 2, u))
                        for b in range(banks):
                            here = min(2, tiles - 2 * b)
                            dve.wait_ge(y_ok.sem, y_ok.at(n, b + 1))
                            nc.vector.tensor_tensor(y[u][:, 2 * b:2 * b + here, :], psY[b % 2][:, 0:here, :],
                                                              b2[w][:].unsqueeze(1).broadcast_to([tile, here, C]), ALU.add).then_inc(yev_ok.sem, 1)

                dve.sem_inc(wl_ok.sem, wl_ok.per)
                positions(dve, position)
                if collect:
                    for part in range(3):
                        add(1, steps - 1, 1, part)

            @block.tensor
            def _(pe):
                for s in (t_ok, g_ok, y_ok):
                    s.open(pe)
                pe.wait_ge(setup, 16)

                def position(i, r):
                    n, u = i * body + r, r % 2
                    if known(n, -1, steps - 1):
                        v = 1 - u
                        e, w = weights_at(i, r + 1)
                        pe.wait_ge(wl_ok.sem, wl_ok.at(e))
                        pe.wait_ge(xl_ok.sem, xl_ok.at(n + 1))
                        for m in range(chunks):
                            pe.wait_ge(gelu_ok.sem, reused(gelu_ok, n + 1, m))
                            rows = slice(128 * m, 128 * m + 128)
                            three_products(nc, psG[m % ahead][:, 0:N], [
                                (w1h[w][:, c, rows], w1l[w][:, c, rows], xh[v][:, c, :], xl[v][:, c, :]) for c in range(2)]).then_inc(g_ok.sem, 1)
                    if known(n, -2, steps - 2):
                        pe.wait_ge(x_in.sems[u], x_in.at(n + 2, u))
                        pe.wait_ge(xl_ok.sem, xl_ok.at(n + 1))
                        for c in range(2):
                            for t in range(tiles):
                                last = nc.tensor.transpose(psT[:, c, t * tile:(t + 1) * tile], xin[u][:, t, c * 128:(c + 1) * 128],
                                                           ident[0:tile, 0:tile])
                        last.then_inc(t_ok.sem, 1)
                    if known(n, 0, steps):
                        _, w = weights_at(i, r)
                        pe.wait_ge(split_ok.sem, split_ok.at(n))
                        for b in range(banks):
                            if b >= 2:
                                pe.wait_ge(yev_ok.sem, yev_ok.at(n, b - 1))
                            else:
                                pe.wait_ge(yev_ok.sem, yev_ok.at(n - 1, max(j for j in range(banks) if j % 2 == b) + 1))
                            for t in range(2 * b, min(2 * b + 2, tiles)):
                                cut = slice(t * tile, (t + 1) * tile)
                                last = three_products(nc, psY[b % 2][:, t % 2, :], [
                                    (gh[u][:, m, cut], gl[u][:, m, cut], w2h[w][:, m, :], w2l[w][:, m, :]) for m in range(chunks)])
                            last.then_inc(y_ok.sem, 1)

                positions(pe, position)


ROWS_ALL = EXPERTS * ROOM
NOWHERE = 4 * ROWS_ALL
BITS = 30


def route(nc, d, networks):
    with stage(nc) as ctx:
        def sb(x, shape, dt=F32):
            return ctx.enter_context(nc.sbuf_tensor("p3_" + x, shape, dt))

        def pb(x, shape, dt=F32):
            return ctx.enter_context(nc.psum_tensor("p3_" + x, shape, dt))

        def signal(x, per=1):
            return Signal(nc, ctx, "p3_" + x, per)

        def transfers(x, per=1):
            return Transfers(nc, ctx, "p3_" + x, per)

        def plain(x):
            return semaphore(nc, ctx, "p3_" + x)

        N = BLOCK * GROUP
        wide = [GROUP, TILES, EXPERTS]
        ident, eps = sb("ident", [128, 128]), sb("eps", [GROUP, 1])
        wz, bz, eb = sb("wz", [128, 2, EXPERTS]), sb("bz", [GROUP, EXPERTS]), sb("eb", [GROUP, EXPERTS])
        iota, rows0 = sb("iota", [GROUP, EXPERTS]), sb("rows0", [GROUP, EXPERTS])
        tri32, ones32 = sb("tri32", [GROUP, GROUP]), sb("ones32", [GROUP, GROUP])
        tri, ones = sb("tri", [GROUP, GROUP], BF16), sb("ones", [GROUP, GROUP], BF16)
        hin = [sb(f"hin{u}", [GROUP, BLOCK, C]) for u in range(2)]
        xf = [sb(f"xf{u}", [GROUP, BLOCK, C]) for u in range(2)]
        stats, mv = sb("stats", [GROUP, BLOCK, 6]), sb("mv", [GROUP, BLOCK, 2])
        std, rstd = sb("std", [GROUP, BLOCK]), sb("rstd", [GROUP, BLOCK])
        xT, zT = sb("xT", [128, 2, N]), sb("zT", [EXPERTS, N])
        z, c, key, oh1, oh2, c2, w, t1, t2 = (sb(x, wide) for x in
                                             ("z", "c", "key", "oh1", "oh2", "c2", "w", "t1", "t2"))
        m16 = sb("m16", wide, BF16)
        m1, m2, i1, r1, w1, w2 = (sb(x, [GROUP, TILES]) for x in ("m1", "m2", "i1", "r1", "w1", "w2"))
        onesrow = sb("onesrow", [GROUP, TILES])
        cur, cand, bit, take = (sb(x, [GROUP, EXPERTS], U32) for x in ("cur", "cand", "bit", "take"))
        bitf, half = sb("bitf", [GROUP, 1]), sb("half", [GROUP, 1])
        part, more = sb("part", [GROUP, EXPERTS]), sb("more", [GROUP, EXPERTS])
        sidx, gidx = sb("sidx", [GROUP, TILES, 2], U32), sb("gidx", [GROUP, TILES, 2], U32)
        gw = sb("gw", [GROUP, TILES, 2])

        raws = [(sb(x.source + "raw1", [128, 2, x.hidden]), sb(x.source + "raw2", [128, x.hidden // 128, C])) for x in networks]

        psT = pb("psT", [128, 2, 512])
        psZ, psB, psC = pb("psZ", [EXPERTS, 512]), pb("psB", [GROUP, BLOCK, EXPERTS]), pb("psC", [GROUP, EXPERTS])
        flatR = psT[0:GROUP].rearrange("p b x -> p (b x)")
        psR = flatR[:, 0:TILES * EXPERTS].rearrange("p (t e) -> p t e", e=EXPERTS)
        psU = pb("psU", [GROUP, 2, 512])
        flatU = psU[:].rearrange("p b x -> p (b x)")
        psUw = flatU[:, 0:TILES * EXPERTS].rearrange("p (t e) -> p t e", e=EXPERTS)

        setup, made = plain("constants_loaded"), plain("constants_made")
        h_in, xf_out = transfers("h1_in"), transfers("xf_out")
        stats_ok, mv_ok, std_ok, rstd_ok, xf_ok = (signal(x) for x in ("stats", "mv", "std", "rstd", "xf"))
        t_ok, xT_ok, z_ok, zT_ok, zz_ok, zw_ok = (signal(x) for x in
                                                 ("xT_in_psum", "xT", "z_in_psum", "zT", "z_transposed", "z"))
        sig_ok = plain("sigmoid")
        w_in, wh_ok = plain("weights_loaded"), plain("weights_hi")
        search, counted = signal("search", 8), signal("counted")
        chain, asked, ranked = plain("chain"), plain("mask_ready"), plain("ranks_in_psum")
        tables_ready, tables_out = plain("tables_ready"), plain("tables_stored")
        passed = {e: plain("passed_" + e) for e in ("sp", "dve", "pe")}

        def positions(eng, position):
            for n in (-2, -1, 0, 1):
                position(n, n % 2)
            with eng.Fori(1, BLOCKS // 2 - 2) as j:
                for u in range(2):
                    position(j * 2 + u, u)
            for n in range(BLOCKS - 4, BLOCKS):
                position(n, n % 2)

        with nc.Block() as block:
            @block.sync
            def _(sp):
                for s in (h_in, xf_out):
                    s.open(sp)

                def load(n, u):
                    sp.dma_start(hin[u][:], tiles_of(d["h1"][bass.ds(n * N, N), :], GROUP)).then_inc(h_in.sems[u], 16)

                load(0, 0)
                load(1, 1)
                for dst, name in ((ident, "ident"), (wz, "proj_w"), (bz, "proj_b"), (eb, "expert_bias"), (iota, "iota"),
                                  (rows0, "rows0"), (tri32, "tri")):
                    sp.dma_start(dst[:], d[name]).then_inc(setup, 16)

                for x, raw in zip(networks, raws):
                    for dst, src in ((raw[0], "w1"), (raw[1], "w2"), (x.b1, "b1"), (x.b2, "b2")):
                        sp.dma_start(dst[:], d[x.source + src][0]).then_inc(w_in, 16)

                def position(n, u):
                    if known(n, -2, BLOCKS - 2):
                        sp.wait_ge(xf_ok.sem, xf_ok.at(n + 2))
                        sp.sem_inc(passed["sp"], 1)
                        if known(n, -2, BLOCKS - 4):
                            load(n + 4, u)
                        sp.dma_start(tiles_of(d["xf"][bass.ds((n + 2) * N, N), :], GROUP), xf[u][:]).then_inc(xf_out.sems[u], 16)

                positions(sp, position)
                sp.wait_ge(xf_out.sems[0], xf_out.at(BLOCKS - 2, 0))
                sp.wait_ge(xf_out.sems[1], xf_out.at(BLOCKS - 1, 1))

                sp.wait_ge(tables_ready, 1)
                for name, src in (("gidx", gidx), ("gw", gw), ("sidx", sidx)):
                    sp.dma_start(d[name], src[:]).then_inc(tables_out, 16)
                sp.wait_ge(tables_out, 48)

            @block.scalar
            def _(act):
                for s in (std_ok, xT_ok, zT_ok):
                    s.open(act)
                act.wait_ge(made, 1)

                def position(n, u):
                    if known(n, -2, BLOCKS - 2):
                        act.wait_ge(mv_ok.sem, mv_ok.at(n + 2))
                        act.wait_ge(rstd_ok.sem, rstd_ok.at(n + 1))
                        act.activation(std[:], mv[:, :, 1], ACT.Sqrt, bias=eps[:, 0:1]).then_inc(std_ok.sem, 1)
                    if known(n, -1, BLOCKS - 1):
                        act.wait_ge(z_ok.sem, z_ok.at(n + 1))
                        act.wait_ge(zz_ok.sem, zz_ok.at(n))
                        act.activation(zT[:], psZ[:, 0:N], ACT.Copy).then_inc(zT_ok.sem, 1)
                    if known(n, -2, BLOCKS - 2):
                        act.wait_ge(t_ok.sem, t_ok.at(n + 2))
                        act.activation(xT[:], psT[:, :, 0:N], ACT.Copy).then_inc(xT_ok.sem, 1)

                positions(act, position)
                act.wait_ge(zw_ok.sem, zw_ok.at(BLOCKS - 1))
                act.activation(c[:], z[:], ACT.Sigmoid).then_inc(sig_ok, 1)
                act.wait_ge(w_in, 16 * 4 * len(networks))
                for x, raw in zip(networks, raws):
                    act.activation(x.w1h[:], raw[0][:], ACT.Copy).then_inc(wh_ok, 1)
                    act.activation(x.w2h[:], raw[1][:], ACT.Copy).then_inc(wh_ok, 1)

            @block.gpsimd
            def _(pool):
                for n, (x, raw) in enumerate(zip(networks, raws)):
                    pool.wait_ge(wh_ok, 2 * n + 1)
                    nc.gpsimd.tensor_tensor(x.w1l[:], raw[0][:], x.w1h[:], ALU.subtract)
                    pool.wait_ge(wh_ok, 2 * n + 2)
                    nc.gpsimd.tensor_tensor(x.w2l[:], raw[1][:], x.w2h[:], ALU.subtract)

            @block.vector
            def _(dve):
                for s in (stats_ok, mv_ok, rstd_ok, xf_ok, zw_ok, search):
                    s.open(dve)
                nc.vector.memset(eps[:], EPS).then_inc(made, 1)
                nc.vector.memset(ones[:], 1.0)
                nc.vector.memset(ones32[:], 1.0)
                nc.vector.memset(onesrow[:], 1.0)
                nc.vector.memset(cur[:], 0)
                nc.vector.memset(bitf[:], 2.0 ** (BITS - 1)).then_inc(made, 1)
                dve.wait_ge(setup, 16 * 7)
                nc.vector.tensor_copy(tri[:], tri32[:]).then_inc(made, 1)

                def position(n, u):
                    if known(n, -2, BLOCKS - 2):
                        dve.wait_ge(h_in.sems[u], h_in.at(n + 2, u))
                        for t in range(BLOCK):
                            last = nc.vector.bn_stats(stats[:, t, :], hin[u][:, t, :])
                        last.then_inc(stats_ok.sem, 1)
                        dve.wait_ge(stats_ok.sem, stats_ok.at(n + 2))
                        dve.wait_ge(std_ok.sem, std_ok.at(n + 1))
                        dve.sem_inc(passed["dve"], 1)
                        for t in range(BLOCK):
                            last = nc.vector.bn_aggr(mv[:, t, :], stats[:, t, :])
                        last.then_inc(mv_ok.sem, 1)
                        dve.wait_ge(std_ok.sem, std_ok.at(n + 2))
                        nc.vector.reciprocal(rstd[:], std[:]).then_inc(rstd_ok.sem, 1)
                        dve.wait_ge(rstd_ok.sem, rstd_ok.at(n + 2))
                        dve.wait_ge(xf_out.sems[u], xf_out.at(n, u))
                        dve.wait_ge(t_ok.sem, t_ok.at(n))
                        for t in range(BLOCK):
                            last = nc.vector.tensor_scalar(xf[u][:, t, :], hin[u][:, t, :], mv[:, t, 0:1], rstd[:, t:t + 1],
                                                           ALU.subtract, ALU.mult)
                        last.then_inc(xf_ok.sem, 1)
                    if known(n, 0, BLOCKS):
                        dve.wait_ge(zz_ok.sem, zz_ok.at(n))
                        nc.vector.tensor_tensor(z[:, bass.ds(n * BLOCK, BLOCK), :], psB[:],
                                                         bz[:].unsqueeze(1).broadcast_to([GROUP, BLOCK, EXPERTS]), ALU.add).then_inc(zw_ok.sem, 1)

                positions(dve, position)

                def links():
                    count[0] += 1
                    return count[0]

                count = [0]

                def over_tiles(a):
                    return a.unsqueeze(1).broadcast_to(wide)

                def over_experts(a):
                    return a.unsqueeze(2).broadcast_to(wide)

                tt, ts, stt = nc.vector.tensor_tensor, nc.vector.tensor_scalar, nc.vector.scalar_tensor_tensor

                def top(scores, best, one_hot):
                    nc.vector.tensor_reduce(best[:], scores[:], AX.X, ALU.max).then_inc(chain, 1)
                    dve.wait_ge(chain, links())
                    tt(key[:], scores[:], over_experts(best[:]), ALU.is_lt).then_inc(chain, 1)
                    dve.wait_ge(chain, links())
                    stt(key[:], key[:], float(EXPERTS), over_tiles(iota[:]), ALU.mult, ALU.add).then_inc(chain, 1)
                    dve.wait_ge(chain, links())
                    nc.vector.tensor_reduce(i1[:], key[:], AX.X, ALU.min).then_inc(chain, 1)
                    dve.wait_ge(chain, links())
                    tt(one_hot[:], over_tiles(iota[:]), over_experts(i1[:]), ALU.is_equal).then_inc(chain, 1)
                    dve.wait_ge(chain, links())

                dve.wait_ge(sig_ok, 1)
                tt(c[:], c[:], over_tiles(eb[:]), ALU.add).then_inc(chain, 1)
                dve.wait_ge(chain, links())
                ts(c[:], c[:], 1e-12, None, ALU.max).then_inc(chain, 1)
                dve.wait_ge(chain, links())
                top(c, m1, oh1)
                stt(c2[:], oh1[:], -1e30, c[:], ALU.mult, ALU.add).then_inc(chain, 1)
                dve.wait_ge(chain, links())
                top(c2, m2, oh2)
                tt(r1[:], m1[:], m2[:], ALU.add).then_inc(chain, 1)
                dve.wait_ge(chain, links())
                nc.vector.reciprocal(r1[:], r1[:]).then_inc(chain, 1)
                dve.wait_ge(chain, links())
                tt(w1[:], m1[:], r1[:], ALU.mult).then_inc(chain, 1)
                dve.wait_ge(chain, links())
                tt(w2[:], m2[:], r1[:], ALU.mult).then_inc(chain, 1)
                dve.wait_ge(chain, links())
                tt(w[:], oh1[:], over_experts(w1[:]), ALU.mult).then_inc(chain, 1)
                dve.wait_ge(chain, links())
                tt(t1[:], oh2[:], over_experts(w2[:]), ALU.mult).then_inc(chain, 1)
                dve.wait_ge(chain, links())
                tt(w[:], w[:], t1[:], ALU.add).then_inc(chain, 1)
                dve.wait_ge(chain, links())

                def per_expert(a):
                    return a[:].rearrange("p t e -> p e t")

                nc.vector.tensor_copy(cand[:], bitf[:].broadcast_to([GROUP, EXPERTS])).then_inc(chain, 1)
                dve.wait_ge(chain, links())
                with dve.Fori(0, BITS) as b:
                    tt(t1[:], w[:], over_tiles(cand[:].bitcast(F32)), ALU.is_ge).then_inc(search.sem, 1)
                    dve.wait_ge(search.sem, search.at(b, 1))
                    nc.vector.tensor_reduce(part[:], per_expert(t1), AX.X, ALU.add).then_inc(search.sem, 1)
                    dve.wait_ge(search.sem, search.at(b, 2))
                    ts(half[:], bitf[:], 0.5, None, ALU.mult).then_inc(search.sem, 1)
                    dve.wait_ge(search.sem, search.at(b, 3))
                    nc.vector.tensor_copy(bit[:], half[:].broadcast_to([GROUP, EXPERTS])).then_inc(search.sem, 1)
                    dve.wait_ge(search.sem, search.at(b, 4))
                    dve.wait_ge(counted.sem, counted.at(b))
                    ts(take[:], psC[:], float(CAP), bitf[:, 0:1], ALU.is_ge, ALU.mult).then_inc(search.sem, 1)
                    dve.wait_ge(search.sem, search.at(b, 5))
                    tt(cur[:], cur[:], take[:], ALU.bitwise_or).then_inc(search.sem, 1)
                    dve.wait_ge(search.sem, search.at(b, 6))
                    tt(cand[:], cur[:], bit[:], ALU.bitwise_or).then_inc(search.sem, 1)
                    dve.wait_ge(search.sem, search.at(b, 7))
                    nc.vector.tensor_copy(bitf[:], half[:]).then_inc(search.sem, 1)
                    dve.wait_ge(search.sem, search.at(b, 8))

                tt(c2[:], w[:], over_tiles(cur[:].bitcast(F32)), ALU.is_gt).then_inc(chain, 1)
                dve.wait_ge(chain, links())
                nc.vector.tensor_reduce(part[:], per_expert(c2), AX.X, ALU.add).then_inc(chain, 1)
                dve.wait_ge(chain, links())
                tt(t1[:], oh1[:], oh2[:], ALU.add).then_inc(chain, 1)
                dve.wait_ge(chain, links())
                tt(t2[:], w[:], over_tiles(cur[:].bitcast(F32)), ALU.is_equal).then_inc(chain, 1)
                dve.wait_ge(chain, links())
                tt(t2[:], t2[:], t1[:], ALU.mult).then_inc(chain, 1)
                dve.wait_ge(chain, links())
                nc.vector.tensor_copy(m16[:], t2[:]).then_inc(asked, 1)

                def ranks(out, n):
                    dve.wait_ge(ranked, n)
                    for e in range(EXPERTS):
                        last = nc.vector.tensor_tensor_scan(key[:, :, e], onesrow[:], psUw[:, :, e], 0.0, ALU.mult, ALU.add)
                    last.then_inc(chain, 1)
                    dve.wait_ge(chain, links())
                    tt(out[:], key[:], psUw, ALU.subtract).then_inc(chain, 1)
                    dve.wait_ge(chain, links())
                    tt(out[:], out[:], psR, ALU.add).then_inc(chain, 1)
                    dve.wait_ge(chain, links())

                ranks(t1, 1)
                ts(more[:], psC[:], -1.0, float(CAP), ALU.mult, ALU.add).then_inc(chain, 1)
                dve.wait_ge(chain, links())
                tt(t1[:], t1[:], over_tiles(more[:]), ALU.is_lt).then_inc(chain, 1)
                dve.wait_ge(chain, links())
                tt(t1[:], t1[:], t2[:], ALU.mult).then_inc(chain, 1)
                dve.wait_ge(chain, links())
                tt(c2[:], c2[:], t1[:], ALU.add).then_inc(chain, 1)
                dve.wait_ge(chain, links())
                nc.vector.tensor_copy(m16[:], c2[:]).then_inc(asked, 1)
                ranks(t1, 2)
                tt(t1[:], t1[:], over_tiles(rows0[:]), ALU.add).then_inc(chain, 1)
                dve.wait_ge(chain, links())
                for k, (one_hot, weight) in enumerate(((oh1, w1), (oh2, w2))):
                    tt(t2[:], one_hot[:], t1[:], ALU.mult).then_inc(chain, 1)
                    dve.wait_ge(chain, links())
                    nc.vector.tensor_reduce(m1[:], t2[:], AX.X, ALU.add).then_inc(chain, 1)
                    dve.wait_ge(chain, links())
                    tt(t2[:], one_hot[:], c2[:], ALU.mult).then_inc(chain, 1)
                    dve.wait_ge(chain, links())
                    nc.vector.tensor_reduce(m2[:], t2[:], AX.X, ALU.add).then_inc(chain, 1)
                    dve.wait_ge(chain, links())
                    tt(gw[:, :, k], weight[:], m2[:], ALU.mult).then_inc(chain, 1)
                    dve.wait_ge(chain, links())
                    tt(i1[:], m1[:], m2[:], ALU.mult).then_inc(chain, 1)
                    dve.wait_ge(chain, links())
                    nc.vector.tensor_copy(gidx[:, :, k], i1[:]).then_inc(chain, 1)
                    dve.wait_ge(chain, links())
                    ts(m2[:], m2[:], -float(NOWHERE), float(NOWHERE), ALU.mult, ALU.add).then_inc(chain, 1)
                    dve.wait_ge(chain, links())
                    tt(m1[:], m1[:], m2[:], ALU.add).then_inc(chain, 1)
                    dve.wait_ge(chain, links())
                    nc.vector.tensor_copy(sidx[:, :, k], m1[:]).then_inc(chain, 1)
                    dve.wait_ge(chain, links())
                dve.sem_inc(tables_ready, 1)

            @block.tensor
            def _(pe):
                for s in (t_ok, z_ok, zz_ok, counted):
                    s.open(pe)
                pe.wait_ge(setup, 16 * 7)
                pe.wait_ge(made, 3)

                def position(n, u):
                    if known(n, -1, BLOCKS - 1):
                        pe.wait_ge(xT_ok.sem, xT_ok.at(n + 1))
                        pe.wait_ge(zT_ok.sem, zT_ok.at(n))
                        for h in range(2):
                            last = nc.tensor.matmul(psZ[:, 0:N], wz[:, h, :], xT[:, h, :], start=(h == 0), stop=(h == 1))
                        last.then_inc(z_ok.sem, 1)
                    if known(n, 0, BLOCKS):
                        pe.wait_ge(zT_ok.sem, zT_ok.at(n))
                        pe.wait_ge(zw_ok.sem, zw_ok.at(n - 1))
                        pe.sem_inc(passed["pe"], 1)
                        for t in range(BLOCK):
                            last = nc.tensor.transpose(psB[:, t, :], zT[:, t * GROUP:(t + 1) * GROUP], ident[0:EXPERTS, 0:EXPERTS])
                        last.then_inc(zz_ok.sem, 1)
                    if known(n, -2, BLOCKS - 2):
                        pe.wait_ge(xf_ok.sem, xf_ok.at(n + 2))
                        pe.wait_ge(xT_ok.sem, xT_ok.at(n + 1))
                        for h in range(2):
                            for t in range(BLOCK):
                                last = nc.tensor.transpose(psT[:, h, t * GROUP:(t + 1) * GROUP], xf[u][:, t, h * 128:(h + 1) * 128],
                                                           ident[0:GROUP, 0:GROUP])
                        last.then_inc(t_ok.sem, 1)

                positions(pe, position)
                with pe.Fori(0, BITS) as b:
                    pe.wait_ge(search.sem, search.at(b, 2))
                    pe.wait_ge(search.sem, search.at(b - 1, 5))
                    nc.tensor.matmul(psC[:], ones32[:], part[:], start=True, stop=True).then_inc(counted.sem, 1)
                for n in range(2):
                    pe.wait_ge(asked, n + 1)
                    if n == 0:
                        nc.tensor.matmul(psC[:], ones32[:], part[:], start=True, stop=True)
                    m = m16[:].rearrange("p t e -> p (t e)")
                    for h in range(2):
                        cut = slice(512 * h, min(512 * h + 512, TILES * EXPERTS))
                        nc.tensor.matmul(flatR[:, cut], tri[:], m[:, cut], start=True, stop=True)
                        last = nc.tensor.matmul(flatU[:, cut], ones[:], m[:, cut], start=True, stop=True)
                    last.then_inc(ranked, 1)


def constants():
    import numpy as np
    bfloat16 = mybir.dt.np(BF16)
    half = DK // 2
    freq = 1.0 / 10000.0 ** (np.arange(0, DK, 2, dtype=np.float64) / DK)
    comp = np.arange(128) % DK
    f = freq[comp % half][:, None]
    is_cos = comp[:, None] < half
    out = {}
    rot = []
    for shift in (0, S):
        angle = (np.tile(np.arange(S), 2)[None, :] + shift) * f
        rot += [np.sin(angle), np.where(is_cos, 1.0, -1.0) * np.cos(angle)]
    out["rot"] = np.stack(rot, 1).astype(np.float32)
    angle = np.arange(S)[None, :] * np.concatenate([freq, freq])[:, None]
    t = np.where(np.arange(DK)[:, None] < half, np.cos(angle), np.sin(angle))
    th = t.astype(np.float32).astype(bfloat16)
    tl = (t - th.astype(np.float64)).astype(np.float32).astype(bfloat16)
    out["keyrows"] = np.concatenate([th, tl, th, np.ones((2, S), bfloat16)], 0)
    out["keyrows"] = np.broadcast_to(np.tile(out["keyrows"], (1, 2))[:, None, :], (DK * 3 + 2, HEADS, PAIR))
    one, other = np.arange(TILE)[:, None], np.arange(TILE)[None, :]
    key = np.arange(TILE + 1)[None, :]
    never = [np.where(key < TILE, key > one, one == TILE - 1)] * 2
    never += [one == key] * 2
    never += [other < one + 2] * 4
    out["never"] = np.concatenate([np.where(x, NEVER, 0.0) for x in never], 1).astype(np.float32)
    out["maskE"] = (one >= other + 2).astype(np.uint32)
    one, other = np.arange(GROUP)[:, None], np.arange(GROUP)[None, :]
    out["tri"] = (one < other).astype(np.float32)
    out["iota"] = np.broadcast_to(np.arange(EXPERTS, dtype=np.float32), (GROUP, EXPERTS))
    out["rows0"] = np.broadcast_to(np.arange(EXPERTS, dtype=np.float32) * ROOM, (GROUP, EXPERTS))
    out["ident"] = np.eye(128, dtype=np.float32)
    out["blk8"] = (np.arange(128)[:, None] // DK == np.arange(8)[None, :]).astype(np.float32)
    return out


def lay_out(i):
    import numpy as np
    a = {k: np.asarray(v) for k, v in i.items()}
    x = a["x"].reshape(IMAGES, CHANNELS, GRID, PATCH, GRID, PATCH).transpose(1, 3, 5, 0, 2, 4)
    swap = (np.arange(C) // DK) * DK + (np.arange(C) % DK + DK // 2) % DK

    def chunks(w):
        return w.reshape(-1, 128, w.shape[-1]).transpose(1, 0, 2)

    u, v = a["L0_attn_u"].reshape(C), a["L0_attn_v"].reshape(C)
    out = {
        "x": x.reshape(PC, 128, T).transpose(1, 0, 2),
        "tok_w": chunks(a["L0_tok_W"].T),
        "tok_b": np.broadcast_to(a["L0_tok_b"], (TILE, C)),
        "qkv_w": chunks(np.concatenate([a["L0_attn_Wq"], a["L0_attn_Wq"][:, swap], a["L0_attn_Wk"], a["L0_attn_Wv"]], 1)),
        "cols": np.stack([u, v, v[swap]], 1).reshape(2, 128, 3).transpose(1, 0, 2),
    }
    out["wo"] = chunks(a["L0_attn_Wo"])
    out["bo"] = np.broadcast_to(a["L0_attn_bo"], (TILE, C))
    def transposed(w):
        return w.transpose(0, 2, 1).reshape(w.shape[0], -1, 128, w.shape[1]).transpose(0, 2, 1, 3)

    for name, kind in (("ex_", "fc"), ("sh_", "sh")):
        w1, b1, w2, b2 = (a[f"L0_ffn_{kind}{x}"] for x in ("1_w", "1_b", "2_w", "2_b"))
        if kind == "sh":
            w1, b1, w2, b2 = w1[None], b1[None], w2[None], b2[None]
        out[name + "w1"], out[name + "w2"] = transposed(w1), transposed(w2)
        out[name + "b1"] = b1.reshape(len(b1), -1, 128).transpose(0, 2, 1)
        out[name + "b2"] = np.broadcast_to(b2[:, None, :], (len(b2), GROUP if kind == "sh" else 128, C))
    out["proj_w"] = chunks(a["L0_ffn_proj_w"].T)
    out["proj_b"] = np.broadcast_to(a["L0_ffn_proj_b"], (GROUP, EXPERTS))
    out["expert_bias"] = np.broadcast_to(a["L0_ffn_expert_bias"], (GROUP, EXPERTS))
    out.update(constants())
    return {k: np.ascontiguousarray(v) for k, v in out.items()}


SCRATCH = {"h1": ([T, C], F32), "h0": ([T, C], F32), "v": ([T + PAD, C], F32), "c": ([T, HEADS], F32),
           "stack": ([2, 128, KINDS, T + PAD], BF16)}
SCRATCH.update(xf=([T, C], F32), xe=([ROWS_ALL, C], F32), ye=([ROWS_ALL, C], F32), ys=([T // 2, C], F32), sidx=([GROUP, TILES, 2], U32),
               gidx=([GROUP, TILES, 2], U32), gw=([GROUP, TILES, 2], F32))


def tower(nc, d):
    half = BLOCKS // 2
    project(nc, d)
    attend(nc, d)
    with ExitStack() as ctx:
        shared, expert = Weights(nc, ctx, "sh_", GROUP, SHARED_HIDDEN), Weights(nc, ctx, "ex_", 128, EXPERT_HIDDEN)
        route(nc, d, (shared, expert))
        feed_forward(nc, d, "sa_", shared, d["xf"], d["ys"], GROUP, BLOCK, 0, half, 2, 1, "send")
        feed_forward(nc, d, "ex_", expert, d["xe"], d["ye"], 128, BLOCK, 0, ROWS_ALL // (BLOCK * 128), 16, EXPERTS)
        feed_forward(nc, d, "sb_", shared, d["xf"], d["out"], GROUP, BLOCK, half, half, 2, 1, "collect")


def kernel(**inputs):
    import concourse.bacc as bacc
    from concourse.bass_utils import run_bass_kernel_spmd

    nc = bacc.Bacc("TRN2", target_bir_lowering=False, num_devices=1)
    arrays = lay_out(inputs)
    d = {k: nc.dram_tensor("in_" + k, a.shape, mybir.dt.from_np(a.dtype), kind="ExternalInput").ap()
         for k, a in arrays.items()}
    for k, (shape, dt) in SCRATCH.items():
        d[k] = nc.dram_tensor("scratch_" + k, shape, dt, kind="Internal").ap()
    d["out"] = nc.dram_tensor("out", [T, C], F32, kind="ExternalOutput").ap()
    tower(nc, d)
    r = run_bass_kernel_spmd(nc, [{"in_" + k: a for k, a in arrays.items()}], core_ids=[0])
    return r.results[0]["out"].reshape(IMAGES, S, C)
```
